# Optimizing a Trainium2 kernel written in Bass

```python
import numpy as np
import jax
import jax.numpy as jnp

def _softmax(x, axis=-1):
    return jax.nn.softmax(x, axis=axis)

def _gelu(x):
    return jax.nn.gelu(x, approximate=True)

def _silu(x):
    return jax.nn.silu(x)

def _sigmoid(x):
    return jax.nn.sigmoid(x)

def _layernorm(x, axis=-1, eps=1e-05):
    m = jnp.mean(x, axis=axis, keepdims=True)
    v = jnp.var(x, axis=axis, keepdims=True)
    return (x - m) / jnp.sqrt(v + eps)

def _scatter_add(tgt, idx, src, axis=0):
    return tgt.at[idx].add(src)

def _segment_sum(src, seg, n):
    return jax.ops.segment_sum(src, seg, n)
kernel_name = 'mk_gnn_resnorm_d4_gnn_r32_1163ca'

def setup_inputs(seed: int=0):
    np.random.seed(seed)
    _w = jnp.asarray

    def _rec_inputs():
        import jax
        import jax.numpy as jnp
        _gk = jax.random.key(seed)
        x = -0.0003713 + 1 * jax.random.normal(jax.random.fold_in(_gk, 1), (3125, 128), jnp.float32)
        src = jax.random.randint(jax.random.fold_in(_gk, 2), (100000,), 0, 3125, jnp.int32)
        dst = jax.random.randint(jax.random.fold_in(_gk, 3), (100000,), 0, 3125, jnp.int32)
        _o = jnp.argsort(dst, stable=True)
        src = src[_o]
        dst = dst[_o]
        edge_attr_32 = 1.36993e-05 + 0.999972 * jax.random.normal(jax.random.fold_in(_gk, 12), (100000, 32), jnp.float32)
        edge_type_8 = jax.random.randint(jax.random.fold_in(_gk, 14), (100000,), 0, 8, jnp.int32)
        edge_weight = jax.random.uniform(jax.random.fold_in(_gk, 15), (100000,), jnp.float32, 0.0, 1)
        edge_weight1 = jax.random.uniform(jax.random.fold_in(_gk, 16), (100000, 1), jnp.float32, 0.0, 0.999999)
        return (x, src, dst, edge_attr_32, edge_type_8, edge_weight, edge_weight1)
    x, src, dst, edge_attr_32, edge_type_8, edge_weight, edge_weight1 = _rec_inputs()

    def _L0_gnn_setup():
        import jax, jax.numpy as jnp
        import numpy as np
        N_NODES = 3125
        N_EDGES = 50000
        D_IN = 128
        D_OUT = 128
        key = jax.random.key(seed)
        k1, k2, k3, k4, k5, k6 = jax.random.split(key, 6)
        x = jax.random.normal(k1, (N_NODES, D_IN), dtype=jnp.float32)
        edge_src = jax.random.randint(k2, (N_EDGES,), 0, N_NODES, dtype=jnp.int32)
        edge_dst = jax.random.randint(k3, (N_EDGES,), 0, N_NODES, dtype=jnp.int32)
        edge_weight = jax.random.uniform(k4, (N_EDGES,), dtype=jnp.float32)
        W = jax.random.normal(k5, (D_IN, D_OUT), dtype=jnp.float32) * (1.0 / np.sqrt(D_IN))
        b = jax.random.normal(k6, (D_OUT,), dtype=jnp.float32) * 0.01
        return {'x': x, 'edge_src': edge_src, 'edge_dst': edge_dst, 'edge_weight': edge_weight, 'W': W, 'b': b}
    _L0_gnn_all = _L0_gnn_setup()
    _L0_gnn_in = {k: v for k, v in _L0_gnn_all.items() if k in ('W', 'b')}
    del _L0_gnn_all

    def _L1_gnn_setup():
        import jax, jax.numpy as jnp
        import numpy as np
        N_NODES = 3125
        N_EDGES = 18750
        H = 128
        T = 8
        L = 2

        def _gru_cell(x, h, wih, whh, bih, bhh):
            gi = x @ wih.T + bih
            gh = h @ whh.T + bhh
            i_r, i_z, i_n = jnp.split(gi, 3, axis=-1)
            h_r, h_z, h_n = jnp.split(gh, 3, axis=-1)
            r = jax.nn.sigmoid(i_r + h_r)
            z = jax.nn.sigmoid(i_z + h_z)
            n = jnp.tanh(i_n + r * h_n)
            return (1.0 - z) * n + z * h
        key = jax.random.key(seed)
        ks = jax.random.split(key, 12)
        s = 1.0 / np.sqrt(H)
        inp = {'node_features': jax.random.normal(ks[0], (N_NODES, H), dtype=jnp.float32), 'edge_index': jax.random.randint(ks[1], (2, N_EDGES), 0, N_NODES, dtype=jnp.int64), 'edge_type': jax.random.randint(ks[2], (N_EDGES,), 0, T, dtype=jnp.int64), 'node_proj_w': jax.random.uniform(ks[3], (H, H), jnp.float32, -s, s), 'node_proj_b': jax.random.uniform(ks[4], (H,), jnp.float32, -s, s), 'edge_W': jax.random.uniform(ks[5], (L, T, H, H), jnp.float32, -s, s), 'edge_b': jax.random.uniform(ks[6], (L, T, H), jnp.float32, -s, s), 'gru_wih': jax.random.uniform(ks[7], (L, 3 * H, H), jnp.float32, -s, s), 'gru_whh': jax.random.uniform(ks[8], (L, 3 * H, H), jnp.float32, -s, s), 'gru_bih': jax.random.uniform(ks[9], (L, 3 * H), jnp.float32, -s, s), 'gru_bhh': jax.random.uniform(ks[10], (L, 3 * H), jnp.float32, -s, s), 'out_w': jax.random.uniform(ks[11], (H, H), jnp.float32, -s, s), 'out_b': jnp.zeros((H,), jnp.float32)}
        return inp
    _L1_gnn_all = _L1_gnn_setup()
    _L1_gnn_in = {k: v for k, v in _L1_gnn_all.items() if k in ('node_proj_w', 'node_proj_b', 'edge_W', 'edge_b', 'gru_wih', 'gru_whh', 'gru_bih', 'gru_bhh', 'out_w', 'out_b')}
    del _L1_gnn_all

    def _L2_gnn_setup():
        import jax, jax.numpy as jnp
        import numpy as np
        N_NODES = 3125
        N_EDGES = 50000
        NODE_DIM = 128
        HIDDEN = 128
        N_LAYERS = 4
        LN_EPS = 1e-05

        def _layernorm(x, g, b):
            mu = jnp.mean(x, axis=-1, keepdims=True)
            var = jnp.mean(jnp.square(x - mu), axis=-1, keepdims=True)
            return (x - mu) * jax.lax.rsqrt(var + LN_EPS) * g + b
        key = jax.random.key(seed)
        ks = jax.random.split(key, 16)
        s = 1.0 / np.sqrt(HIDDEN)
        inp = {'x': jax.random.normal(ks[0], (N_NODES, NODE_DIM), dtype=jnp.float32), 'edge_index': jax.random.randint(ks[1], (2, N_EDGES), 0, N_NODES, dtype=jnp.int64), 'Wn': jax.random.normal(ks[2], (NODE_DIM, HIDDEN), dtype=jnp.float32) / np.sqrt(NODE_DIM), 'bn': jnp.zeros((HIDDEN,), dtype=jnp.float32), 'WQ': jax.random.normal(ks[3], (N_LAYERS, HIDDEN, HIDDEN), dtype=jnp.float32) * s, 'bQ': jnp.zeros((N_LAYERS, HIDDEN), dtype=jnp.float32), 'WK': jax.random.normal(ks[4], (N_LAYERS, HIDDEN, HIDDEN), dtype=jnp.float32) * s, 'bK': jnp.zeros((N_LAYERS, HIDDEN), dtype=jnp.float32), 'WV': jax.random.normal(ks[5], (N_LAYERS, HIDDEN, HIDDEN), dtype=jnp.float32) * s, 'bV': jnp.zeros((N_LAYERS, HIDDEN), dtype=jnp.float32), 'WO': jax.random.normal(ks[6], (N_LAYERS, HIDDEN, HIDDEN), dtype=jnp.float32) * s, 'bO': jnp.zeros((N_LAYERS, HIDDEN), dtype=jnp.float32), 'ln_g': jnp.ones((N_LAYERS, HIDDEN), dtype=jnp.float32), 'ln_b': jnp.zeros((N_LAYERS, HIDDEN), dtype=jnp.float32), 'Wout': jax.random.normal(ks[7], (HIDDEN, NODE_DIM), dtype=jnp.float32) * s, 'bout': jnp.zeros((NODE_DIM,), dtype=jnp.float32)}
        return inp
    _L2_gnn_all = _L2_gnn_setup()
    _L2_gnn_in = {k: v for k, v in _L2_gnn_all.items() if k in ('Wn', 'bn', 'WQ', 'bQ', 'WK', 'bK', 'WV', 'bV', 'WO', 'bO', 'ln_g', 'ln_b', 'Wout', 'bout')}
    del _L2_gnn_all

    def _L3_gnn_setup():
        import jax, jax.numpy as jnp
        import numpy as np
        N, E, H, EF = (1250, 20000, 128, 32)

        def _residual(x, W, b):
            h = jax.nn.silu(x @ W[0] + b[0])
            h = jax.nn.silu(h @ W[1] + b[1])
            return x + h
        key = jax.random.key(seed)
        ks = jax.random.split(key, 10)
        s = 1.0 / np.sqrt(H)
        return {'scalar': jax.random.normal(ks[0], (N, H), jnp.float32), 'ef': jax.random.normal(ks[1], (E, EF), jnp.float32), 'edge_index': jax.random.randint(ks[2], (2, E), 0, N, dtype=jnp.int32), 'C': jnp.ones((1,), jnp.float32), 'conv_smooth': jax.random.uniform(ks[3], (E, 1), jnp.float32), 'W_emb': jax.random.normal(ks[4], (2, 2, H, H), jnp.float32) * s, 'b_emb': jnp.zeros((2, 2, H), jnp.float32), 'We': jax.random.normal(ks[5], (EF, H), jnp.float32) * (1.0 / np.sqrt(EF)), 'W_conv': jax.random.normal(ks[6], (2, 2, H, H), jnp.float32) * s, 'b_conv': jnp.zeros((2, 2, H), jnp.float32), 'W_out': jax.random.normal(ks[7], (2, 2, H, H), jnp.float32) * s, 'b_out': jnp.zeros((2, 2, H), jnp.float32)}
    _L3_gnn_all = _L3_gnn_setup()
    _L3_gnn_in = {k: v for k, v in _L3_gnn_all.items() if k in ('C', 'W_emb', 'b_emb', 'We', 'W_conv', 'b_conv', 'W_out', 'b_out')}
    del _L3_gnn_all
    return {'x': x, 'src': src, 'dst': dst, 'edge_attr_32': edge_attr_32, 'edge_type_8': edge_type_8, 'edge_weight': edge_weight, 'edge_weight1': edge_weight1, 'L0_gnn_W': _L0_gnn_in['W'], 'L0_gnn_b': _L0_gnn_in['b'], 'L1_gnn_node_proj_w': _L1_gnn_in['node_proj_w'], 'L1_gnn_node_proj_b': _L1_gnn_in['node_proj_b'], 'L1_gnn_edge_W': _L1_gnn_in['edge_W'], 'L1_gnn_edge_b': _L1_gnn_in['edge_b'], 'L1_gnn_gru_wih': _L1_gnn_in['gru_wih'], 'L1_gnn_gru_whh': _L1_gnn_in['gru_whh'], 'L1_gnn_gru_bih': _L1_gnn_in['gru_bih'], 'L1_gnn_gru_bhh': _L1_gnn_in['gru_bhh'], 'L1_gnn_out_w': _L1_gnn_in['out_w'], 'L1_gnn_out_b': _L1_gnn_in['out_b'], 'L2_gnn_Wn': _L2_gnn_in['Wn'], 'L2_gnn_bn': _L2_gnn_in['bn'], 'L2_gnn_WQ': _L2_gnn_in['WQ'], 'L2_gnn_bQ': _L2_gnn_in['bQ'], 'L2_gnn_WK': _L2_gnn_in['WK'], 'L2_gnn_bK': _L2_gnn_in['bK'], 'L2_gnn_WV': _L2_gnn_in['WV'], 'L2_gnn_bV': _L2_gnn_in['bV'], 'L2_gnn_WO': _L2_gnn_in['WO'], 'L2_gnn_bO': _L2_gnn_in['bO'], 'L2_gnn_ln_g': _L2_gnn_in['ln_g'], 'L2_gnn_ln_b': _L2_gnn_in['ln_b'], 'L2_gnn_Wout': _L2_gnn_in['Wout'], 'L2_gnn_bout': _L2_gnn_in['bout'], 'L3_gnn_C': _L3_gnn_in['C'], 'L3_gnn_W_emb': _L3_gnn_in['W_emb'], 'L3_gnn_b_emb': _L3_gnn_in['b_emb'], 'L3_gnn_We': _L3_gnn_in['We'], 'L3_gnn_W_conv': _L3_gnn_in['W_conv'], 'L3_gnn_b_conv': _L3_gnn_in['b_conv'], 'L3_gnn_W_out': _L3_gnn_in['W_out'], 'L3_gnn_b_out': _L3_gnn_in['b_out']}

def reference(x, src, dst, edge_attr_32, edge_type_8, edge_weight, edge_weight1, L0_gnn_W, L0_gnn_b, L1_gnn_node_proj_w, L1_gnn_node_proj_b, L1_gnn_edge_W, L1_gnn_edge_b, L1_gnn_gru_wih, L1_gnn_gru_whh, L1_gnn_gru_bih, L1_gnn_gru_bhh, L1_gnn_out_w, L1_gnn_out_b, L2_gnn_Wn, L2_gnn_bn, L2_gnn_WQ, L2_gnn_bQ, L2_gnn_WK, L2_gnn_bK, L2_gnn_WV, L2_gnn_bV, L2_gnn_WO, L2_gnn_bO, L2_gnn_ln_g, L2_gnn_ln_b, L2_gnn_Wout, L2_gnn_bout, L3_gnn_C, L3_gnn_W_emb, L3_gnn_b_emb, L3_gnn_We, L3_gnn_W_conv, L3_gnn_b_conv, L3_gnn_W_out, L3_gnn_b_out):
    import jax
    import jax.numpy as jnp

    def _L0_gnn_ref(x, edge_src, edge_dst, edge_weight, W, b):
        import jax, jax.numpy as jnp
        import numpy as np
        N_NODES = 3125
        N_EDGES = 50000
        D_IN = 128
        D_OUT = 128
        msgs = edge_weight[:, None] * x[edge_src]
        agg = jax.ops.segment_sum(msgs, edge_dst, num_segments=x.shape[0])
        out = jax.nn.relu(agg @ W + b)
        return out

    def _L1_gnn_ref(node_features, edge_index, edge_type, node_proj_w, node_proj_b, edge_W, edge_b, gru_wih, gru_whh, gru_bih, gru_bhh, out_w, out_b):
        import jax, jax.numpy as jnp
        import numpy as np
        N_NODES = 3125
        N_EDGES = 18750
        H = 128
        T = 8
        L = 2

        def _gru_cell(x, h, wih, whh, bih, bhh):
            gi = x @ wih.T + bih
            gh = h @ whh.T + bhh
            i_r, i_z, i_n = jnp.split(gi, 3, axis=-1)
            h_r, h_z, h_n = jnp.split(gh, 3, axis=-1)
            r = jax.nn.sigmoid(i_r + h_r)
            z = jax.nn.sigmoid(i_z + h_z)
            n = jnp.tanh(i_n + r * h_n)
            return (1.0 - z) * n + z * h
        num_nodes = node_features.shape[0]
        src, dst = (edge_index[0], edge_index[1])
        h = jax.nn.relu(node_features @ node_proj_w.T + node_proj_b)
        for l in range(L):
            trans = jnp.einsum('nh,tdh->tnd', h, edge_W[l])
            msgs = trans[edge_type, src]
            agg = jax.ops.segment_sum(msgs, dst, num_segments=num_nodes)
            h = _gru_cell(agg, h, gru_wih[l], gru_whh[l], gru_bih[l], gru_bhh[l])
            h = jax.nn.relu(h)
        return h @ out_w.T + out_b

    def _L2_gnn_ref(x, edge_index, Wn, bn, WQ, bQ, WK, bK, WV, bV, WO, bO, ln_g, ln_b, Wout, bout):
        import jax, jax.numpy as jnp
        import numpy as np
        N_NODES = 3125
        N_EDGES = 50000
        NODE_DIM = 128
        HIDDEN = 128
        N_LAYERS = 4
        LN_EPS = 1e-05

        def _layernorm(x, g, b):
            mu = jnp.mean(x, axis=-1, keepdims=True)
            var = jnp.mean(jnp.square(x - mu), axis=-1, keepdims=True)
            return (x - mu) * jax.lax.rsqrt(var + LN_EPS) * g + b
        n = x.shape[0]
        src, dst = (edge_index[0], edge_index[1])
        scale = 1.0 / np.sqrt(HIDDEN)
        h = x @ Wn + bn
        for l in range(N_LAYERS):
            Q = h @ WQ[l] + bQ[l]
            K = h @ WK[l] + bK[l]
            V = h @ WV[l] + bV[l]
            scores = jnp.sum(Q[dst] * K[src], axis=-1) * scale
            seg_max = jax.ops.segment_max(scores, dst, num_segments=n)
            e = jnp.exp(scores - seg_max[dst])
            seg_sum = jax.ops.segment_sum(e, dst, num_segments=n)
            attn = e / seg_sum[dst]
            messages = jax.ops.segment_sum(attn[:, None] * V[src], dst, num_segments=n)
            out = messages @ WO[l] + bO[l]
            h = _layernorm(h + out, ln_g[l], ln_b[l])
        return h @ Wout + bout

    def _L3_gnn_ref(scalar, ef, edge_index, C, conv_smooth, W_emb, b_emb, We, W_conv, b_conv, W_out, b_out):
        import jax, jax.numpy as jnp
        import numpy as np
        N, E, H, EF = (1250, 20000, 128, 32)

        def _residual(x, W, b):
            h = jax.nn.silu(x @ W[0] + b[0])
            h = jax.nn.silu(h @ W[1] + b[1])
            return x + h
        row, col = (edge_index[0], edge_index[1])
        scalar_src = _residual(scalar, W_emb[0], b_emb[0])
        scalar_dst = _residual(scalar, W_emb[1], b_emb[1])
        conv_filter = ef @ We * conv_smooth
        scalar_edge = scalar_dst[col] * conv_filter
        conv = jax.ops.segment_sum(scalar_edge, row, num_segments=scalar.shape[0]) * C
        conv = _residual(_residual(conv, W_conv[0], b_conv[0]), W_conv[1], b_conv[1])
        out = scalar_src * conv
        out = _residual(_residual(out, W_out[0], b_out[0]), W_out[1], b_out[1])
        return out
    edge_index = jnp.stack([src, dst])
    x = _layernorm(x + _L0_gnn_ref(x, src, dst, edge_weight, L0_gnn_W, L0_gnn_b), axis=-1)
    x = _layernorm(x + _L1_gnn_ref(x, edge_index, edge_type_8, L1_gnn_node_proj_w, L1_gnn_node_proj_b, L1_gnn_edge_W, L1_gnn_edge_b, L1_gnn_gru_wih, L1_gnn_gru_whh, L1_gnn_gru_bih, L1_gnn_gru_bhh, L1_gnn_out_w, L1_gnn_out_b), axis=-1)
    x = _layernorm(x + _L2_gnn_ref(x, edge_index, L2_gnn_Wn, L2_gnn_bn, L2_gnn_WQ, L2_gnn_bQ, L2_gnn_WK, L2_gnn_bK, L2_gnn_WV, L2_gnn_bV, L2_gnn_WO, L2_gnn_bO, L2_gnn_ln_g, L2_gnn_ln_b, L2_gnn_Wout, L2_gnn_bout), axis=-1)
    x = _layernorm(x + _L3_gnn_ref(x, edge_attr_32, edge_index, L3_gnn_C, edge_weight1, L3_gnn_W_emb, L3_gnn_b_emb, L3_gnn_We, L3_gnn_W_conv, L3_gnn_b_conv, L3_gnn_W_out, L3_gnn_b_out), axis=-1)
    return x

_drawn_inputs = setup_inputs


def setup_inputs(seed=0):
    import zlib

    import numpy as np

    out = dict(_drawn_inputs(seed))
    spreads = {'L1_gnn_out_b': (0.0, 0.1),
     'L2_gnn_bn': (0.0, 0.1),
     'L2_gnn_bQ': (0.0, 0.1),
     'L2_gnn_bK': (0.0, 0.8),
     'L2_gnn_bV': (0.0, 0.1),
     'L2_gnn_bO': (0.0, 0.1),
     'L2_gnn_ln_g': (1.0, 0.2),
     'L2_gnn_ln_b': (0.0, 0.1),
     'L2_gnn_bout': (0.0, 0.1),
     'L3_gnn_b_emb': (0.0, 0.1),
     'L3_gnn_b_conv': (0.0, 0.1),
     'L3_gnn_b_out': (0.0, 0.352)}
    factors = {'L0_gnn_b': 6.718, 'L1_gnn_gru_bhh': 3.772}
    for name, (base, spread) in spreads.items():
        noise = np.random.default_rng([zlib.crc32(name.encode()), seed]).standard_normal(out[name].shape)
        drawn = base * np.exp(spread * noise) if base else spread * noise
        out[name] = jnp.asarray(drawn.astype(out[name].dtype))
    for name, factor in factors.items():
        out[name] = (out[name] * factor).astype(out[name].dtype)
    return out
```

```python
import concourse.bass as bass
from concourse import mybir
from contextlib import ExitStack

F32 = mybir.dt.float32
BF16 = mybir.dt.bfloat16
I32 = mybir.dt.int32
I16 = mybir.dt.int16
ALU = mybir.AluOpType
ACT = mybir.ActivationFunctionType
AX = mybir.AxisListType
ds = bass.ds

P = 128
NODES = 3125
EDGES = 100000
NB = -(-NODES // P)
NP = NB * P
FULL_TILES = EDGES // P
LAST = EDGES - FULL_TILES * P
TILES = -(-EDGES // P)
TG = 4
NT = -(-(TILES + TG) // (2 * TG)) * 2 * TG
TC = -(-NT // P)
PAD_NODE = NP + 5
TYPES = 8
LAYERS1 = 2
LAYERS2 = 4
EF = 32
HALF = 400
CH = 2 * HALF
NCH = NP // CH
EPS = 1e-5
BIG = 4096.0
SHRINK = 2.0 ** -64
SCALE = float(P) ** -0.5
REC = P + 4


class Shared:
    pass


def halves(ap):
    return ap.rearrange("p (h n) -> p h n", h=2)


def bounded(value, top):
    return value.with_bounds(min_val=0, max_val=top, guaranteed_mod_val=0, out_of_modulus=1)


def constants(nc, s):
    filled, made = s.sem("const_filled"), s.sem("const_made")
    with nc.sbuf_tensor("ramp_i", [P, NP], I32) as ramp_i, nc.Block() as block:

        @block.vector
        def _(dve):
            dve.sem_inc(s.norm.normed, 1)

        @block.gpsimd
        def _(pool):
            pool.memset(s.ident[:, :], 0.0).then_inc(filled, 1)
            pool.memset(s.before[:, :], 0.0).then_inc(filled, 1)
            pool.memset(s.mean_w[:, :], 1.0 / P).then_inc(filled, 1)
            pool.memset(s.ones[:, :], 1.0).then_inc(filled, 1)
            pool.memset(s.zeros_bf[:, :], 0.0).then_inc(filled, 1)
            pool.memset(s.eps[:, :], EPS).then_inc(filled, 1)
            pool.iota(ramp_i[:, :], pattern=[[1, NP]], base=0, channel_multiplier=0).then_inc(filled, 1)
            pool.iota(s.tile_i[:, :], pattern=[[P, TC]], base=0, channel_multiplier=1).then_inc(filled, 1)
            pool.iota(s.start_i[:, :], pattern=[[P, NB + 1]], base=0, channel_multiplier=0).then_inc(filled, 1)
            pool.wait_ge(filled, 9)
            pool.affine_select(out=s.ident[:, :], in_=s.ident[:, :], compare_op=ALU.not_equal, fill=1.0,
                               base=0, pattern=[[-1, P]], channel_multiplier=1).then_inc(made, 1)
            pool.affine_select(out=s.before[:, :], in_=s.before[:, :], compare_op=ALU.is_ge, fill=1.0,
                               base=0, pattern=[[-1, P]], channel_multiplier=1).then_inc(made, 1)
            pool.tensor_copy(s.ramp[:, :], ramp_i[:, :]).then_inc(made, 1)
            pool.tensor_copy(s.ramp16[:, :], ramp_i[:, :]).then_inc(made, 1)
            pool.tensor_copy(s.tile_no[:, :], s.tile_i[:, :]).then_inc(made, 1)
            pool.tensor_copy(s.start[:, :], s.start_i[:, :]).then_inc(made, 1)
            pool.wait_ge(made, 6)


def load_edges(nc, s):
    padded, loaded, cast = s.sem("edge_padded"), s.sem("edge_loaded"), s.sem("edge_cast")
    turned, copied, ranged = s.sem("edge_turned"), s.sem("edge_copied"), s.sem("edge_ranged")
    range_pe, indexed = s.sem("edge_range_pe"), s.sem("edge_indexed")
    with ExitStack() as ctx:
        nat_i = ctx.enter_context(nc.sbuf_tensor("nat_i", [P, 3, TC, P], I32))
        nat = ctx.enter_context(nc.sbuf_tensor("nat", [P, 5, TC, P], F32))
        span = ctx.enter_context(nc.sbuf_tensor("span", [P, 2, TC], F32))
        tile_m = ctx.enter_context(nc.sbuf_tensor("tile_m", [P, 2, TC], F32))
        hit = ctx.enter_context(nc.sbuf_tensor("hit", [P, 3, TC, NB], F32))
        edge_t = ctx.enter_context(nc.sbuf_tensor("edge_t", [NB, 8], F32))
        edge_i = ctx.enter_context(nc.sbuf_tensor("edge_i", [NB, 2], I32))
        tmp = ctx.enter_context(nc.sbuf_tensor("index_tmp", [P, NT], F32))
        block = ctx.enter_context(nc.Block())
        sources = [(nat_i[:, 0], s.d_src), (nat_i[:, 1], s.d_dst), (nat_i[:, 2], s.d_type),
                   (nat[:, 3], s.d_weight), (nat[:, 4], s.d_weight1)]
        whole = FULL_TILES // P
        rest = FULL_TILES - whole * P

        @block.gpsimd
        def _(pool):
            for (dest, _), pad in zip(sources, [PAD_NODE, PAD_NODE, 0, 0.0, 0.0]):
                pool.memset(dest[:, whole, :], pad).then_inc(padded, 1)

        @block.sync
        def _(sp):
            sp.wait_ge(padded, 5)
            for dest, dram in sources:
                sp.dma_start(dest[:, 0:whole, :],
                             dram[0:whole * P * P].rearrange("(c p j) -> p c j", c=whole, p=P)).then_inc(loaded, 16)
                sp.dma_start(dest[0:rest, whole, :],
                             dram[whole * P * P:FULL_TILES * P].rearrange("(p j) -> p j", j=P)).then_inc(loaded, 16)
                sp.dma_start(dest[rest:rest + 1, whole, 0:LAST],
                             dram[FULL_TILES * P:EDGES].rearrange("(p j) -> p j", p=1)).then_inc(loaded, 16)

        banks = [s.ps[:, n, :] for n in range(8)]

        @block.tensor
        def _(pe):
            pe.wait_ge(cast, 3)
            for n in range(5):
                if n >= 3:
                    pe.wait_ge(copied, 2 * (n - 2))
                for c in range(TC):
                    nc.tensor.transpose(banks[2 * (n % 3) + c // 4][:, (c % 4) * P:(c % 4 + 1) * P],
                                        nat[:, n, c, :], s.ident[:, :]).then_inc(turned, 1)
            pe.wait_ge(ranged, 2 + 4 * TC + 2)
            pe.wait_ge(copied, 10)
            for v in range(2):
                for c in range(TC):
                    nc.tensor.transpose(banks[2 * v + c // 4][0:NB, (c % 4) * P:(c % 4 + 1) * P],
                                        hit[:, 1 + v, c, :], s.ident[:, :]).then_inc(range_pe, 1)
            pe.wait_ge(indexed, 7)
            nc.tensor.matmul(banks[4][0:1, 0:NB], edge_t[:, 4:5], s.ident[0:NB, 0:NB], start=True, stop=True).then_inc(range_pe, 1)
            nc.tensor.matmul(banks[5][0:1, 0:NB], edge_t[:, 5:6], s.ident[0:NB, 0:NB], start=True, stop=True).then_inc(range_pe, 1)
            nc.tensor.matmul(banks[6][0:1, 0:NB], edge_t[:, 5:6], s.before[0:NB, 0:NB], start=True, stop=True).then_inc(range_pe, 1)

        @block.vector
        def _(dve):
            dve.wait_ge(loaded, 16 * 15)
            for n in range(3):
                nc.vector.tensor_copy(nat[:, n], nat_i[:, n]).then_inc(cast, 1)
            dve.wait_ge(cast, 3)
            nc.vector.tensor_reduce(out=span[:, 0, :], in_=nat[:, 1], axis=AX.X, op=ALU.min).then_inc(ranged, 1)
            nc.vector.tensor_reduce(out=span[:, 1, :], in_=nat[:, 1], axis=AX.X, op=ALU.max).then_inc(ranged, 1)
            nc.vector.tensor_scalar(tile_m[:, 0, :], s.tile_no[:, :], -BIG, None, ALU.add).then_inc(ranged, 1)
            nc.vector.tensor_scalar(tile_m[:, 1, :], s.tile_no[:, :], 1.0, None, ALU.add).then_inc(ranged, 1)
            dve.wait_ge(ranged, 4)
            for c in range(TC):
                nc.vector.tensor_scalar(hit[:, 0, c, :], s.start[:, 0:NB], span[:, 1, c:c + 1], None, ALU.is_le).then_inc(ranged, 1)
                dve.wait_ge(ranged, 4 + 4 * c + 1)
                nc.vector.scalar_tensor_tensor(out=hit[:, 0, c, :], in0=s.start[:, 1:NB + 1], scalar=span[:, 0, c:c + 1],
                                               in1=hit[:, 0, c, :], op0=ALU.is_gt, op1=ALU.mult).then_inc(ranged, 1)
                dve.wait_ge(ranged, 4 + 4 * c + 2)
                nc.vector.tensor_scalar(hit[:, 1, c, :], hit[:, 0, c, :], tile_m[:, 0, c:c + 1], BIG, ALU.mult, ALU.add).then_inc(ranged, 1)
                nc.vector.tensor_scalar(hit[:, 2, c, :], hit[:, 0, c, :], tile_m[:, 1, c:c + 1], None, ALU.mult).then_inc(ranged, 1)
            for n, column in enumerate([s.src, s.dst, s.typ, s.weight, s.weight1]):
                for h, (lo, hi) in enumerate([(0, 4), (4, TC)]):
                    dve.wait_ge(turned, TC * n + hi)
                    nc.vector.tensor_copy(column[:, lo * P:hi * P], banks[2 * (n % 3) + h][:, 0:(hi - lo) * P]).then_inc(copied, 1)
            dve.wait_ge(range_pe, 2 * TC)
            for v, op in enumerate([ALU.min, ALU.max]):
                nc.vector.tensor_reduce(out=edge_t[:, 2 * v:2 * v + 1], in_=banks[2 * v][0:NB, 0:4 * P], axis=AX.X, op=op).then_inc(indexed, 1)
                nc.vector.tensor_reduce(out=edge_t[:, 2 * v + 1:2 * v + 2], in_=banks[2 * v + 1][0:NB, 0:(TC - 4) * P], axis=AX.X, op=op).then_inc(indexed, 1)
            dve.wait_ge(indexed, 4)
            nc.vector.tensor_tensor(edge_t[:, 4:5], edge_t[:, 0:1], edge_t[:, 1:2], ALU.min).then_inc(indexed, 1)
            nc.vector.tensor_tensor(edge_t[:, 6:7], edge_t[:, 2:3], edge_t[:, 3:4], ALU.max).then_inc(indexed, 1)
            dve.wait_ge(indexed, 6)
            s.groups_of(nc, dve, edge_t, edge_i, 4, 6, 5, s.sem("edge_groups"), indexed)
            dve.wait_ge(range_pe, 2 * TC + 3)
            for r in range(3):
                nc.vector.tensor_copy(s.dst_range[0:1, r, :], banks[4 + r][0:1, 0:NB]).then_inc(ranged, 1)
            dve.wait_ge(copied, 10)
            nc.vector.tensor_scalar(s.src_row[:, :], s.src[:, 0:NT], float(NODES - 1), None, ALU.min).then_inc(ranged, 1)
            nc.vector.tensor_scalar(s.dst_row[:, :], s.dst[:, 0:NT], float(NODES - 1), None, ALU.min).then_inc(ranged, 1)
            nc.vector.tensor_scalar(tmp[:, :], s.src[:, 0:NT], float(NODES - 1), None, ALU.min).then_inc(indexed, 1)
            dve.wait_ge(indexed, 8)
            nc.vector.scalar_tensor_tensor(out=s.typed_row[:, :], in0=s.typ[:, 0:NT], scalar=float(NP), in1=tmp[:, :],
                                           op0=ALU.mult, op1=ALU.add).then_inc(ranged, 1)


def groups_of(nc, dve, t, ti, lo, hi, out, chain, done):
    nc.vector.tensor_scalar(t[:, lo:lo + 1], t[:, lo:lo + 1], float(NT - TG), None, ALU.min).then_inc(chain, 1)
    dve.wait_ge(chain, 1)
    nc.vector.tensor_tensor(t[:, hi:hi + 1], t[:, hi:hi + 1], t[:, lo:lo + 1], ALU.subtract).then_inc(chain, 1)
    dve.wait_ge(chain, 2)
    nc.vector.tensor_scalar(ti[:, 0:1], t[:, hi:hi + 1], float(TG - 1), float(TG), ALU.add, ALU.max).then_inc(chain, 1)
    dve.wait_ge(chain, 3)
    nc.vector.tensor_scalar(ti[:, 1:2], ti[:, 0:1], TG.bit_length() - 1, None, ALU.arith_shift_right).then_inc(chain, 1)
    dve.wait_ge(chain, 4)
    nc.vector.tensor_copy(t[:, out:out + 1], ti[:, 1:2]).then_inc(done, 1)


def load_nodes(nc, s):
    loaded, turned, copied, padded = s.sem("node_loaded"), s.sem("node_turned"), s.sem("node_copied"), s.sem("node_padded")
    with ExitStack() as ctx:
        xn = ctx.enter_context(nc.sbuf_tensor("x_nodes", [P, NB, P], F32))
        nw = 2 + LAYERS1 * (TYPES + 6)
        wn = ctx.enter_context(nc.sbuf_tensor("w_rows", [P, nw, P], F32))
        block = ctx.enter_context(nc.Block())

        @block.gpsimd
        def _(pool):
            pool.memset(xn[:, NB - 1, :], 0.0).then_inc(padded, 1)

        @block.scalar
        def _(act):
            act.dma_start(wn[:, 0, :], s.d_proj_w).then_inc(loaded, 16)
            act.dma_start(wn[:, 1, :], s.d_out_w).then_inc(loaded, 16)
            for l in range(LAYERS1):
                o = 2 + l * (TYPES + 6)
                act.dma_start(wn[:, o:o + TYPES, :], s.d_edge_W[l].rearrange("t d h -> d t h")).then_inc(loaded, 16)
                act.dma_start(wn[:, o + TYPES:o + TYPES + 3, :], s.d_wih[l].rearrange("(g d) h -> d g h", d=P)).then_inc(loaded, 16)
                act.dma_start(wn[:, o + TYPES + 3:o + TYPES + 6, :], s.d_whh[l].rearrange("(g d) h -> d g h", d=P)).then_inc(loaded, 16)
            for column, dram in s.bias_loads:
                act.dma_start(column, dram).then_inc(loaded, 16)
            act.dma_start(s.W0[:, :], s.d_W0).then_inc(loaded, 16)
            act.dma_start(s.Wn[:, :], s.d_Wn).then_inc(loaded, 16)
            act.dma_start(s.Wout[:, :], s.d_Wout).then_inc(loaded, 16)

        @block.sync
        def _(sp):
            sp.wait_ge(padded, 1)
            sp.dma_start(xn[:, 0:NB - 1, :], s.d_x[0:(NB - 1) * P, :].rearrange("(b p) f -> p b f", p=P)).then_inc(loaded, 16)
            sp.dma_start(xn[0:NODES - (NB - 1) * P, NB - 1, :], s.d_x[(NB - 1) * P:NODES, :]).then_inc(loaded, 16)

        count = 16 * (2 + 2 + 3 * LAYERS1 + len(s.bias_loads) + 3)
        todo = [(xn[:, b, :], s.xT[:, b * P:(b + 1) * P]) for b in range(NB)]
        todo += [(wn[:, n, :], s.wT[:, n, :]) for n in range(nw)]

        @block.tensor
        def _(pe):
            pe.wait_ge(loaded, count)
            for k, (source, _) in enumerate(todo):
                if k >= 8:
                    pe.wait_ge(copied, k - 7)
                nc.tensor.transpose(s.ps[:, k % 8, 0:P], source, s.ident[:, :]).then_inc(turned, 1)

        @block.vector
        def _(dve):
            for k, (_, dest) in enumerate(todo):
                dve.wait_ge(turned, k + 1)
                nc.vector.tensor_copy(dest, s.ps[:, k % 8, 0:P]).then_inc(copied, 1)
            dve.wait_ge(loaded, count)
            nc.vector.tensor_tensor(s.b_rz[:, :, :], s.bih[:, :, 0:2], s.bhh[:, :, 0:2], ALU.add).then_inc(padded, 1)


def edge_pass(nc, s, name, table, rows, ranges, weighted=False, build_counts=False):
    copied, granted = s.sem(name + "_index_copied"), s.sem(name + "_granted")
    gathered = [s.sem(f"{name}_gathered{h}") for h in range(2)]
    row_free = [s.sem(f"{name}_row_free{h}") for h in range(2)]
    stored = [s.sem(f"{name}_stored{h}") for h in range(2)]
    back = [s.sem(f"{name}_back{h}") for h in range(2)]
    picked = [s.sem(f"{name}_picked{h}") for h in range(2)]
    used = [s.sem(f"{name}_used{h}") for h in range(2)]
    summed, sum_read = s.sem(name + "_summed"), s.sem(name + "_sum_read")
    count_read, count_stored = s.sem(name + "_count_read"), s.sem(name + "_count_stored")
    turns = NT // (2 * TG)
    with ExitStack() as ctx:
        index = [ctx.enter_context(nc.sbuf_tensor(f"{name}_index{h}", [P, TG], I32)) for h in range(2)]
        fetched = [ctx.enter_context(nc.sbuf_tensor(f"{name}_fetched{h}", [P, TG, P], F32)) for h in range(2)]
        width = P if table is not None else REC
        store = s.edge_rows if table is not None else s.records
        edge_rows = store[:, :].rearrange("(t p) f -> p t f", p=P)
        feat = [ctx.enter_context(nc.sbuf_tensor(f"{name}_feat{h}", [P, TG // 2, width], F32)) for h in range(2)]
        pick = [ctx.enter_context(nc.sbuf_tensor(f"{name}_pick{h}", [P, TG // 2, P], F32)) for h in range(2)]
        if build_counts:
            pick_d = [ctx.enter_context(nc.sbuf_tensor(f"{name}_pick_d{h}", [P, TG // 2, P], BF16)) for h in range(2)]
            pick_s = [ctx.enter_context(nc.sbuf_tensor(f"{name}_pick_s{h}", [P, TG // 2, NP], BF16)) for h in range(2)]
            count_row = ctx.enter_context(nc.sbuf_tensor(f"{name}_count_row", [P, NP], F32))
        block = ctx.enter_context(nc.Block())
        agg = s.ps[:, 7, 0:P]
        counts = s.ps[:, 0:7, :].rearrange("p b n -> p (b n)")
        ACT_COLS = 3 * 512

        @block.gpsimd
        def _(pool):
            if table is None:
                return
            with pool.Fori(0, turns) as i:
                for h in range(2):
                    pool.wait_ge(row_free[h], i + 1)
                    nc.gpsimd.tensor_copy(index[h][:, :], rows[:, ds(i * (2 * TG) + TG * h, TG)]).then_inc(copied, 1)
                    pool.wait_ge(copied, i * 2 + h + 1)
                    pool.sem_inc(granted, 1)
                    for j in range(TG):
                        nc.gpsimd.indirect_dma_start(out=fetched[h][:, j, :], out_offset=None, in_=table,
                                                     in_offset=bass.IndirectOffsetOnAxis(ap=index[h][:, j:j + 1], axis=0)
                                                     ).then_inc(gathered[h], 16)

        @block.sync
        def _(sp):
            if table is None:
                return
            for h in range(2):
                sp.sem_inc(row_free[h], 1)
            with sp.Fori(0, turns) as i:
                for h in range(2):
                    sp.wait_ge(gathered[h], i * (16 * TG) + 16 * TG)
                    sp.dma_start(edge_rows[:, ds(i * (2 * TG) + TG * h, TG), :], fetched[h][:, :, :]).then_inc(stored[h], 16)
                    sp.wait_ge(stored[h], i * 16 + 16)
                    sp.sem_inc(row_free[h], 1)

        @block.scalar
        def _(act):
            act.sem_inc(sum_read, 1)
            if build_counts:
                act.sem_inc(count_read, 2)

            def node_block(b):
                first = act.value_load(ranges[0:1, 0, ds(b, 1)], min_val=0, max_val=NT - TG)
                groups = act.value_load(ranges[0:1, 1, ds(b, 1)], min_val=1, max_val=NT // TG)
                before = act.value_load(ranges[0:1, 2, ds(b, 1)], min_val=0, max_val=NB * NT // TG)
                with act.Fori(0, groups) as i:
                    for h in range(2):
                        tile = bounded(first + i * TG + 2 * h, NT - 2)
                        turn = ((tile + 1) >> 3) + 1
                        if table is not None:
                            act.wait_ge(stored[0], turn * 16)
                            act.wait_ge(stored[1], turn * 16)
                        act.wait_ge(used[h], before + i + 1)
                        act.dma_start(feat[h][:, :, :], edge_rows[:, ds(tile, 2), :]).then_inc(back[h], 16)
                act.wait_ge(summed, b + 1)
                nc.scalar.activation(s.aggT[:, ds(b * P, P)], agg, ACT.Copy).then_inc(sum_read, 1)
                if build_counts:
                    if not isinstance(b, int):
                        act.wait_ge(count_stored, b * 16)
                    nc.scalar.activation(count_row[:, 0:ACT_COLS], counts[:, 0:ACT_COLS], ACT.Copy).then_inc(count_read, 1)
                    act.wait_ge(count_read, b * 2 + 4)
                    act.dma_start(s.counts[ds(b, 1), :, :].rearrange("o p n -> (o p) n"), count_row[:, :]).then_inc(count_stored, 16)

            node_block(0)
            with act.Fori(1, NB) as b:
                node_block(b)
            if build_counts:
                act.wait_ge(count_stored, 16 * NB)

        @block.vector
        def _(dve):
            def node_block(b):
                first = dve.value_load(ranges[0:1, 0, ds(b, 1)], min_val=0, max_val=NT - TG)
                groups = dve.value_load(ranges[0:1, 1, ds(b, 1)], min_val=1, max_val=NT // TG)
                before = dve.value_load(ranges[0:1, 2, ds(b, 1)], min_val=0, max_val=NB * NT // TG)
                with dve.Fori(0, groups) as i:
                    for h in range(2):
                        dve.wait_ge(used[h], before + i + 1)
                        if table is None:
                            dve.wait_ge(back[h], (before + i) * 16 + 16)
                        for j in range(2):
                            tile = bounded(first + i * TG + 2 * h + j, NT - 1)
                            here = s.ramp[:, ds(b * P, P)]
                            if build_counts:
                                nc.vector.tensor_scalar(pick_s[h][:, j, :], s.ramp16[:, :], s.src[:, ds(tile, 1)], None, ALU.is_equal)
                                nc.vector.tensor_scalar(pick_d[h][:, j, :], here, s.dst[:, ds(tile, 1)], None, ALU.is_equal)
                            if weighted:
                                last = nc.vector.tensor_scalar(pick[h][:, j, :], here, s.dst[:, ds(tile, 1)],
                                                               s.weight[:, ds(tile, 1)], ALU.is_equal, ALU.mult)
                            elif table is None:
                                last = nc.vector.tensor_scalar(pick[h][:, j, :], here, feat[h][:, j, P:P + 1], None, ALU.is_equal)
                            else:
                                last = nc.vector.tensor_scalar(pick[h][:, j, :], here, s.dst[:, ds(tile, 1)], None, ALU.is_equal)
                        last.then_inc(picked[h], 1)
                if build_counts:
                    dve.wait_ge(summed, b + 1)
                    if not isinstance(b, int):
                        dve.wait_ge(count_stored, b * 16)
                    nc.vector.tensor_copy(count_row[:, ACT_COLS:NP], counts[:, ACT_COLS:NP]).then_inc(count_read, 1)

            node_block(0)
            with dve.Fori(1, NB) as b:
                node_block(b)

        @block.tensor
        def _(pe):
            cuts = [(c, min(512, NP - c)) for c in range(0, NP, 512)]
            for h in range(2):
                pe.sem_inc(used[h], 1)
            with pe.Fori(0, NB) as b:
                groups = pe.value_load(ranges[0:1, 1, ds(b, 1)], min_val=1, max_val=NT // TG)
                before = pe.value_load(ranges[0:1, 2, ds(b, 1)], min_val=0, max_val=NB * NT // TG)
                pe.wait_ge(sum_read, b + 1)
                nc.tensor.matmul(agg, s.zeros_bf[:, 0:P], s.zeros_bf[:, 0:P], start=True, stop=False)
                if build_counts:
                    pe.wait_ge(count_read, b * 2 + 2)
                    for c, n in cuts:
                        nc.tensor.matmul(counts[:, c:c + n], s.zeros_bf[:, 0:P], s.zeros_bf[:, 0:n], start=True, stop=False)
                with pe.Fori(0, groups) as i:
                    for h in range(2):
                        pe.wait_ge(picked[h], before + i + 1)
                        if build_counts:
                            for j in range(2):
                                for c, n in cuts:
                                    nc.tensor.matmul(counts[:, c:c + n], pick_d[h][:, j, :], pick_s[h][:, j, c:c + n],
                                                     start=False, stop=False)
                        pe.wait_ge(back[h], (before + i) * 16 + 16)
                        for j in range(2):
                            last = nc.tensor.matmul(agg, feat[h][:, j, 0:P], pick[h][:, j, :], start=False, stop=False)
                        last.then_inc(used[h], 1)
                if build_counts:
                    for c, n in cuts:
                        nc.tensor.matmul(counts[:, c:c + n], s.zeros_bf[:, 0:P], s.zeros_bf[:, 0:n], start=False, stop=True)
                nc.tensor.matmul(agg, s.zeros_bf[:, 0:P], s.zeros_bf[:, 0:P], start=False, stop=True).then_inc(summed, 1)


class Norm:

    def __init__(self, s):
        self.given, self.mean_ready, self.centred = s.sem("norm_given"), s.sem("norm_mean"), s.sem("norm_centred")
        self.squared, self.var_ready, self.std_ready = s.sem("norm_squared"), s.sem("norm_var"), s.sem("norm_std")
        self.rstd_ready, self.scaled, self.normed = s.sem("norm_rstd"), s.sem("norm_scaled"), s.sem("norm_done")
        self.turns = 0
        self.gained = 0

    def pe(self, nc, pe, s, t):
        pe.wait_ge(self.given, t + 1)
        for h in range(2):
            last = nc.tensor.matmul(s.ps[:, h, 0:HALF], s.mean_w[:, :], s.y[:, h, :], start=True, stop=True)
        last.then_inc(self.mean_ready, 1)
        pe.wait_ge(self.squared, t + 1)
        for h in range(2):
            last = nc.tensor.matmul(s.ps[:, 2 + h, 0:HALF], s.mean_w[:, :], s.sq[:, h, :], start=True, stop=True)
        last.then_inc(self.var_ready, 1)

    def act(self, nc, act, s, t):
        act.wait_ge(self.var_ready, t + 1)
        nc.scalar.activation(s.std[:, :, :], s.ps[:, 2:4, 0:HALF], ACT.Sqrt, bias=s.eps[:, 0:1]).then_inc(self.std_ready, 1)

    def dve(self, nc, dve, s, t, out, gain=None, shift=None, gained=0):
        dve.wait_ge(self.given, t + 1)
        dve.wait_ge(self.mean_ready, t + 1)
        nc.vector.tensor_tensor(s.yc[:, :, :], s.y[:, :, :], s.ps[:, 0:2, 0:HALF], ALU.subtract).then_inc(self.centred, 1)
        dve.wait_ge(self.centred, t + 1)
        nc.vector.tensor_tensor(s.sq[:, :, :], s.yc[:, :, :], s.yc[:, :, :], ALU.mult).then_inc(self.squared, 1)
        dve.wait_ge(self.std_ready, t + 1)
        nc.vector.reciprocal(s.std[:, :, :], s.std[:, :, :]).then_inc(self.rstd_ready, 1)
        dve.wait_ge(self.rstd_ready, t + 1)
        if gain is None:
            nc.vector.tensor_tensor(out, s.yc[:, :, :], s.std[:, :, :], ALU.mult).then_inc(self.normed, 1)
        else:
            nc.vector.tensor_tensor(s.yc[:, :, :], s.yc[:, :, :], s.std[:, :, :], ALU.mult).then_inc(self.scaled, 1)
            dve.wait_ge(self.scaled, gained + 1)
            nc.vector.tensor_scalar(out, s.yc[:, :, :], gain, shift, ALU.mult, ALU.add).then_inc(self.normed, 1)


def node_phase(nc, s, name, weight, source, func, bias, base, gain=None, shift=None, second=None, layer=0):
    key = "node_" + name
    lin, applied, lin2, applied2 = s.sem(key + "_lin"), s.sem(key + "_applied"), s.sem(key + "_lin2"), s.sem(key + "_applied2")
    n = s.norm
    start = n.turns + layer * NCH
    with nc.Block() as block:

        @block.tensor
        def _(pe):
            with pe.Fori(0, NCH) as c:
                pe.wait_ge(n.normed, start + c + 1)
                for h in range(2):
                    last = nc.tensor.matmul(s.ps[:, 4 + h, 0:HALF], weight, source[:, ds(c * CH + h * HALF, HALF)], start=True, stop=True)
                last.then_inc(lin, 1)
                n.pe(nc, pe, s, start + c)
                if second:
                    pe.wait_ge(n.normed, start + c + 2)
                    for h in range(2):
                        last = nc.tensor.matmul(s.ps[:, 6 + h, 0:HALF], second[0], base[:, ds(c * CH + h * HALF, HALF)], start=True, stop=True)
                    last.then_inc(lin2, 1)
                    pe.wait_ge(applied2, c + 1)

        @block.scalar
        def _(act):
            with act.Fori(0, NCH) as c:
                act.wait_ge(lin, layer * NCH + c + 1)
                nc.scalar.activation(s.y[:, :, :], s.ps[:, 4:6, 0:HALF], func, bias=bias).then_inc(applied, 1)
                n.act(nc, act, s, start + c)
                if second:
                    act.wait_ge(lin2, c + 1)
                    nc.scalar.activation(halves(second[3][:, ds(c * CH, CH)]), s.ps[:, 6:8, 0:HALF], second[1], bias=second[2]).then_inc(applied2, 1)

        @block.vector
        def _(dve):
            with dve.Fori(0, NCH) as c:
                dve.wait_ge(applied, layer * NCH + c + 1)
                nc.vector.tensor_tensor(s.y[:, :, :], s.y[:, :, :], halves(base[:, ds(c * CH, CH)]), ALU.add).then_inc(n.given, 1)
                n.dve(nc, dve, s, start + c, halves(base[:, ds(c * CH, CH)]), gain, shift, n.gained + layer * NCH + c)


def node_rows(nc, s, name, source, right, width, write):
    key = "rows_" + name
    held, made, read = s.sem(key + "_held"), s.sem(key + "_made"), s.sem(key + "_read")
    row_free, stored = s.sem(key + "_free"), s.sem(key + "_stored")
    with ExitStack() as ctx:
        hold = ctx.enter_context(nc.sbuf_tensor(key + "_hold", [P, P], F32))
        row = ctx.enter_context(nc.sbuf_tensor(key + "_row", [P, 2, width], F32))
        block = ctx.enter_context(nc.Block())
        banks = -(-width // 512)
        ps = s.ps[:, :, :].rearrange("p b n -> p (b n)")

        @block.vector
        def _(dve):
            def step(b):
                if not isinstance(b, int):
                    dve.wait_ge(made, b)
                nc.vector.tensor_copy(hold[:, :], source[:, ds(b * P, P)]).then_inc(held, 1)
            step(0)
            with dve.Fori(1, NB) as b:
                step(b)

        @block.tensor
        def _(pe):
            with pe.Fori(0, NB) as b:
                pe.wait_ge(held, b + 1)
                pe.wait_ge(read, b + 1)
                base = (b & 1) * (512 * banks)
                for c in range(0, width, 512):
                    last = nc.tensor.matmul(ps[:, ds(base + c, min(512, width - c))], hold[:, :],
                                            right[:, c:min(c + 512, width)], start=True, stop=True)
                last.then_inc(made, 1)

        @block.scalar
        def _(act):
            act.sem_inc(read, 2)
            with act.Fori(0, NB) as b:
                act.wait_ge(made, b + 1)
                act.wait_ge(row_free, b + 1)
                nc.scalar.activation(row[:, ds(b & 1, 1), :].rearrange("p o n -> p (o n)"), ps[:, ds((b & 1) * (512 * banks), width)], ACT.Copy).then_inc(read, 1)

        @block.sync
        def _(sp):
            sp.sem_inc(row_free, 2)

            def step(b, parity):
                sp.wait_ge(read, b + 3)
                write(sp, b, row[:, ds(parity, 1), :].rearrange("p o n -> p (o n)"), stored)
                sp.wait_ge(stored, b * 16 + 16)
                sp.sem_inc(row_free, 1)
            with sp.Fori(0, NB - 1) as b:
                step(b, b & 1)
            step(NB - 1, (NB - 1) & 1)


def gru(nc, s, l):
    key = f"gru{l}"
    gates, rz, hn, pre, tanh = (s.sem(f"{key}_{x}") for x in ("gates", "rz", "hn", "pre", "tanh"))
    diff, mixed, summed, done = (s.sem(f"{key}_{x}") for x in ("diff", "mixed", "summed", "done"))
    with ExitStack() as ctx:
        r, z, n, d = (ctx.enter_context(nc.sbuf_tensor(f"{key}_t{x}", [P, 2, HALF], F32)) for x in "rznd")
        block = ctx.enter_context(nc.Block())
        o = 2 + l * (TYPES + 6) + TYPES

        @block.tensor
        def _(pe):
            def turn(c):
                if not isinstance(c, int):
                    pe.wait_ge(done, c)
                for h in range(2):
                    at = ds(c * CH + h * HALF, HALF)
                    for g in range(2):
                        nc.tensor.matmul(s.ps[:, 2 * g + h, 0:HALF], s.wT[:, o + g, :], s.aggT[:, at], start=True, stop=False)
                        nc.tensor.matmul(s.ps[:, 2 * g + h, 0:HALF], s.wT[:, o + 3 + g, :], s.hT[:, at], start=False, stop=True)
                    nc.tensor.matmul(s.ps[:, 4 + h, 0:HALF], s.wT[:, o + 2, :], s.aggT[:, at], start=True, stop=True)
                    last = nc.tensor.matmul(s.ps[:, 6 + h, 0:HALF], s.wT[:, o + 5, :], s.hT[:, at], start=True, stop=True)
                last.then_inc(gates, 1)
            turn(0)
            with pe.Fori(1, NCH) as c:
                turn(c)

        @block.scalar
        def _(act):
            with act.Fori(0, NCH) as c:
                act.wait_ge(gates, c + 1)
                nc.scalar.activation(r[:, :, :], s.ps[:, 0:2, 0:HALF], ACT.Sigmoid, bias=s.b_rz[:, l, 0:1]).then_inc(rz, 1)
                nc.scalar.activation(z[:, :, :], s.ps[:, 2:4, 0:HALF], ACT.Sigmoid, bias=s.b_rz[:, l, 1:2]).then_inc(rz, 1)
                act.wait_ge(pre, c + 1)
                nc.scalar.activation(n[:, :, :], d[:, :, :], ACT.Tanh, bias=s.bih[:, l, 2:3]).then_inc(tanh, 1)

        @block.vector
        def _(dve):
            with dve.Fori(0, NCH) as c:
                h = halves(s.hT[:, ds(c * CH, CH)])
                dve.wait_ge(rz, c * 2 + 2)
                nc.vector.scalar_tensor_tensor(out=r[:, :, :], in0=s.ps[:, 6:8, 0:HALF], scalar=s.bhh[:, l, 2:3], in1=r[:, :, :],
                                               op0=ALU.add, op1=ALU.mult).then_inc(hn, 1)
                dve.wait_ge(hn, c + 1)
                nc.vector.tensor_tensor(d[:, :, :], r[:, :, :], s.ps[:, 4:6, 0:HALF], ALU.add).then_inc(pre, 1)
                dve.wait_ge(tanh, c + 1)
                nc.vector.tensor_tensor(d[:, :, :], h, n[:, :, :], ALU.subtract).then_inc(diff, 1)
                dve.wait_ge(diff, c + 1)
                nc.vector.tensor_tensor(d[:, :, :], d[:, :, :], z[:, :, :], ALU.mult).then_inc(mixed, 1)
                dve.wait_ge(mixed, c + 1)
                nc.vector.tensor_tensor(d[:, :, :], d[:, :, :], n[:, :, :], ALU.add).then_inc(summed, 1)
                dve.wait_ge(summed, c + 1)
                nc.vector.tensor_scalar(h, d[:, :, :], 0.0, None, ALU.max).then_inc(done, 1)


def project(nc, s, a, l):
    loaded, cols, lin, moved = a.weights_loaded, a.columns, a.lin, a.moved
    held, made, read = a.held, a.made, a.read
    with nc.Block() as block:

        @block.sync
        def _(sp):
            for n, w in enumerate((a.WQ, a.WK, a.WV, a.WO)):
                sp.dma_start(a.w[:, n, :], w[ds(l, 1), :, :].rearrange("l i o -> (l i) o")).then_inc(loaded, 16)
            sp.dma_start(a.bv[:, :], a.bV[ds(l, 1), :]).then_inc(loaded, 16)

        @block.tensor
        def _(pe):
            pe.wait_ge(loaded, l * 80 + 80)
            pe.sem_inc(a.passed, 1)
            with pe.Fori(0, NCH) as c:
                pe.wait_ge(moved, (l * NCH + c) * 2 + 2)
                for n in range(2):
                    for h in range(2):
                        last = nc.tensor.matmul(s.ps[:, 2 * n + h, 0:HALF], a.w[:, n, :], s.hT[:, ds(c * CH + h * HALF, HALF)], start=True, stop=True)
                last.then_inc(lin, 1)
            with pe.Fori(0, NB) as b:
                pe.wait_ge(held, l * NB + b + 1)
                pe.wait_ge(read, l * NB + b + 1)
                nc.tensor.matmul(s.ps[:, 4, 0:P], a.hold[:, :], a.w[:, 2, :], start=True, stop=False)
                nc.tensor.matmul(s.ps[:, 4, 0:P], s.ones[0:1, :], a.bv[0:1, :], start=False, stop=True).then_inc(made, 1)

        @block.scalar
        def _(act):
            act.wait_ge(cols, (l + 1) * 5)
            with act.Fori(0, NCH) as c:
                act.wait_ge(lin, l * NCH + c + 1)
                nc.scalar.activation(halves(a.qT[:, ds(c * CH, CH)]), s.ps[:, 0:2, 0:HALF], ACT.Identity, bias=a.col[:, 0:1]).then_inc(moved, 1)
                nc.scalar.activation(halves(a.kT[:, ds(c * CH, CH)]), s.ps[:, 2:4, 0:HALF], ACT.Identity, bias=a.col[:, 1:2], scale=SHRINK).then_inc(moved, 1)
            with act.Fori(0, NB) as b:
                act.wait_ge(made, l * NB + b + 2)
                nc.scalar.activation(a.v[:, ds(b, 1), 0:P].rearrange("p o f -> p (o f)"), s.ps[:, 4, 0:P], ACT.Copy).then_inc(read, 1)

        @block.vector
        def _(dve):
            for n, (column, factor) in enumerate(((s.bQ, 1.0), (s.bK, SHRINK), (s.bO, 1.0), (s.ln_g, 1.0), (s.ln_b, 1.0))):
                nc.vector.tensor_scalar(a.col[:, n:n + 1], column[:, ds(l, 1)], factor, None, ALU.mult).then_inc(cols, 1)
            with dve.Fori(0, NB) as b:
                dve.wait_ge(made, l * NB + b + 1)
                nc.vector.tensor_copy(a.hold[:, :], s.hT[:, ds(b * P, P)]).then_inc(held, 1)


def attend(nc, s, a, l):
    SC = NP // HALF
    GROUPS = -(-NB // 4)
    with nc.Block() as block:
        def k(b):
            return l * NB + b

        @block.sync
        def _(sp):
            with sp.Fori(0, NB) as b:
                sp.wait_ge(a.count_used, k(b) + 1)
                sp.sem_inc(a.passed, 1)
                sp.dma_start(a.cnt[:, ds(k(b) & 1, 1), :].rearrange("p o n -> p (o n)"),
                             s.counts[ds(b, 1), :, :].rearrange("o p n -> (o p) n")).then_inc(a.count_back, 16)
                sp.wait_ge(a.count_back, k(b) * 16 + 16)
                sp.sem_inc(a.passed, 1)

        @block.tensor
        def _(pe):
            def scores(b):
                pe.wait_ge(a.q_held, k(b) + 1)
                for c in range(SC):
                    pe.wait_ge(a.masked, k(b) * SC + c + 1)
                    nc.tensor.matmul(s.ps[:, c % 4, 0:HALF], a.q[:, :], a.kT[:, c * HALF:(c + 1) * HALF], start=True, stop=True).then_inc(a.scored, 1)

            def turn_result(b):
                pe.wait_ge(a.msg_read, k(b) + 2)
                pe.wait_ge(a.att_read, k(b) + 1)
                nc.tensor.transpose(s.ps[:, 7, 0:P], a.msg[:, :], s.ident[:, :]).then_inc(a.msg_turned, 1)

            def values(b):
                def turn_group(g):
                    pe.wait_ge(a.pt_read, k(b) * GROUPS + g + 1)
                    for n in range(4 * g, min(4 * g + 4, NB)):
                        last = nc.tensor.transpose(s.ps[:, 4 + g % 2, (n % 4) * P:(n % 4 + 1) * P], a.pm[:, n * P:(n + 1) * P], s.ident[:, :])
                    last.then_inc(a.turned, 1)

                def add_group(g):
                    pe.wait_ge(a.pt_read, k(b) * GROUPS + g + 3)
                    for n in range(4 * g, min(4 * g + 4, NB)):
                        last = nc.tensor.matmul(s.ps[:, 6, 0:P + 1], a.pt[:, n * P:(n + 1) * P], a.v[:, n, 0:P + 1], start=n == 0, stop=n == NB - 1)
                    return last

                pe.wait_ge(a.weighed, k(b) * SC + SC)
                turn_group(0)
                turn_group(1)
                pe.wait_ge(a.msg_read, k(b) + 1)
                for g in range(GROUPS):
                    last = add_group(g)
                    if g + 2 < GROUPS:
                        turn_group(g + 2)
                last.then_inc(a.summed, 1)

            scores(0)
            scores(1)
            values(0)
            with pe.Fori(2, NB) as b:
                scores(b)
                turn_result(b - 2)
                values(b - 1)
            turn_result(NB - 2)
            values(NB - 1)
            turn_result(NB - 1)

        @block.scalar
        def _(act):
            def exps(b):
                act.wait_ge(a.biased, k(b) + 1)
                for h in range(2):
                    at = ds((k(b) & 1) * NP + h * (NP // 2), NP // 2)
                    nc.scalar.activation(a.t[:, at], a.t[:, at], ACT.Exp, bias=a.bias[:, 0:1], scale=-SCALE / SHRINK).then_inc(a.exped, 1)

            def copy_result(b):
                act.wait_ge(a.msg_turned, k(b) + 1)
                nc.scalar.activation(s.aggT[:, ds(b * P, P)], s.ps[:, 7, 0:P], ACT.Copy).then_inc(a.att_read, 1)

            def copy_groups(b):
                act.wait_ge(a.summed, k(b) + 1)
                for g in range(GROUPS):
                    n = min(4 * g + 4, NB) - 4 * g
                    act.wait_ge(a.turned, k(b) * GROUPS + g + 2)
                    nc.scalar.activation(a.pt[:, 4 * g * P:(4 * g + n) * P], s.ps[:, 4 + g % 2, 0:n * P], ACT.Copy).then_inc(a.pt_read, 1)

            exps(0)
            copy_groups(0)
            exps(1)
            with act.Fori(2, NB) as b:
                copy_result(b - 2)
                copy_groups(b - 1)
                exps(b)
            copy_result(NB - 2)
            copy_groups(NB - 1)
            copy_result(NB - 1)

        @block.vector
        def _(dve):
            def hold_q(b):
                if isinstance(b, int) and b == 0:
                    pass
                else:
                    dve.wait_ge(a.scored, k(b) * SC)
                nc.vector.tensor_copy(a.q[:, :], a.qT[:, ds(b * P, P)]).then_inc(a.q_held, 1)

            def chunk(b, c, mark, weigh):
                here = k(b) & 1
                if mark:
                    if c == 0:
                        dve.wait_ge(a.count_back, k(b) * 16 + 16)
                    dve.wait_ge(a.scored, k(b) * SC + c + 1)
                    nc.vector.scalar_tensor_tensor(out=a.t[:, ds(here * NP + c * HALF, HALF)],
                                                   in0=a.cnt[:, ds(here, 1), c * HALF:(c + 1) * HALF].rearrange("p o n -> p (o n)"),
                                                   scalar=0.5, in1=s.ps[:, c % 4, 0:HALF], op0=ALU.is_lt, op1=ALU.subtract).then_inc(a.masked, 1)
                if weigh:
                    w = b - 1
                    there = k(w) & 1
                    if c == 0:
                        dve.wait_ge(a.turned, k(w) * GROUPS + 1)
                    if c % (SC // 2) == 0:
                        dve.wait_ge(a.exped, k(w) * 2 + c // (SC // 2) + 1)
                    ins = nc.vector.tensor_tensor(a.pm[:, c * HALF:(c + 1) * HALF], a.t[:, ds(there * NP + c * HALF, HALF)],
                                                  a.cnt[:, ds(there, 1), c * HALF:(c + 1) * HALF].rearrange("p o n -> p (o n)"), ALU.mult)
                    ins.then_inc(a.weighed, 1)
                    if c == SC - 1:
                        dve.wait_ge(a.weighed, k(w) * SC + SC)
                        dve.sem_inc(a.count_used, 1)

            def greatest(b):
                dve.wait_ge(a.masked, k(b) * SC + SC + 4)
                dve.sem_inc(a.passed, 1)
                nc.vector.tensor_reduce(out=a.least[:, 0:1], in_=a.t[:, ds((k(b) & 1) * NP, NP)], axis=AX.X, op=ALU.min).then_inc(a.least_ready, 1)
                dve.wait_ge(a.least_ready, k(b) + 1)
                dve.wait_ge(a.exped, k(b) * 2) if not (isinstance(b, int) and b == 0) else None
                nc.vector.tensor_scalar(a.bias[:, 0:1], a.least[:, 0:1], SCALE / SHRINK, None, ALU.mult).then_inc(a.biased, 1)

            def result(b):
                dve.wait_ge(a.summed, k(b) + 2)
                nc.vector.tensor_scalar(a.den[:, 0:1], s.ps[:, 6, P:P + 1], 1e-30, None, ALU.max).then_inc(a.den_ready, 1)
                dve.wait_ge(a.den_ready, k(b) + 1)
                nc.vector.reciprocal(a.den[:, 1:2], a.den[:, 0:1]).then_inc(a.inv_ready, 1)
                dve.wait_ge(a.inv_ready, k(b) + 1)
                dve.wait_ge(a.msg_turned, k(b)) if not (isinstance(b, int) and b == 0) else None
                nc.vector.tensor_scalar(a.msg[:, :], s.ps[:, 6, 0:P], a.den[:, 1:2], None, ALU.mult).then_inc(a.msg_read, 1)

            hold_q(0)
            for c in range(SC):
                chunk(0, c, True, False)
            hold_q(1)
            greatest(0)
            for c in range(SC):
                chunk(1, c, True, True)
            hold_q(2)
            greatest(1)
            with dve.Fori(2, NB - 1) as b:
                for c in range(SC):
                    chunk(b, c, True, True)
                hold_q(b + 1)
                result(b - 2)
                greatest(b)
            for c in range(SC):
                chunk(NB - 1, c, True, True)
            result(NB - 3)
            greatest(NB - 1)
            for c in range(SC):
                chunk(NB, c, False, True)
            result(NB - 2)
            result(NB - 1)


def attention_layers(nc, s, WQ, WK, WV, bV, WO):
    a = Shared()
    a.WQ, a.WK, a.WV, a.bV, a.WO = WQ, WK, WV, bV, WO
    a.weights_loaded, a.columns, a.lin, a.moved, a.held, a.made, a.read, a.count_used, a.count_back = (
        s.sem("att_" + n) for n in "weights_loaded columns lin moved held made read count_used count_back".split())
    a.q_held, a.scored, a.masked, a.least_ready, a.biased, a.exped, a.weighed, a.turned, a.pt_read = (
        s.sem("att_" + n) for n in "q_held scored masked least_ready biased exped weighed turned pt_read".split())
    a.summed, a.den_ready, a.inv_ready, a.msg_read, a.msg_turned, a.att_read, a.passed = (
        s.sem("att_" + n) for n in "summed den_ready inv_ready msg_read msg_turned att_read passed".split())
    with ExitStack() as ctx:
        def sb(name, shape):
            return ctx.enter_context(nc.sbuf_tensor("att_" + name, shape, F32))
        a.w, a.bv, a.col, a.hold, a.q = sb("w", [P, 4, P]), sb("bv", [1, P]), sb("col", [P, 5]), sb("hold", [P, P]), sb("q", [P, P])
        a.qT, a.kT, a.v = sb("qT", [P, NP]), sb("kT", [P, NP]), sb("v", [P, NB, P + 1])
        a.cnt, a.t, a.pm, a.pt = sb("cnt", [P, 2, NP]), sb("t", [P, 2 * NP]), sb("pm", [P, NP]), sb("pt", [P, NP])
        a.least, a.bias, a.den, a.msg = sb("least", [P, 1]), sb("bias", [P, 1]), sb("den", [P, 2]), sb("msg", [P, P])
        with nc.Block() as block:
            @block.vector
            def _(dve):
                nc.vector.memset(a.v[:, :, P:P + 1], 1.0)
                for sem, credit in ((a.moved, 2), (a.read, 1), (a.made, 1), (a.count_used, 2), (a.masked, 4), (a.pt_read, 2),
                                    (a.summed, 1), (a.turned, 1), (a.msg_read, 1), (a.att_read, 1)):
                    dve.sem_inc(sem, credit)
        with nc.Fori(0, LAYERS2) as l:
            project(nc, s, a, l)
            attend(nc, s, a, l)
            node_phase(nc, s, "att", a.w[:, 3, :], s.aggT, ACT.Identity, a.col[:, 2:3], s.hT, gain=a.col[:, 3:4], shift=a.col[:, 4:5], layer=l)
    s.norm.turns += LAYERS2 * NCH
    s.norm.gained += LAYERS2 * NCH


class Residual:

    def __init__(self, s):
        self.given, self.lin, self.sig, self.gated, self.added = (s.sem("res_" + n) for n in ("given", "lin", "sig", "gated", "added"))

    def pe(self, nc, pe, s, r, w0, w1, source):
        pe.wait_ge(self.given, r + 1)
        for stage, (w, x) in enumerate(((w0, source), (w1, s.res_h))):
            if stage:
                pe.wait_ge(self.gated, r * 2 + 1)
            for h in range(2):
                last = nc.tensor.matmul(s.ps[:, 4 + h, 0:HALF], w, x[:, h, :], start=True, stop=True)
            last.then_inc(self.lin, 1)

    def act(self, nc, act, s, r, b0, b1):
        for stage, b in enumerate((b0, b1)):
            act.wait_ge(self.lin, r * 2 + stage + 1)
            nc.scalar.activation(s.res_g[:, :, :], s.ps[:, 4:6, 0:HALF], ACT.Sigmoid, bias=b).then_inc(self.sig, 1)

    def dve(self, nc, dve, s, r, b0, b1, source, out):
        for stage, b in enumerate((b0, b1)):
            dve.wait_ge(self.sig, r * 2 + stage + 1)
            nc.vector.scalar_tensor_tensor(out=s.res_h[:, :, :], in0=s.ps[:, 4:6, 0:HALF], scalar=b, in1=s.res_g[:, :, :],
                                           op0=ALU.add, op1=ALU.mult).then_inc(self.gated, 1)
        dve.wait_ge(self.gated, r * 2 + 2)
        nc.vector.tensor_tensor(out, s.res_h[:, :, :], source, ALU.add).then_inc(self.added, 1)


def embed(nc, s, f):
    with nc.Block() as block:

        @block.sync
        def _(sp):
            for dest, dram in f.loads:
                sp.dma_start(dest, dram).then_inc(f.loaded, 16)

        @block.tensor
        def _(pe):
            pe.wait_ge(f.loaded, 16 * len(f.loads))
            with pe.Fori(0, NCH) as c:
                for e in range(2):
                    s.res.pe(nc, pe, s, c * 2 + e, f.W_emb[:, 2 * e, :], f.W_emb[:, 2 * e + 1, :], halves(s.xT[:, ds(c * CH, CH)]))

        @block.scalar
        def _(act):
            act.wait_ge(f.loaded, 16 * len(f.loads))
            with act.Fori(0, NCH) as c:
                for e in range(2):
                    s.res.act(nc, act, s, c * 2 + e, f.b_emb[:, 2 * e:2 * e + 1], f.b_emb[:, 2 * e + 1:2 * e + 2])

        @block.vector
        def _(dve):
            dve.wait_ge(f.loaded, 16 * len(f.loads))
            with dve.Fori(0, NCH) as c:
                for e, out in enumerate((f.srcT, s.hT)):
                    dve.sem_inc(s.res.given, 1)
                    s.res.dve(nc, dve, s, c * 2 + e, f.b_emb[:, 2 * e:2 * e + 1], f.b_emb[:, 2 * e + 1:2 * e + 2],
                              halves(s.xT[:, ds(c * CH, CH)]), halves(out[:, ds(c * CH, CH)]))
                    dve.wait_ge(s.res.added, c * 2 + e + 1)


def place_edges(nc, s, f):
    done, counted, based, chain = s.sem("place_done"), s.sem("place_counted"), s.sem("place_based"), s.sem("place_chain")
    BUCKETS = NB + 1
    with ExitStack() as ctx:
        def sb(name, shape, dt=F32):
            return ctx.enter_context(nc.sbuf_tensor("place_" + name, shape, dt))
        blk_i, blk, hit, run, slot = sb("blk_i", [P, NT], I32), sb("blk", [P, NT]), sb("hit", [P, NT]), sb("run", [P, NT]), sb("slot", [P, NT])
        count, total, upto, base = sb("count", [P, BUCKETS]), sb("total", [P, BUCKETS]), sb("upto", [P, BUCKETS]), sb("base", [P, BUCKETS])
        row_i, row = sb("row_i", [1, 3, NB], I32), sb("row", [1, NB])
        block = ctx.enter_context(nc.Block())

        @block.tensor
        def _(pe):
            pe.wait_ge(counted, 1)
            nc.tensor.matmul(s.ps[:, 0, 0:BUCKETS], s.ones[:, :], count[:, :], start=True, stop=True).then_inc(based, 1)
            nc.tensor.matmul(s.ps[:, 1, 0:BUCKETS], s.before[:, :], count[:, :], start=True, stop=True).then_inc(based, 1)

        @block.vector
        def _(dve):
            step = [0]

            def link(ins):
                step[0] += 1
                ins.then_inc(done, 1)
                dve.wait_ge(done, step[0])

            link(nc.vector.tensor_copy(blk_i[:, :], s.src[:, 0:NT]))
            link(nc.vector.tensor_scalar(blk_i[:, :], blk_i[:, :], P.bit_length() - 1, None, ALU.arith_shift_right))
            link(nc.vector.tensor_copy(blk[:, :], blk_i[:, :]))
            link(nc.vector.memset(slot[:, :], 0.0))
            with dve.Fori(0, BUCKETS) as b:
                nc.vector.tensor_scalar(hit[:, :], blk[:, :], s.ramp[:, ds(b, 1)], None, ALU.is_equal, ALU.add,
                                        accum_out=count[:, ds(b, 1)]).then_inc(chain, 1)
                dve.wait_ge(chain, b + 1)
            dve.sem_inc(counted, 1)
            dve.wait_ge(based, 2)
            link(nc.vector.tensor_copy(total[:, :], s.ps[:, 0, 0:BUCKETS]))
            link(nc.vector.tensor_tensor_scan(upto[:, :], total[:, :], total[:, :], 0.0, ALU.add, ALU.max))
            link(nc.vector.tensor_tensor(total[:, :], upto[:, :], total[:, :], ALU.subtract))
            link(nc.vector.tensor_tensor(base[:, :], total[:, :], s.ps[:, 1, 0:BUCKETS], ALU.add))
            link(nc.vector.tensor_scalar(base[:, :], base[:, :], -1.0, None, ALU.add))
            with dve.Fori(0, BUCKETS) as b:
                nc.vector.tensor_scalar(hit[:, :], blk[:, :], s.ramp[:, ds(b, 1)], None, ALU.is_equal).then_inc(chain, 1)
                dve.wait_ge(chain, b * 4 + BUCKETS + 1)
                nc.vector.tensor_tensor_scan(run[:, :], hit[:, :], hit[:, :], 0.0, ALU.add, ALU.max).then_inc(chain, 1)
                dve.wait_ge(chain, b * 4 + BUCKETS + 2)
                nc.vector.scalar_tensor_tensor(out=run[:, :], in0=run[:, :], scalar=base[:, ds(b, 1)], in1=hit[:, :],
                                               op0=ALU.add, op1=ALU.mult).then_inc(chain, 1)
                dve.wait_ge(chain, b * 4 + BUCKETS + 3)
                nc.vector.tensor_tensor(slot[:, :], slot[:, :], run[:, :], ALU.add).then_inc(chain, 1)
            dve.wait_ge(chain, BUCKETS * 5)
            link(nc.vector.tensor_copy(f.place[:, :], slot[:, :]))
            SHIFT = P.bit_length() - 1
            link(nc.vector.tensor_copy(row_i[0:1, 0, :], total[0:1, 0:NB]))
            link(nc.vector.tensor_scalar(row[0:1, :], upto[0:1, 0:NB], float(P - 1), None, ALU.add))
            link(nc.vector.tensor_copy(row_i[0:1, 1, :], row[0:1, :]))
            link(nc.vector.tensor_scalar(row_i[0:1, 0:2, :], row_i[0:1, 0:2, :], SHIFT, None, ALU.arith_shift_right))
            link(nc.vector.tensor_copy(s.src_range[0:1, 0, :], row_i[0:1, 0, :]))
            link(nc.vector.tensor_tensor(row_i[0:1, 1, :], row_i[0:1, 1, :], row_i[0:1, 0, :], ALU.subtract))
            link(nc.vector.tensor_scalar(row_i[0:1, 1, :], row_i[0:1, 1, :], float(TG - 1), float(TG), ALU.add, ALU.max))
            link(nc.vector.tensor_scalar(row_i[0:1, 2, :], row_i[0:1, 1, :], TG.bit_length() - 1, None, ALU.arith_shift_right))
            link(nc.vector.tensor_copy(s.src_range[0:1, 1, :], row_i[0:1, 2, :]))
            link(nc.vector.tensor_copy(row[0:1, :], row_i[0:1, 2, :]))
            link(nc.vector.tensor_tensor_scan(upto[0:1, 0:NB], row[0:1, :], row[0:1, :], 0.0, ALU.add, ALU.max))
            link(nc.vector.tensor_tensor(s.src_range[0:1, 2, :], upto[0:1, 0:NB], row[0:1, :], ALU.subtract))


def messages(nc, s, f, d_ef):
    copied, granted = s.sem("msg_index_copied"), s.sem("msg_granted")
    names = "gathered ef_back gathered_free turned turned_read filtered made scattered record_free".split()
    g = {n: [s.sem(f"msg_{n}{h}") for h in range(2)] for n in names}
    padded, cleared = s.sem("msg_padded"), s.sem("msg_cleared")
    turns = NT // (2 * TG)
    full_turns = FULL_TILES // (2 * TG)
    with ExitStack() as ctx:
        def sb(name, shape, dt=F32):
            return [ctx.enter_context(nc.sbuf_tensor(f"msg_{name}{h}", shape, dt)) for h in range(2)]
        from_row, to_row = sb("from_row", [P, TG], I32), sb("to_row", [P, TG], I32)
        node, ef, efT, record = sb("node", [P, TG, P]), sb("ef", [P, TG, EF]), sb("efT", [EF, TG * P]), sb("record", [P, TG, REC])
        block = ctx.enter_context(nc.Block())
        ef_tiles = d_ef[0:FULL_TILES * P, :].rearrange("(t p) k -> p t k", p=P)

        @block.gpsimd
        def _(pool):
            with pool.Fori(0, turns) as i:
                for h in range(2):
                    at = ds(i * (2 * TG) + TG * h, TG)
                    pool.wait_ge(g["gathered_free"][h], i + 1)
                    nc.gpsimd.tensor_copy(from_row[h][:, :], s.dst_row[:, at]).then_inc(copied, 1)
                    pool.wait_ge(copied, i * 4 + 2 * h + 1)
                    pool.sem_inc(granted, 1)
                    for j in range(TG):
                        nc.gpsimd.indirect_dma_start(out=node[h][:, j, :], out_offset=None, in_=s.plain[:, :],
                                                     in_offset=bass.IndirectOffsetOnAxis(ap=from_row[h][:, j:j + 1], axis=0)
                                                     ).then_inc(g["gathered"][h], 16)
                    pool.wait_ge(g["record_free"][h], i + 1)
                    nc.gpsimd.tensor_copy(to_row[h][:, :], f.place[:, at]).then_inc(copied, 1)
                    pool.wait_ge(copied, i * 4 + 2 * h + 2)
                    pool.wait_ge(g["made"][h], i + 1)
                    pool.sem_inc(granted, 1)
                    for j in range(TG):
                        nc.gpsimd.indirect_dma_start(out=s.records[:, :],
                                                     out_offset=bass.IndirectOffsetOnAxis(ap=to_row[h][:, j:j + 1], axis=0),
                                                     in_=record[h][:, j, :], in_offset=None).then_inc(g["scattered"][h], 16)
            for h in range(2):
                pool.wait_ge(g["scattered"][h], turns * TG * 16)

        @block.sync
        def _(sp):
            def load(i, h):
                sp.wait_ge(g["turned"][h], i + 1)
                sp.dma_start(ef[h][:, :, :], ef_tiles[:, ds(i * (2 * TG) + TG * h, TG), :]).then_inc(g["ef_back"][h], 16)

            def free(i, h):
                sp.wait_ge(g["scattered"][h], i * (16 * TG) + 16 * TG)
                sp.sem_inc(g["record_free"][h], 1)

            for h in range(2):
                sp.sem_inc(g["record_free"][h], 1)
            with sp.Fori(0, full_turns) as i:
                for h in range(2):
                    load(i, h)
                    free(i, h)
            for i in range(full_turns, turns):
                for h in range(2):
                    first = i * 2 * TG + TG * h
                    whole = min(max(FULL_TILES - first, 0), TG)
                    if first < TILES:
                        sp.wait_ge(g["turned"][h], i + 1)
                        sp.wait_ge(padded, 2 * (i - full_turns) + h + 1)
                        if whole:
                            sp.dma_start(ef[h][:, 0:whole, :], ef_tiles[:, first:first + whole, :]).then_inc(g["ef_back"][h], 16)
                        if whole < TG:
                            sp.dma_start(ef[h][0:LAST, whole, :], d_ef[FULL_TILES * P:EDGES, :]).then_inc(g["ef_back"][h], 16)
                    free(i, h)

        def ef_arrived(i, h):
            if not isinstance(i, int) or i < full_turns:
                return i * 16 + 16
            n = full_turns
            for j in range(full_turns, i + 1):
                first = j * 2 * TG + TG * h
                whole = min(max(FULL_TILES - first, 0), TG)
                n += (whole > 0) + (first < TILES and whole < TG)
            return 16 * n

        @block.tensor
        def _(pe):
            for h in range(2):
                pe.sem_inc(g["turned"][h], 1)

            def turn(i, h):
                pe.wait_ge(g["ef_back"][h], ef_arrived(i, h))
                if isinstance(i, int):
                    pe.wait_ge(padded, 2 * (i - full_turns) + h + 1)
                pe.wait_ge(g["turned_read"][h], i + 1)
                for j in range(TG):
                    last = nc.tensor.transpose(s.ps[0:EF, h, j * P:(j + 1) * P], ef[h][:, j, :], s.ident[:, :])
                last.then_inc(g["turned"][h], 1)
                pe.wait_ge(g["turned_read"][h], i + 2)
                pe.wait_ge(g["gathered_free"][h], i + 1)
                for j in range(TG):
                    last = nc.tensor.matmul(s.ps[:, 2 + h, j * P:(j + 1) * P], efT[h][:, j * P:(j + 1) * P], f.We[:, :], start=True, stop=True)
                last.then_inc(g["filtered"][h], 1)

            with pe.Fori(0, full_turns) as i:
                for h in range(2):
                    turn(i, h)
            for i in range(full_turns, turns):
                for h in range(2):
                    turn(i, h)

        @block.scalar
        def _(act):
            for h in range(2):
                act.sem_inc(g["turned_read"][h], 1)
            with act.Fori(0, turns) as i:
                for h in range(2):
                    act.wait_ge(g["turned"][h], i + 2)
                    act.wait_ge(g["gathered_free"][h], i + 1)
                    nc.scalar.activation(efT[h][:, :], s.ps[0:EF, h, :], ACT.Copy).then_inc(g["turned_read"][h], 1)

        @block.vector
        def _(dve):
            for h in range(2):
                nc.vector.memset(record[h][:, :, :], 0.0).then_inc(cleared, 1)
                dve.sem_inc(g["gathered_free"][h], 1)
            dve.wait_ge(cleared, 2)

            def make(i, h):
                dve.wait_ge(g["record_free"][h], i + 1)
                dve.wait_ge(g["filtered"][h], i + 1)
                dve.wait_ge(g["gathered"][h], i * (16 * TG) + 16 * TG)
                for j in range(TG):
                    tile = i * (2 * TG) + TG * h + j
                    last = nc.vector.scalar_tensor_tensor(out=record[h][:, j, 0:P], in0=s.ps[:, 2 + h, j * P:(j + 1) * P],
                                                          scalar=s.weight1[:, ds(tile, 1)], in1=node[h][:, j, :], op0=ALU.mult, op1=ALU.mult)
                last.then_inc(g["gathered_free"][h], 1)
                nc.vector.tensor_copy(record[h][:, :, P:P + 1].rearrange("p t o -> p (t o)"),
                                      s.src[:, ds(i * (2 * TG) + TG * h, TG)]).then_inc(g["made"][h], 1)

            with dve.Fori(0, full_turns) as i:
                for h in range(2):
                    make(i, h)
            for i in range(full_turns, turns):
                for h in range(2):
                    dve.wait_ge(g["turned"][h], i + 1)
                    nc.vector.memset(ef[h][:, :, :], 0.0).then_inc(padded, 1)
                    make(i, h)


def convolve(nc, s, f):
    scaled, mixed = s.sem("conv_scaled"), s.sem("conv_mixed")
    R0 = 2 * NCH
    weights = [(f.W_conv, f.b_conv, 0), (f.W_conv, f.b_conv, 1), (f.W_out, f.b_out, 0), (f.W_out, f.b_out, 1)]
    n = s.norm
    with nc.Block() as block:

        @block.tensor
        def _(pe):
            with pe.Fori(0, NCH) as c:
                for e, (w, _, r) in enumerate(weights):
                    s.res.pe(nc, pe, s, c * 4 + (R0 + e), w[:, 2 * r, :], w[:, 2 * r + 1, :], s.y)
                n.pe(nc, pe, s, n.turns + c)

        @block.scalar
        def _(act):
            with act.Fori(0, NCH) as c:
                for e, (_, b, r) in enumerate(weights):
                    s.res.act(nc, act, s, c * 4 + (R0 + e), b[:, 2 * r:2 * r + 1], b[:, 2 * r + 1:2 * r + 2])
                n.act(nc, act, s, n.turns + c)

        @block.vector
        def _(dve):
            with dve.Fori(0, NCH) as c:
                at = ds(c * CH, CH)
                dve.wait_ge(n.normed, n.turns + c + 1)
                nc.vector.tensor_scalar(s.y[:, :, :], halves(s.aggT[:, at]), f.C[:, 0:1], None, ALU.mult).then_inc(scaled, 1)
                dve.wait_ge(scaled, c + 1)
                dve.sem_inc(s.res.given, 1)
                for e, (_, b, r) in enumerate(weights):
                    s.res.dve(nc, dve, s, c * 4 + (R0 + e), b[:, 2 * r:2 * r + 1], b[:, 2 * r + 1:2 * r + 2], s.y[:, :, :], s.y[:, :, :])
                    dve.wait_ge(s.res.added, c * 4 + (R0 + e + 1))
                    if e == 1:
                        nc.vector.tensor_tensor(s.y[:, :, :], s.y[:, :, :], halves(f.srcT[:, at]), ALU.mult).then_inc(mixed, 1)
                        dve.wait_ge(mixed, c + 1)
                    if e < 3:
                        dve.sem_inc(s.res.given, 1)
                nc.vector.tensor_tensor(s.y[:, :, :], s.y[:, :, :], halves(s.xT[:, at]), ALU.add).then_inc(n.given, 1)
                n.dve(nc, dve, s, n.turns + c, halves(s.xT[:, at]))


def gnn_kernel(nc, d_x, d_src, d_dst, d_ef, d_type, d_weight, d_weight1, W0, b0, proj_w, proj_b, edge_W, edge_b,
               wih, whh, bih, bhh, out_w, out_b, Wn, bn, WQ, bQ, WK, bK, WV, bV, WO, bO, ln_g, ln_b, Wout, bout,
               C, W_emb, b_emb, We, W_conv, b_conv, W_out, b_out, out):
    with ExitStack() as ctx:
        def sb(name, shape, dt=F32):
            return ctx.enter_context(nc.sbuf_tensor(name, shape, dt))

        s = Shared()
        s.sem = lambda name: ctx.enter_context(nc.semaphore(name))

        def phase(step, *args, **kwargs):
            kept, own = s.sem, []

            def take(name):
                own.append(nc.alloc_semaphore(name))
                return own[-1]
            s.sem = take
            step(nc, s, *args, **kwargs)
            s.sem = kept
            nc.clear_and_free_semaphores(own)
            nc.all_engine_barrier()
        s.ps = ctx.enter_context(nc.psum_tensor("ps", [P, 8, 512], F32))
        s.groups_of = groups_of
        s.d_x, s.d_src, s.d_dst, s.d_type, s.d_weight = d_x, d_src, d_dst, d_type, d_weight
        s.d_weight1 = d_weight1.rearrange("e o -> (e o)")
        s.d_proj_w, s.d_out_w, s.d_edge_W, s.d_wih, s.d_whh = proj_w, out_w, edge_W, wih, whh
        s.d_W0, s.d_Wn, s.d_Wout = W0, Wn, Wout

        s.edge_rows = nc.dram_tensor("edge_rows", (NT * P, P), F32, kind="Internal").ap()
        s.counts = nc.dram_tensor("counts", (NB, P, NP), F32, kind="Internal").ap()
        s.typed = nc.dram_tensor("typed", (TYPES * NP, P), F32, kind="Internal").ap()
        s.plain = nc.dram_tensor("plain", (NP, P), F32, kind="Internal").ap()
        s.records = nc.dram_tensor("records", (NT * P, REC), F32, kind="Internal").ap()

        s.ident, s.before, s.mean_w, s.ones = (sb(n, [P, P]) for n in ("ident", "before", "mean_w", "ones"))
        s.zeros_bf = sb("zeros_bf", [P, 512], BF16)
        s.eps = sb("eps", [P, 1])
        s.ramp = sb("ramp", [P, NP])
        s.tile_i, s.tile_no = sb("tile_i", [P, TC], I32), sb("tile_no", [P, TC])
        s.start_i, s.start = sb("start_i", [P, NB + 1], I32), sb("start", [P, NB + 1])
        s.src, s.weight1, s.dst_row = sb("src", [P, TC * P]), sb("weight1", [P, TC * P]), sb("dst_row", [P, NT], I32)
        s.dst_range = sb("dst_range", [1, 3, NB], I32)
        s.src_range = sb("src_range", [1, 3, NB], I32)
        s.xT, s.hT, s.aggT = (sb(n, [P, NP]) for n in ("xT", "hT", "aggT"))
        s.W0, s.Wn, s.Wout = (sb(n, [P, P]) for n in ("W0", "Wn", "Wout"))
        s.y, s.yc, s.sq, s.std = (sb(n, [P, 2, HALF]) for n in ("norm_y", "norm_yc", "norm_sq", "norm_sd"))
        s.bih, s.bhh, s.b_rz = sb("bih", [P, LAYERS1, 3]), sb("bhh", [P, LAYERS1, 3]), sb("b_rz", [P, LAYERS1, 2])
        s.bias_loads = []

        def column(name, dram, cols):
            c = sb("col_" + name, [P, cols])
            s.bias_loads.append((c[:, :], dram))
            return c
        one = "(f o) -> f o"
        s.b0, s.b_proj, s.b_out1 = (column(n, a.rearrange(one, o=1), 1) for n, a in (("b0", b0), ("proj", proj_b), ("out1", out_b)))
        s.bn, s.b_out2 = (column(n, a.rearrange(one, o=1), 1) for n, a in (("bn", bn), ("out2", bout)))
        s.bQ, s.bK, s.bO, s.ln_g, s.ln_b = (column(n, a.rearrange("l f -> f l"), LAYERS2)
                                            for n, a in (("bQ", bQ), ("bK", bK), ("bO", bO), ("g", ln_g), ("b", ln_b)))
        for l in range(LAYERS1):
            s.bias_loads += [(s.bih[:, l, :], bih[l].rearrange("(g f) -> f g", f=P)), (s.bhh[:, l, :], bhh[l].rearrange("(g f) -> f g", f=P))]
        s.norm = Norm(s)

        early = ExitStack()

        def sb_early(name, shape, dt=F32):
            return early.enter_context(nc.sbuf_tensor(name, shape, dt))
        s.ramp16 = sb_early("ramp16", [P, NP], I16)
        s.dst, s.typ, s.weight = (sb_early(n, [P, TC * P]) for n in ("dst", "typ", "weight"))
        s.src_row, s.typed_row = (sb_early(n, [P, NT], I32) for n in ("src_row", "typed_row"))
        s.wT = sb_early("wT", [P, 2 + LAYERS1 * (TYPES + 6), P])

        with nc.allow_non_contiguous_dma(reason="bias columns"):
            phase(constants)
            phase(load_edges)
            phase(load_nodes)

        def write_table(table, types):
            view = table.rearrange("(t n) f -> n t f", t=types)

            def write(sp, b, row, stored):
                sp.dma_start(view[ds(b * P, P), :, :], row.rearrange("p (t f) -> p t f", t=types)).then_inc(stored, 16)
            return write

        def write_out(sp, b, row, stored):
            if isinstance(b, int):
                sp.dma_start(out[b * P:NODES, :], row[0:NODES - b * P, :]).then_inc(stored, 16)
            else:
                sp.dma_start(out[ds(b * P, P), :], row).then_inc(stored, 16)

        def run():
            phase(edge_pass, "sum0", s.d_x[:, :], s.src_row, s.dst_range, weighted=True, build_counts=True)
            node_phase(nc, s, "0", s.W0[:, :], s.aggT, ACT.Relu, s.b0[:, 0:1], s.xT,
                       second=(s.wT[:, 0, :], ACT.Relu, s.b_proj[:, 0:1], s.hT))
            s.norm.turns += NCH
            for l in range(LAYERS1):
                o = 2 + l * (TYPES + 6)
                phase(node_rows, f"typed{l}", s.hT, s.wT[:, o:o + TYPES, :].rearrange("p t f -> p (t f)"), TYPES * P, write_table(s.typed, TYPES))
                phase(edge_pass, f"sum1{l}", s.typed[:, :], s.typed_row, s.dst_range)
                phase(gru, l)
            node_phase(nc, s, "1", s.wT[:, 1, :], s.hT, ACT.Identity, s.b_out1[:, 0:1], s.xT,
                       second=(s.Wn[:, :], ACT.Identity, s.bn[:, 0:1], s.hT))
            s.norm.turns += NCH
            early.close()
            attention_layers(nc, s, WQ, WK, WV, bV, WO)
            node_phase(nc, s, "2", s.Wout[:, :], s.hT, ACT.Identity, s.b_out2[:, 0:1], s.xT)
            s.norm.turns += NCH
            late = ExitStack()
            f = Shared()
            f.loaded, f.loads = s.sem("late_loaded"), []

            def sb_late(name, shape, dram=None, dt=F32):
                t = late.enter_context(nc.sbuf_tensor("late_" + name, shape, dt))
                if dram is not None:
                    f.loads.append((t[:], dram))
                return t
            two = "a b i o -> i (a b) o"
            f.W_emb, f.W_conv, f.W_out = (sb_late(n, [P, 4, P], a.rearrange(two)) for n, a in (("W_emb", W_emb), ("W_conv", W_conv), ("W_out", W_out)))
            f.b_emb, f.b_conv, f.b_out = (sb_late(n, [P, 4], a.rearrange("a b f -> f (a b)")) for n, a in (("b_emb", b_emb), ("b_conv", b_conv), ("b_out", b_out)))
            f.We = sb_late("We", [EF, P], We)
            f.C = sb_late("C", [P, 1], C.rearrange("(o c) -> o c", o=1).broadcast_to([P, 1]))
            f.srcT = sb_late("srcT", [P, NP])
            f.place = sb_late("place", [P, NT], dt=I32)
            s.res_h, s.res_g = sb_late("res_h", [P, 2, HALF]), sb_late("res_g", [P, 2, HALF])
            s.res = Residual(s)
            with nc.allow_non_contiguous_dma(reason="bias columns"):
                embed(nc, s, f)
            phase(node_rows, "plain", s.hT, s.ident[:, :], P, write_table(s.plain, 1))
            phase(place_edges, f)
            phase(messages, f, d_ef)
            phase(edge_pass, "sum3", None, None, s.src_range)
            phase(convolve, f)
            late.close()
            return s.xT
        final = run()
        phase(node_rows, "out", final, s.ident[:, :], P, write_out)




_INS = ['x', 'src', 'dst', 'edge_attr_32', 'edge_type_8', 'edge_weight', 'edge_weight1', 'L0_gnn_W', 'L0_gnn_b',
        'L1_gnn_node_proj_w', 'L1_gnn_node_proj_b', 'L1_gnn_edge_W', 'L1_gnn_edge_b', 'L1_gnn_gru_wih',
        'L1_gnn_gru_whh', 'L1_gnn_gru_bih', 'L1_gnn_gru_bhh', 'L1_gnn_out_w', 'L1_gnn_out_b', 'L2_gnn_Wn',
        'L2_gnn_bn', 'L2_gnn_WQ', 'L2_gnn_bQ', 'L2_gnn_WK', 'L2_gnn_bK', 'L2_gnn_WV', 'L2_gnn_bV', 'L2_gnn_WO',
        'L2_gnn_bO', 'L2_gnn_ln_g', 'L2_gnn_ln_b', 'L2_gnn_Wout', 'L2_gnn_bout', 'L3_gnn_C', 'L3_gnn_W_emb',
        'L3_gnn_b_emb', 'L3_gnn_We', 'L3_gnn_W_conv', 'L3_gnn_b_conv', 'L3_gnn_W_out', 'L3_gnn_b_out']
_OUTS = [((3125, 128), 'float32')]


def kernel(**inputs):
    import numpy as _np
    import concourse.bacc as _bacc
    from concourse import mybir as _mybir
    from concourse.bass_utils import run_bass_kernel_spmd as _run

    nc = _bacc.Bacc("TRN2", target_bir_lowering=False, num_devices=1)
    arrays, args = {}, []
    for name in _INS:
        a = _np.ascontiguousarray(inputs[name])
        arrays[f"in_{name}_dram"] = a
        args.append(nc.dram_tensor(f"in_{name}_dram", a.shape, _mybir.dt.from_np(a.dtype), kind="ExternalInput").ap())
    for i, (shape, dtype) in enumerate(_OUTS):
        dt = _mybir.dt.from_np(_np.dtype(dtype))
        args.append(nc.dram_tensor(f"out_{i}_dram", shape, dt, kind="ExternalOutput").ap())
    gnn_kernel(nc, *args)
    r = _run(nc, [arrays], core_ids=[0])
    got = tuple(r.results[0][f"out_{i}_dram"] for i in range(len(_OUTS)))
    return got[0]
```

```python
import concourse.bass as bass
from concourse import mybir
from contextlib import ExitStack

F32 = mybir.dt.float32
BF16 = mybir.dt.bfloat16
I32 = mybir.dt.int32
I16 = mybir.dt.int16
ALU = mybir.AluOpType
ACT = mybir.ActivationFunctionType
AX = mybir.AxisListType
ds = bass.ds

P = 128
NODES = 3125
EDGES = 100000
NB = -(-NODES // P)
NP = NB * P
FULL_TILES = EDGES // P
LAST = EDGES - FULL_TILES * P
TILES = -(-EDGES // P)
TG = 8
PARTS = 4
PT = TG // PARTS
GT = 4
RT = 10
NT = -(-(TILES + TG) // (2 * TG)) * 2 * TG
TC = -(-NT // P)
PAD_NODE = NP + 5
TYPES = 8
LAYERS1 = 2
LAYERS2 = 4
EF = 32
HALF = 400
CH = 2 * HALF
NCH = NP // CH
EPS = 1e-5
BIG = 4096.0
SHRINK = 2.0 ** -64
SCALE = float(P) ** -0.5
REC = EF + 4
PLACE_TURNS = FULL_TILES // (LAYERS2 * RT)


class Shared:
    pass


def halves(ap):
    return ap.rearrange("p (h n) -> p h n", h=2)


def bounded(value, top):
    return value.with_bounds(min_val=0, max_val=top, guaranteed_mod_val=0, out_of_modulus=1)


def constants(nc, s):
    filled, made = s.sem("const_filled"), s.sem("const_made")
    with nc.sbuf_tensor("ramp_i", [P, NP], I32) as ramp_i, nc.Block() as block:

        @block.vector
        def _(dve):
            dve.sem_inc(s.norm.normed, 1)

        @block.gpsimd
        def _(pool):
            pool.memset(s.ident[:, :], 0.0).then_inc(filled, 1)
            pool.memset(s.before[:, :], 0.0).then_inc(filled, 1)
            pool.memset(s.mean_w[:, :], 1.0 / P).then_inc(filled, 1)
            pool.memset(s.ones[:, :], 1.0).then_inc(filled, 1)
            pool.memset(s.zeros_bf[:, :], 0.0).then_inc(filled, 1)
            pool.memset(s.eps[:, :], EPS).then_inc(filled, 1)
            pool.iota(ramp_i[:, :], pattern=[[1, NP]], base=0, channel_multiplier=0).then_inc(filled, 1)
            pool.iota(s.tile_i[:, :], pattern=[[P, TC]], base=0, channel_multiplier=1).then_inc(filled, 1)
            pool.iota(s.start_i[:, :], pattern=[[P, NB + 1]], base=0, channel_multiplier=0).then_inc(filled, 1)
            pool.wait_ge(filled, 9)
            pool.affine_select(out=s.ident[:, :], in_=s.ident[:, :], compare_op=ALU.not_equal, fill=1.0,
                               base=0, pattern=[[-1, P]], channel_multiplier=1).then_inc(made, 1)
            pool.affine_select(out=s.before[:, :], in_=s.before[:, :], compare_op=ALU.is_ge, fill=1.0,
                               base=0, pattern=[[-1, P]], channel_multiplier=1).then_inc(made, 1)
            pool.tensor_copy(s.ramp[:, :], ramp_i[:, :]).then_inc(made, 1)
            pool.tensor_copy(s.ramp16[:, :], ramp_i[:, :]).then_inc(made, 1)
            pool.tensor_copy(s.tile_no[:, :], s.tile_i[:, :]).then_inc(made, 1)
            pool.tensor_copy(s.start[:, :], s.start_i[:, :]).then_inc(made, 1)
            pool.wait_ge(made, 6)


def load_edges(nc, s):
    padded, loaded, cast = s.sem("edge_padded"), s.sem("edge_loaded"), s.sem("edge_cast")
    turned, copied, ranged = s.sem("edge_turned"), s.sem("edge_copied"), s.sem("edge_ranged")
    range_pe, indexed = s.sem("edge_range_pe"), s.sem("edge_indexed")
    with ExitStack() as ctx:
        nat_i = ctx.enter_context(nc.sbuf_tensor("nat_i", [P, 3, TC, P], I32))
        nat = ctx.enter_context(nc.sbuf_tensor("nat", [P, 5, TC, P], F32))
        span = ctx.enter_context(nc.sbuf_tensor("span", [P, 2, TC], F32))
        tile_m = ctx.enter_context(nc.sbuf_tensor("tile_m", [P, 2, TC], F32))
        hit = ctx.enter_context(nc.sbuf_tensor("hit", [P, 3, TC, NB], F32))
        edge_t = ctx.enter_context(nc.sbuf_tensor("edge_t", [NB, 8], F32))
        edge_i = ctx.enter_context(nc.sbuf_tensor("edge_i", [NB, 2], I32))
        tmp = ctx.enter_context(nc.sbuf_tensor("index_tmp", [P, NT], F32))
        block = ctx.enter_context(nc.Block())
        sources = [(nat_i[:, 0], s.d_src), (nat_i[:, 1], s.d_dst), (nat_i[:, 2], s.d_type),
                   (nat[:, 3], s.d_weight), (nat[:, 4], s.d_weight1)]
        whole = FULL_TILES // P
        rest = FULL_TILES - whole * P

        @block.gpsimd
        def _(pool):
            for (dest, _), pad in zip(sources, [PAD_NODE, PAD_NODE, 0, 0.0, 0.0]):
                pool.memset(dest[:, whole, :], pad).then_inc(padded, 1)

        @block.sync
        def _(sp):
            sp.wait_ge(padded, 5)
            for dest, dram in sources:
                sp.dma_start(dest[:, 0:whole, :],
                             dram[0:whole * P * P].rearrange("(c p j) -> p c j", c=whole, p=P)).then_inc(loaded, 16)
                sp.dma_start(dest[0:rest, whole, :],
                             dram[whole * P * P:FULL_TILES * P].rearrange("(p j) -> p j", j=P)).then_inc(loaded, 16)
                sp.dma_start(dest[rest:rest + 1, whole, 0:LAST],
                             dram[FULL_TILES * P:EDGES].rearrange("(p j) -> p j", p=1)).then_inc(loaded, 16)

        banks = [s.ps[:, n, :] for n in range(8)]

        @block.tensor
        def _(pe):
            pe.wait_ge(cast, 3)
            for n in range(5):
                if n >= 3:
                    pe.wait_ge(copied, 2 * (n - 2))
                for c in range(TC):
                    nc.tensor.transpose(banks[2 * (n % 3) + c // 4][:, (c % 4) * P:(c % 4 + 1) * P],
                                        nat[:, n, c, :], s.ident[:, :]).then_inc(turned, 1)
            pe.wait_ge(ranged, 2 + 4 * TC + 2)
            pe.wait_ge(copied, 10)
            for v in range(2):
                for c in range(TC):
                    nc.tensor.transpose(banks[2 * v + c // 4][0:NB, (c % 4) * P:(c % 4 + 1) * P],
                                        hit[:, 1 + v, c, :], s.ident[:, :]).then_inc(range_pe, 1)
            pe.wait_ge(indexed, 7)
            nc.tensor.matmul(banks[4][0:1, 0:NB], edge_t[:, 4:5], s.ident[0:NB, 0:NB], start=True, stop=True).then_inc(range_pe, 1)
            nc.tensor.matmul(banks[5][0:1, 0:NB], edge_t[:, 5:6], s.ident[0:NB, 0:NB], start=True, stop=True).then_inc(range_pe, 1)
            nc.tensor.matmul(banks[6][0:1, 0:NB], edge_t[:, 5:6], s.before[0:NB, 0:NB], start=True, stop=True).then_inc(range_pe, 1)

        @block.vector
        def _(dve):
            dve.wait_ge(loaded, 16 * 15)
            for n in range(3):
                nc.vector.tensor_copy(nat[:, n], nat_i[:, n]).then_inc(cast, 1)
            dve.wait_ge(cast, 3)
            nc.vector.tensor_reduce(out=span[:, 0, :], in_=nat[:, 1], axis=AX.X, op=ALU.min).then_inc(ranged, 1)
            nc.vector.tensor_reduce(out=span[:, 1, :], in_=nat[:, 1], axis=AX.X, op=ALU.max).then_inc(ranged, 1)
            nc.vector.tensor_scalar(tile_m[:, 0, :], s.tile_no[:, :], -BIG, None, ALU.add).then_inc(ranged, 1)
            nc.vector.tensor_scalar(tile_m[:, 1, :], s.tile_no[:, :], 1.0, None, ALU.add).then_inc(ranged, 1)
            dve.wait_ge(ranged, 4)
            for c in range(TC):
                nc.vector.tensor_scalar(hit[:, 0, c, :], s.start[:, 0:NB], span[:, 1, c:c + 1], None, ALU.is_le).then_inc(ranged, 1)
                dve.wait_ge(ranged, 4 + 4 * c + 1)
                nc.vector.scalar_tensor_tensor(out=hit[:, 0, c, :], in0=s.start[:, 1:NB + 1], scalar=span[:, 0, c:c + 1],
                                               in1=hit[:, 0, c, :], op0=ALU.is_gt, op1=ALU.mult).then_inc(ranged, 1)
                dve.wait_ge(ranged, 4 + 4 * c + 2)
                nc.vector.tensor_scalar(hit[:, 1, c, :], hit[:, 0, c, :], tile_m[:, 0, c:c + 1], BIG, ALU.mult, ALU.add).then_inc(ranged, 1)
                nc.vector.tensor_scalar(hit[:, 2, c, :], hit[:, 0, c, :], tile_m[:, 1, c:c + 1], None, ALU.mult).then_inc(ranged, 1)
            for n, column in enumerate([s.src, s.dst, s.typ, s.weight, s.weight1]):
                for h, (lo, hi) in enumerate([(0, 4), (4, TC)]):
                    dve.wait_ge(turned, TC * n + hi)
                    nc.vector.tensor_copy(column[:, lo * P:hi * P], banks[2 * (n % 3) + h][:, 0:(hi - lo) * P]).then_inc(copied, 1)
            dve.wait_ge(range_pe, 2 * TC)
            for v, op in enumerate([ALU.min, ALU.max]):
                nc.vector.tensor_reduce(out=edge_t[:, 2 * v:2 * v + 1], in_=banks[2 * v][0:NB, 0:4 * P], axis=AX.X, op=op).then_inc(indexed, 1)
                nc.vector.tensor_reduce(out=edge_t[:, 2 * v + 1:2 * v + 2], in_=banks[2 * v + 1][0:NB, 0:(TC - 4) * P], axis=AX.X, op=op).then_inc(indexed, 1)
            dve.wait_ge(indexed, 4)
            nc.vector.tensor_tensor(edge_t[:, 4:5], edge_t[:, 0:1], edge_t[:, 1:2], ALU.min).then_inc(indexed, 1)
            nc.vector.tensor_tensor(edge_t[:, 6:7], edge_t[:, 2:3], edge_t[:, 3:4], ALU.max).then_inc(indexed, 1)
            dve.wait_ge(indexed, 6)
            s.groups_of(nc, dve, edge_t, edge_i, 4, 6, 5, s.sem("edge_groups"), indexed)
            dve.wait_ge(range_pe, 2 * TC + 3)
            for r in range(3):
                nc.vector.tensor_copy(s.dst_range[0:1, r, :], banks[4 + r][0:1, 0:NB]).then_inc(ranged, 1)
            dve.wait_ge(copied, 10)
            nc.vector.tensor_scalar(s.src_row[:, :], s.src[:, 0:NT], float(NODES - 1), None, ALU.min).then_inc(ranged, 1)
            nc.vector.tensor_scalar(s.dst_row[:, :], s.dst[:, 0:NT], float(NODES - 1), None, ALU.min).then_inc(ranged, 1)
            nc.vector.tensor_scalar(tmp[:, :], s.src[:, 0:NT], float(NODES - 1), None, ALU.min).then_inc(indexed, 1)
            dve.wait_ge(indexed, 8)
            nc.vector.scalar_tensor_tensor(out=s.typed_row[:, :], in0=s.typ[:, 0:NT], scalar=float(NP), in1=tmp[:, :],
                                           op0=ALU.mult, op1=ALU.add).then_inc(ranged, 1)


def groups_of(nc, dve, t, ti, lo, hi, out, chain, done):
    nc.vector.tensor_scalar(t[:, lo:lo + 1], t[:, lo:lo + 1], float(NT - TG), None, ALU.min).then_inc(chain, 1)
    dve.wait_ge(chain, 1)
    nc.vector.tensor_tensor(t[:, hi:hi + 1], t[:, hi:hi + 1], t[:, lo:lo + 1], ALU.subtract).then_inc(chain, 1)
    dve.wait_ge(chain, 2)
    nc.vector.tensor_scalar(ti[:, 0:1], t[:, hi:hi + 1], float(TG - 1), float(TG), ALU.add, ALU.max).then_inc(chain, 1)
    dve.wait_ge(chain, 3)
    nc.vector.tensor_scalar(ti[:, 1:2], ti[:, 0:1], TG.bit_length() - 1, None, ALU.arith_shift_right).then_inc(chain, 1)
    dve.wait_ge(chain, 4)
    nc.vector.tensor_copy(t[:, out:out + 1], ti[:, 1:2]).then_inc(done, 1)


def load_nodes(nc, s):
    loaded, turned, copied, padded = s.sem("node_loaded"), s.sem("node_turned"), s.sem("node_copied"), s.sem("node_padded")
    with ExitStack() as ctx:
        xn = ctx.enter_context(nc.sbuf_tensor("x_nodes", [P, NB, P], F32))
        nw = 2 + LAYERS1 * (TYPES + 6)
        wn = ctx.enter_context(nc.sbuf_tensor("w_rows", [P, nw, P], F32))
        block = ctx.enter_context(nc.Block())

        @block.gpsimd
        def _(pool):
            pool.memset(xn[:, NB - 1, :], 0.0).then_inc(padded, 1)

        @block.scalar
        def _(act):
            act.dma_start(wn[:, 0, :], s.d_proj_w).then_inc(loaded, 16)
            act.dma_start(wn[:, 1, :], s.d_out_w).then_inc(loaded, 16)
            for l in range(LAYERS1):
                o = 2 + l * (TYPES + 6)
                act.dma_start(wn[:, o:o + TYPES, :], s.d_edge_W[l].rearrange("t d h -> d t h")).then_inc(loaded, 16)
                act.dma_start(wn[:, o + TYPES:o + TYPES + 3, :], s.d_wih[l].rearrange("(g d) h -> d g h", d=P)).then_inc(loaded, 16)
                act.dma_start(wn[:, o + TYPES + 3:o + TYPES + 6, :], s.d_whh[l].rearrange("(g d) h -> d g h", d=P)).then_inc(loaded, 16)
            for column, dram in s.bias_loads:
                act.dma_start(column, dram).then_inc(loaded, 16)
            act.dma_start(s.W0[:, :], s.d_W0).then_inc(loaded, 16)
            act.dma_start(s.Wn[:, :], s.d_Wn).then_inc(loaded, 16)
            act.dma_start(s.Wout[:, :], s.d_Wout).then_inc(loaded, 16)

        @block.sync
        def _(sp):
            sp.wait_ge(padded, 1)
            sp.dma_start(xn[:, 0:NB - 1, :], s.d_x[0:(NB - 1) * P, :].rearrange("(b p) f -> p b f", p=P)).then_inc(loaded, 16)
            sp.dma_start(xn[0:NODES - (NB - 1) * P, NB - 1, :], s.d_x[(NB - 1) * P:NODES, :]).then_inc(loaded, 16)

        count = 16 * (2 + 2 + 3 * LAYERS1 + len(s.bias_loads) + 3)
        todo = [(xn[:, b, :], s.xT[:, b * P:(b + 1) * P]) for b in range(NB)]
        todo += [(wn[:, n, :], s.wT[:, n, :]) for n in range(nw)]

        @block.tensor
        def _(pe):
            pe.wait_ge(loaded, count)
            for k, (source, _) in enumerate(todo):
                if k >= 8:
                    pe.wait_ge(copied, k - 7)
                nc.tensor.transpose(s.ps[:, k % 8, 0:P], source, s.ident[:, :]).then_inc(turned, 1)

        @block.vector
        def _(dve):
            for k, (_, dest) in enumerate(todo):
                dve.wait_ge(turned, k + 1)
                nc.vector.tensor_copy(dest, s.ps[:, k % 8, 0:P]).then_inc(copied, 1)
            dve.wait_ge(loaded, count)
            nc.vector.tensor_tensor(s.b_rz[:, :, :], s.bih[:, :, 0:2], s.bhh[:, :, 0:2], ALU.add).then_inc(padded, 1)


def edge_pass(nc, s, name, table, rows, ranges, weighted=False, columns=None, We=None):
    records = We is not None
    copied, granted = s.sem(name + "_index_copied"), s.sem(name + "_granted")
    gathered = [s.sem(f"{name}_gathered{h}") for h in range(2)]
    row_free = [s.sem(f"{name}_row_free{h}") for h in range(2)]
    stored = [s.sem(f"{name}_stored{h}") for h in range(2)]
    record_back = [s.sem(f"{name}_record_back{h}") for h in range(2)]
    back = [s.sem(f"{name}_back{h}") for h in range(PARTS)]
    picked = [s.sem(f"{name}_picked{h}") for h in range(PARTS)]
    used = [s.sem(f"{name}_used{h}") for h in range(PARTS)]
    turned = [s.sem(f"{name}_turned{h}") for h in range(PARTS)]
    turned_read = [s.sem(f"{name}_turned_read{h}") for h in range(PARTS)]
    filtered = [s.sem(f"{name}_filtered{h}") for h in range(PARTS)]
    summed, sum_read = s.sem(name + "_summed"), s.sem(name + "_sum_read")
    count_read, count_stored = s.sem(name + "_count_read"), s.sem(name + "_count_stored")
    turns = NT // (2 * GT)
    arrivals = 32 if records else 16
    with ExitStack() as ctx:
        def sb(key, count, shape, dt=F32):
            return [ctx.enter_context(nc.sbuf_tensor(f"{name}_{key}{h}", shape, dt)) for h in range(count)]
        index, fetched = sb("index", 2, [P, GT], I32), sb("fetched", 2, [P, GT, P])
        feat, pick = sb("feat", PARTS, [P, PT, P]), sb("pick", PARTS, [P, PT, P])
        edge_rows = s.edge_rows[:, :].rearrange("(t p) f -> p t f", p=P)
        record_rows = s.records[:, :].rearrange("(t p) f -> p t f", p=P)
        if records:
            index_rec, rec, efT = sb("index_rec", 2, [P, GT, REC]), sb("rec", PARTS, [P, PT, REC]), sb("efT", PARTS, [EF, PT * P])
        if columns:
            lo, hi = columns
            width = hi - lo
            cuts = [(c, min(-(-width // 3), width - c)) for c in range(0, width, -(-width // 3))]
            pick_d, pick_s = sb("pick_d", PARTS, [P, PT, P], BF16), sb("pick_s", PARTS, [P, PT, width], BF16)
            count_row = sb("count_row", 1, [P, width])[0]
        block = ctx.enter_context(nc.Block())
        ps = s.ps[:, :, :].rearrange("p b n -> p (b n)")

        def agg(b):
            return ps[:, ds((b & 1) * 512 + 6 * 512, P)]

        def pairs(b, bank, n):
            return ps[:, ds((b & 1) * (3 * 512) + bank * 512, n)]

        @block.gpsimd
        def _(pool):
            with pool.Fori(0, turns) as i:
                for h in range(2):
                    pool.wait_ge(row_free[h], i + 1)
                    if records:
                        pool.wait_ge(record_back[h], i * 16 + 16)
                        pool.sem_inc(granted, 1)
                        source = index_rec[h][:, :, EF + 2:EF + 3].rearrange("p t o -> p (t o)")
                    else:
                        source = rows[:, ds(i * (2 * GT) + GT * h, GT)]
                    nc.gpsimd.tensor_copy(index[h][:, :], source).then_inc(copied, 1)
                    pool.wait_ge(copied, i * 2 + h + 1)
                    pool.sem_inc(granted, 1)
                    for j in range(GT):
                        nc.gpsimd.indirect_dma_start(out=fetched[h][:, j, :], out_offset=None, in_=table,
                                                     in_offset=bass.IndirectOffsetOnAxis(ap=index[h][:, j:j + 1], axis=0)
                                                     ).then_inc(gathered[h], 16)

        @block.sync
        def _(sp):
            def load_index(i, h):
                sp.dma_start(index_rec[h][:, :, :], record_rows[:, ds(i * (2 * GT) + GT * h, GT), :]).then_inc(record_back[h], 16)

            def turn(i, last):
                for h in range(2):
                    sp.wait_ge(gathered[h], i * (16 * GT) + 16 * GT)
                    sp.dma_start(edge_rows[:, ds(i * (2 * GT) + GT * h, GT), :], fetched[h][:, :, :]).then_inc(stored[h], 16)
                    if records and not last:
                        load_index(i + 1, h)
                    sp.wait_ge(stored[h], i * 16 + 16)
                    sp.sem_inc(row_free[h], 1)

            for h in range(2):
                sp.sem_inc(row_free[h], 1)
                if records:
                    load_index(0, h)
            with sp.Fori(0, turns - 1) as i:
                turn(i, False)
            turn(turns - 1, True)

        @block.scalar
        def _(act):
            def load_block(b):
                first = act.value_load(ranges[0:1, 0, ds(b, 1)], min_val=0, max_val=NT - TG)
                groups = act.value_load(ranges[0:1, 1, ds(b, 1)], min_val=1, max_val=NT // TG)
                before = act.value_load(ranges[0:1, 2, ds(b, 1)], min_val=0, max_val=NB * NT // TG)
                with act.Fori(0, groups) as i:
                    for h in range(PARTS):
                        tile = bounded(first + i * TG + PT * h, NT - PT)
                        turn = ((tile + (PT - 1)) >> (2 * GT).bit_length() - 1) + 1
                        act.wait_ge(used[h], before + i + 1)
                        act.wait_ge(stored[0], turn * 16)
                        act.wait_ge(stored[1], turn * 16)
                        act.dma_start(feat[h][:, :, :], edge_rows[:, ds(tile, PT), :]).then_inc(back[h], 16)
                        if records:
                            act.dma_start(rec[h][:, :, :], record_rows[:, ds(tile, PT), :]).then_inc(back[h], 16)

            def store_counts(b):
                act.wait_ge(count_read, b + 3)
                act.sem_inc(granted, 1)
                act.dma_start(s.counts[ds(b, 1), :, lo:hi].rearrange("o p n -> (o p) n"), count_row[:, :]).then_inc(count_stored, 16)

            load_block(0)
            with act.Fori(1, NB) as b:
                load_block(b)
                if columns:
                    store_counts(b - 1)
            if columns:
                store_counts(NB - 1)
                act.wait_ge(count_stored, 16 * NB)

        @block.vector
        def _(dve):
            def picks(h, tile, n, here):
                for j in range(PT):
                    if records:
                        last = nc.vector.tensor_scalar(pick[h][:, j, :], here, rec[h][:, j, EF + 1:EF + 2], None, ALU.is_equal)
                        continue
                    at = ds(bounded(tile + j, NT - 1), 1)
                    if columns:
                        nc.vector.tensor_scalar(pick_s[h][:, j, :], s.ramp16[:, lo:hi], s.src[:, at], None, ALU.is_equal)
                        nc.vector.tensor_scalar(pick_d[h][:, j, :], here, s.dst[:, at], None, ALU.is_equal)
                    if weighted:
                        last = nc.vector.tensor_scalar(pick[h][:, j, :], here, s.dst[:, at], s.weight[:, at], ALU.is_equal, ALU.mult)
                    else:
                        last = nc.vector.tensor_scalar(pick[h][:, j, :], here, s.dst[:, at], None, ALU.is_equal)
                return last

            def node_block(b):
                first = dve.value_load(ranges[0:1, 0, ds(b, 1)], min_val=0, max_val=NT - TG)
                groups = dve.value_load(ranges[0:1, 1, ds(b, 1)], min_val=1, max_val=NT // TG)
                before = dve.value_load(ranges[0:1, 2, ds(b, 1)], min_val=0, max_val=NB * NT // TG)
                here = s.ramp[:, ds(b * P, P)]
                with dve.Fori(0, groups) as i:
                    n = before + i
                    if records:
                        for h in range(PARTS):
                            dve.wait_ge(turned[h], n + 1)
                            dve.wait_ge(filtered[h], n + 1)
                            nc.vector.tensor_copy(efT[h][:, :], s.ps[0:EF, h, 0:PT * P]).then_inc(turned_read[h], 1)
                    for h in range(PARTS):
                        dve.wait_ge(used[h], n + 1)
                        if records:
                            dve.wait_ge(filtered[h], n + 2)
                            for j in range(PT):
                                nc.vector.scalar_tensor_tensor(out=feat[h][:, j, :], in0=s.ps[:, 4 + h % 2, j * P:(j + 1) * P],
                                                               scalar=rec[h][:, j, EF:EF + 1], in1=feat[h][:, j, :], op0=ALU.mult, op1=ALU.mult)
                        picks(h, first + i * TG + PT * h, n, here).then_inc(picked[h], 1)
                dve.wait_ge(summed, b + 1)
                nc.vector.tensor_copy(s.aggT[:, ds(b * P, P)], agg(b)).then_inc(sum_read, 1)
                if columns:
                    if not isinstance(b, int):
                        dve.wait_ge(count_stored, b * 16)
                    for k, (c, n) in enumerate(cuts):
                        last = nc.vector.tensor_copy(count_row[:, c:c + n], pairs(b, k, n))
                    last.then_inc(count_read, 1)

            node_block(0)
            with dve.Fori(1, NB) as b:
                node_block(b)

        @block.tensor
        def _(pe):
            for h in range(PARTS):
                pe.sem_inc(used[h], 1)
                if records:
                    for sem in (turned_read[h], filtered[h], picked[h]):
                        pe.sem_inc(sem, 1)
            pe.sem_inc(sum_read, 2)
            pe.sem_inc(count_read, 2)

            def turn_features(n, h):
                pe.wait_ge(back[h], n * arrivals + arrivals)
                pe.wait_ge(turned_read[h], n + 1)
                for j in range(PT):
                    last = nc.tensor.transpose(s.ps[0:EF, h, j * P:(j + 1) * P], rec[h][:, j, 0:EF], s.ident[:, :])
                last.then_inc(turned[h], 1)

            def filter_part(n, h):
                pe.wait_ge(turned_read[h], n + 2)
                pe.wait_ge(picked[(h + 2) % PARTS], n + 1 + h // 2)
                for j in range(PT):
                    last = nc.tensor.matmul(s.ps[:, 4 + h % 2, j * P:(j + 1) * P], efT[h][:, j * P:(j + 1) * P], We, start=True, stop=True)
                last.then_inc(filtered[h], 1)

            def collect(b, n, h):
                pe.wait_ge(picked[h], n + (2 if records else 1))
                if columns:
                    for j in range(PT):
                        for k, (c, m) in enumerate(cuts):
                            nc.tensor.matmul(pairs(b, k, m), pick_d[h][:, j, :], pick_s[h][:, j, c:c + m], start=False, stop=False)
                pe.wait_ge(back[h], n * arrivals + arrivals)
                for j in range(PT):
                    last = nc.tensor.matmul(agg(b), feat[h][:, j, :], pick[h][:, j, :], start=False, stop=False)
                last.then_inc(used[h], 1)

            with pe.Fori(0, NB) as b:
                groups = pe.value_load(ranges[0:1, 1, ds(b, 1)], min_val=1, max_val=NT // TG)
                before = pe.value_load(ranges[0:1, 2, ds(b, 1)], min_val=0, max_val=NB * NT // TG)
                pe.wait_ge(sum_read, b + 1)
                nc.tensor.matmul(agg(b), s.zeros_bf[:, 0:P], s.zeros_bf[:, 0:P], start=True, stop=False)
                if columns:
                    pe.wait_ge(count_read, b + 1)
                    for k, (c, m) in enumerate(cuts):
                        nc.tensor.matmul(pairs(b, k, m), s.zeros_bf[:, 0:P], s.zeros_bf[:, 0:m], start=True, stop=False)
                with pe.Fori(0, groups) as i:
                    n = before + i
                    if records:
                        for h in range(PARTS):
                            turn_features(n, h)
                        filter_part(n, 0)
                        filter_part(n, 1)
                        for h in range(PARTS):
                            collect(b, n, h)
                            if h < 2:
                                filter_part(n, h + 2)
                    else:
                        for h in range(PARTS):
                            collect(b, n, h)
                if columns:
                    for k, (c, m) in enumerate(cuts):
                        nc.tensor.matmul(pairs(b, k, m), s.zeros_bf[:, 0:P], s.zeros_bf[:, 0:m], start=False, stop=True)
                nc.tensor.matmul(agg(b), s.zeros_bf[:, 0:P], s.zeros_bf[:, 0:P], start=False, stop=True).then_inc(summed, 1)


class Norm:

    def __init__(self, s):
        self.given, self.mean_ready, self.centred = s.sem("norm_given"), s.sem("norm_mean"), s.sem("norm_centred")
        self.squared, self.var_ready, self.std_ready = s.sem("norm_squared"), s.sem("norm_var"), s.sem("norm_std")
        self.rstd_ready, self.scaled, self.normed = s.sem("norm_rstd"), s.sem("norm_scaled"), s.sem("norm_done")
        self.turns = 0
        self.gained = 0

    def pe(self, nc, pe, s, t):
        pe.wait_ge(self.given, t + 1)
        for h in range(2):
            last = nc.tensor.matmul(s.ps[:, h, 0:HALF], s.mean_w[:, :], s.y[:, h, :], start=True, stop=True)
        last.then_inc(self.mean_ready, 1)
        pe.wait_ge(self.squared, t + 1)
        for h in range(2):
            last = nc.tensor.matmul(s.ps[:, 2 + h, 0:HALF], s.mean_w[:, :], s.sq[:, h, :], start=True, stop=True)
        last.then_inc(self.var_ready, 1)

    def act(self, nc, act, s, t):
        act.wait_ge(self.var_ready, t + 1)
        nc.scalar.activation(s.std[:, :, :], s.ps[:, 2:4, 0:HALF], ACT.Sqrt, bias=s.eps[:, 0:1]).then_inc(self.std_ready, 1)

    def dve(self, nc, dve, s, t, out, gain=None, shift=None, gained=0):
        dve.wait_ge(self.given, t + 1)
        dve.wait_ge(self.mean_ready, t + 1)
        nc.vector.tensor_tensor(s.yc[:, :, :], s.y[:, :, :], s.ps[:, 0:2, 0:HALF], ALU.subtract).then_inc(self.centred, 1)
        dve.wait_ge(self.centred, t + 1)
        nc.vector.tensor_tensor(s.sq[:, :, :], s.yc[:, :, :], s.yc[:, :, :], ALU.mult).then_inc(self.squared, 1)
        dve.wait_ge(self.std_ready, t + 1)
        nc.vector.reciprocal(s.std[:, :, :], s.std[:, :, :]).then_inc(self.rstd_ready, 1)
        dve.wait_ge(self.rstd_ready, t + 1)
        if gain is None:
            nc.vector.tensor_tensor(out, s.yc[:, :, :], s.std[:, :, :], ALU.mult).then_inc(self.normed, 1)
        else:
            nc.vector.tensor_tensor(s.yc[:, :, :], s.yc[:, :, :], s.std[:, :, :], ALU.mult).then_inc(self.scaled, 1)
            dve.wait_ge(self.scaled, gained + 1)
            nc.vector.tensor_scalar(out, s.yc[:, :, :], gain, shift, ALU.mult, ALU.add).then_inc(self.normed, 1)


def node_phase(nc, s, name, weight, source, func, bias, base, gain=None, shift=None, second=None, layer=0):
    key = "node_" + name
    lin, applied, lin2, applied2 = s.sem(key + "_lin"), s.sem(key + "_applied"), s.sem(key + "_lin2"), s.sem(key + "_applied2")
    n = s.norm
    start = n.turns + layer * NCH
    with nc.Block() as block:

        @block.tensor
        def _(pe):
            with pe.Fori(0, NCH) as c:
                pe.wait_ge(n.normed, start + c + 1)
                for h in range(2):
                    last = nc.tensor.matmul(s.ps[:, 4 + h, 0:HALF], weight, source[:, ds(c * CH + h * HALF, HALF)], start=True, stop=True)
                last.then_inc(lin, 1)
                n.pe(nc, pe, s, start + c)
                if second:
                    pe.wait_ge(n.normed, start + c + 2)
                    for h in range(2):
                        last = nc.tensor.matmul(s.ps[:, 6 + h, 0:HALF], second[0], base[:, ds(c * CH + h * HALF, HALF)], start=True, stop=True)
                    last.then_inc(lin2, 1)
                    pe.wait_ge(applied2, c + 1)

        @block.scalar
        def _(act):
            with act.Fori(0, NCH) as c:
                act.wait_ge(lin, layer * NCH + c + 1)
                nc.scalar.activation(s.y[:, :, :], s.ps[:, 4:6, 0:HALF], func, bias=bias).then_inc(applied, 1)
                n.act(nc, act, s, start + c)
                if second:
                    act.wait_ge(lin2, c + 1)
                    nc.scalar.activation(halves(second[3][:, ds(c * CH, CH)]), s.ps[:, 6:8, 0:HALF], second[1], bias=second[2]).then_inc(applied2, 1)

        @block.vector
        def _(dve):
            with dve.Fori(0, NCH) as c:
                dve.wait_ge(applied, layer * NCH + c + 1)
                nc.vector.tensor_tensor(s.y[:, :, :], s.y[:, :, :], halves(base[:, ds(c * CH, CH)]), ALU.add).then_inc(n.given, 1)
                n.dve(nc, dve, s, start + c, halves(base[:, ds(c * CH, CH)]), gain, shift, n.gained + layer * NCH + c)


def node_rows(nc, s, name, source, right, width, write):
    key = "rows_" + name
    held, made, read = s.sem(key + "_held"), s.sem(key + "_made"), s.sem(key + "_read")
    row_free, stored = s.sem(key + "_free"), s.sem(key + "_stored")
    with ExitStack() as ctx:
        hold = ctx.enter_context(nc.sbuf_tensor(key + "_hold", [P, P], F32))
        row = ctx.enter_context(nc.sbuf_tensor(key + "_row", [P, 2, width], F32))
        block = ctx.enter_context(nc.Block())
        banks = -(-width // 512)
        ps = s.ps[:, :, :].rearrange("p b n -> p (b n)")

        @block.vector
        def _(dve):
            def step(b):
                if not isinstance(b, int):
                    dve.wait_ge(made, b)
                nc.vector.tensor_copy(hold[:, :], source[:, ds(b * P, P)]).then_inc(held, 1)
            step(0)
            with dve.Fori(1, NB) as b:
                step(b)

        @block.tensor
        def _(pe):
            with pe.Fori(0, NB) as b:
                pe.wait_ge(held, b + 1)
                pe.wait_ge(read, b + 1)
                base = (b & 1) * (512 * banks)
                for c in range(0, width, 512):
                    last = nc.tensor.matmul(ps[:, ds(base + c, min(512, width - c))], hold[:, :],
                                            right[:, c:min(c + 512, width)], start=True, stop=True)
                last.then_inc(made, 1)

        @block.scalar
        def _(act):
            act.sem_inc(read, 2)
            with act.Fori(0, NB) as b:
                act.wait_ge(made, b + 1)
                act.wait_ge(row_free, b + 1)
                nc.scalar.activation(row[:, ds(b & 1, 1), :].rearrange("p o n -> p (o n)"), ps[:, ds((b & 1) * (512 * banks), width)], ACT.Copy).then_inc(read, 1)

        @block.sync
        def _(sp):
            sp.sem_inc(row_free, 2)

            def step(b, parity):
                sp.wait_ge(read, b + 3)
                write(sp, b, row[:, ds(parity, 1), :].rearrange("p o n -> p (o n)"), stored)
                sp.wait_ge(stored, b * 16 + 16)
                sp.sem_inc(row_free, 1)
            with sp.Fori(0, NB - 1) as b:
                step(b, b & 1)
            step(NB - 1, (NB - 1) & 1)


def gru(nc, s, l):
    key = f"gru{l}"
    gates, rz, hn, pre, tanh = (s.sem(f"{key}_{x}") for x in ("gates", "rz", "hn", "pre", "tanh"))
    diff, mixed, summed, done = (s.sem(f"{key}_{x}") for x in ("diff", "mixed", "summed", "done"))
    with ExitStack() as ctx:
        r, z, n, d = (ctx.enter_context(nc.sbuf_tensor(f"{key}_t{x}", [P, 2, HALF], F32)) for x in "rznd")
        block = ctx.enter_context(nc.Block())
        o = 2 + l * (TYPES + 6) + TYPES

        @block.tensor
        def _(pe):
            def turn(c):
                if not isinstance(c, int):
                    pe.wait_ge(done, c)
                for h in range(2):
                    at = ds(c * CH + h * HALF, HALF)
                    for g in range(2):
                        nc.tensor.matmul(s.ps[:, 2 * g + h, 0:HALF], s.wT[:, o + g, :], s.aggT[:, at], start=True, stop=False)
                        nc.tensor.matmul(s.ps[:, 2 * g + h, 0:HALF], s.wT[:, o + 3 + g, :], s.hT[:, at], start=False, stop=True)
                    nc.tensor.matmul(s.ps[:, 4 + h, 0:HALF], s.wT[:, o + 2, :], s.aggT[:, at], start=True, stop=True)
                    last = nc.tensor.matmul(s.ps[:, 6 + h, 0:HALF], s.wT[:, o + 5, :], s.hT[:, at], start=True, stop=True)
                last.then_inc(gates, 1)
            turn(0)
            with pe.Fori(1, NCH) as c:
                turn(c)

        @block.scalar
        def _(act):
            with act.Fori(0, NCH) as c:
                act.wait_ge(gates, c + 1)
                nc.scalar.activation(r[:, :, :], s.ps[:, 0:2, 0:HALF], ACT.Sigmoid, bias=s.b_rz[:, l, 0:1]).then_inc(rz, 1)
                nc.scalar.activation(z[:, :, :], s.ps[:, 2:4, 0:HALF], ACT.Sigmoid, bias=s.b_rz[:, l, 1:2]).then_inc(rz, 1)
                act.wait_ge(pre, c + 1)
                nc.scalar.activation(n[:, :, :], d[:, :, :], ACT.Tanh, bias=s.bih[:, l, 2:3]).then_inc(tanh, 1)

        @block.vector
        def _(dve):
            with dve.Fori(0, NCH) as c:
                h = halves(s.hT[:, ds(c * CH, CH)])
                dve.wait_ge(rz, c * 2 + 2)
                nc.vector.scalar_tensor_tensor(out=r[:, :, :], in0=s.ps[:, 6:8, 0:HALF], scalar=s.bhh[:, l, 2:3], in1=r[:, :, :],
                                               op0=ALU.add, op1=ALU.mult).then_inc(hn, 1)
                dve.wait_ge(hn, c + 1)
                nc.vector.tensor_tensor(d[:, :, :], r[:, :, :], s.ps[:, 4:6, 0:HALF], ALU.add).then_inc(pre, 1)
                dve.wait_ge(tanh, c + 1)
                nc.vector.tensor_tensor(d[:, :, :], h, n[:, :, :], ALU.subtract).then_inc(diff, 1)
                dve.wait_ge(diff, c + 1)
                nc.vector.tensor_tensor(d[:, :, :], d[:, :, :], z[:, :, :], ALU.mult).then_inc(mixed, 1)
                dve.wait_ge(mixed, c + 1)
                nc.vector.tensor_tensor(d[:, :, :], d[:, :, :], n[:, :, :], ALU.add).then_inc(summed, 1)
                dve.wait_ge(summed, c + 1)
                nc.vector.tensor_scalar(h, d[:, :, :], 0.0, None, ALU.max).then_inc(done, 1)


def place_records(nc, pool, s, turn):
    r = s.placing
    if isinstance(turn, int):
        first = turn * RT
        whole = min(max(FULL_TILES - first, 0), RT)
        if whole < RT:
            pool.memset(r.record[:, :, :], 0.0).then_inc(r.cleared, 1)
            r.clears += 1
            pool.wait_ge(r.cleared, r.clears)
        if whole:
            pool.dma_start(r.record[:, 0:whole, 0:EF], r.features[:, first:first + whole, :]).then_inc(r.ef_back, 16)
            r.loads += 1
        if whole < RT and first + whole == FULL_TILES:
            pool.dma_start(r.record[0:LAST, whole, 0:EF], r.last_features).then_inc(r.ef_back, 16)
            r.loads += 1
        loads = r.loads * 16
    else:
        first = bounded(turn * RT, (LAYERS2 * PLACE_TURNS - 1) * RT)
        pool.dma_start(r.record[:, :, 0:EF], r.features[:, ds(first, RT), :]).then_inc(r.ef_back, 16)
        loads = turn * 16 + 16
    for n, column in enumerate((s.weight1, s.src, s.dst_row)):
        nc.gpsimd.tensor_copy(r.record[:, :, EF + n:EF + n + 1].rearrange("p t o -> p (t o)"), column[:, ds(first, RT)]).then_inc(r.copied, 1)
    nc.gpsimd.tensor_copy(r.place[:, :], s.place[:, ds(first, RT)]).then_inc(r.copied, 1)
    pool.wait_ge(r.copied, turn * 4 + 4)
    pool.sem_inc(r.passed, 1)
    pool.wait_ge(r.ef_back, loads)
    pool.sem_inc(r.passed, 1)
    for j in range(RT):
        nc.gpsimd.indirect_dma_start(out=s.records[:, :], out_offset=bass.IndirectOffsetOnAxis(ap=r.place[:, j:j + 1], axis=0),
                                     in_=r.record[:, j, :], in_offset=None).then_inc(r.scattered, 16)
    pool.wait_ge(r.scattered, turn * (16 * RT) + 16 * RT)
    pool.sem_inc(r.passed, 1)


def project(nc, s, a, l):
    loaded, cols, lin, moved = a.weights_loaded, a.columns, a.lin, a.moved
    held, made, read = a.held, a.made, a.read
    with nc.Block() as block:

        @block.sync
        def _(sp):
            for n, w in enumerate((a.WQ, a.WK, a.WV, a.WO)):
                sp.dma_start(a.w[:, n, :], w[ds(l, 1), :, :].rearrange("l i o -> (l i) o")).then_inc(loaded, 16)
            sp.dma_start(a.bv[:, :], a.bV[ds(l, 1), :]).then_inc(loaded, 16)

        @block.tensor
        def _(pe):
            pe.wait_ge(loaded, l * 80 + 80)
            pe.sem_inc(a.passed, 1)
            with pe.Fori(0, NCH) as c:
                pe.wait_ge(moved, (l * NCH + c) * 2 + 2)
                for n in range(2):
                    for h in range(2):
                        last = nc.tensor.matmul(s.ps[:, 2 * n + h, 0:HALF], a.w[:, n, :], s.hT[:, ds(c * CH + h * HALF, HALF)], start=True, stop=True)
                last.then_inc(lin, 1)
            with pe.Fori(0, NB) as b:
                pe.wait_ge(held, l * NB + b + 1)
                pe.wait_ge(read, l * NB + b + 1)
                nc.tensor.matmul(s.ps[:, 4, 0:P], a.hold[:, :], a.w[:, 2, :], start=True, stop=False)
                nc.tensor.matmul(s.ps[:, 4, 0:P], s.ones[0:1, :], a.bv[0:1, :], start=False, stop=True).then_inc(made, 1)

        @block.scalar
        def _(act):
            act.wait_ge(cols, (l + 1) * 5)
            with act.Fori(0, NCH) as c:
                act.wait_ge(lin, l * NCH + c + 1)
                nc.scalar.activation(halves(a.qT[:, ds(c * CH, CH)]), s.ps[:, 0:2, 0:HALF], ACT.Identity, bias=a.col[:, 0:1]).then_inc(moved, 1)
                nc.scalar.activation(halves(a.kT[:, ds(c * CH, CH)]), s.ps[:, 2:4, 0:HALF], ACT.Identity, bias=a.col[:, 1:2], scale=SHRINK).then_inc(moved, 1)
            with act.Fori(0, NB) as b:
                act.wait_ge(made, l * NB + b + 2)
                nc.scalar.activation(a.v[:, ds(b, 1), 0:P].rearrange("p o f -> p (o f)"), s.ps[:, 4, 0:P], ACT.Copy).then_inc(read, 1)

        @block.vector
        def _(dve):
            for n, (column, factor) in enumerate(((s.bQ, 1.0), (s.bK, SHRINK), (s.bO, 1.0), (s.ln_g, 1.0), (s.ln_b, 1.0))):
                nc.vector.tensor_scalar(a.col[:, n:n + 1], column[:, ds(l, 1)], factor, None, ALU.mult).then_inc(cols, 1)
            with dve.Fori(0, NB) as b:
                dve.wait_ge(made, l * NB + b + 1)
                nc.vector.tensor_copy(a.hold[:, :], s.hT[:, ds(b * P, P)]).then_inc(held, 1)


def attend(nc, s, a, l):
    SC = NP // HALF
    GROUPS = -(-NB // 4)
    with nc.Block() as block:
        def k(b):
            return l * NB + b

        @block.sync
        def _(sp):
            with sp.Fori(0, NB) as b:
                sp.wait_ge(a.count_used, k(b) + 1)
                sp.sem_inc(a.passed, 1)
                sp.dma_start(a.cnt[:, ds(k(b) & 1, 1), :].rearrange("p o n -> p (o n)"),
                             s.counts[ds(b, 1), :, :].rearrange("o p n -> (o p) n")).then_inc(a.count_back, 16)
                sp.wait_ge(a.count_back, k(b) * 16 + 16)
                sp.sem_inc(a.passed, 1)

        @block.gpsimd
        def _(pool):
            with pool.Fori(0, PLACE_TURNS) as i:
                place_records(nc, pool, s, l * PLACE_TURNS + i)

        @block.tensor
        def _(pe):
            def scores(b):
                pe.wait_ge(a.q_held, k(b) + 1)
                for c in range(SC):
                    pe.wait_ge(a.masked, k(b) * SC + c + 1)
                    nc.tensor.matmul(s.ps[:, c % 4, 0:HALF], a.q[:, :], a.kT[:, c * HALF:(c + 1) * HALF], start=True, stop=True).then_inc(a.scored, 1)

            def turn_result(b):
                pe.wait_ge(a.msg_read, k(b) + 2)
                pe.wait_ge(a.att_read, k(b) + 1)
                nc.tensor.transpose(s.ps[:, 7, 0:P], a.msg[:, :], s.ident[:, :]).then_inc(a.msg_turned, 1)

            def values(b):
                def turn_group(g):
                    pe.wait_ge(a.pt_read, k(b) * GROUPS + g + 1)
                    for n in range(4 * g, min(4 * g + 4, NB)):
                        last = nc.tensor.transpose(s.ps[:, 4 + g % 2, (n % 4) * P:(n % 4 + 1) * P], a.pm[:, n * P:(n + 1) * P], s.ident[:, :])
                    last.then_inc(a.turned, 1)

                def add_group(g):
                    pe.wait_ge(a.pt_read, k(b) * GROUPS + g + 3)
                    for n in range(4 * g, min(4 * g + 4, NB)):
                        last = nc.tensor.matmul(s.ps[:, 6, 0:P + 1], a.pt[:, n * P:(n + 1) * P], a.v[:, n, 0:P + 1], start=n == 0, stop=n == NB - 1)
                    return last

                pe.wait_ge(a.weighed, k(b) * SC + SC)
                turn_group(0)
                turn_group(1)
                pe.wait_ge(a.msg_read, k(b) + 1)
                for g in range(GROUPS):
                    last = add_group(g)
                    if g + 2 < GROUPS:
                        turn_group(g + 2)
                last.then_inc(a.summed, 1)

            scores(0)
            scores(1)
            values(0)
            with pe.Fori(2, NB) as b:
                scores(b)
                turn_result(b - 2)
                values(b - 1)
            turn_result(NB - 2)
            values(NB - 1)
            turn_result(NB - 1)

        @block.scalar
        def _(act):
            def exps(b):
                act.wait_ge(a.biased, k(b) + 1)
                for h in range(2):
                    at = ds((k(b) & 1) * NP + h * (NP // 2), NP // 2)
                    nc.scalar.activation(a.t[:, at], a.t[:, at], ACT.Exp, bias=a.bias[:, 0:1], scale=-SCALE / SHRINK).then_inc(a.exped, 1)

            def copy_result(b):
                act.wait_ge(a.msg_turned, k(b) + 1)
                nc.scalar.activation(s.aggT[:, ds(b * P, P)], s.ps[:, 7, 0:P], ACT.Copy).then_inc(a.att_read, 1)

            def copy_groups(b):
                act.wait_ge(a.summed, k(b) + 1)
                for g in range(GROUPS):
                    n = min(4 * g + 4, NB) - 4 * g
                    act.wait_ge(a.turned, k(b) * GROUPS + g + 2)
                    nc.scalar.activation(a.pt[:, 4 * g * P:(4 * g + n) * P], s.ps[:, 4 + g % 2, 0:n * P], ACT.Copy).then_inc(a.pt_read, 1)

            exps(0)
            copy_groups(0)
            exps(1)
            with act.Fori(2, NB) as b:
                copy_result(b - 2)
                copy_groups(b - 1)
                exps(b)
            copy_result(NB - 2)
            copy_groups(NB - 1)
            copy_result(NB - 1)

        @block.vector
        def _(dve):
            def hold_q(b):
                if isinstance(b, int) and b == 0:
                    pass
                else:
                    dve.wait_ge(a.scored, k(b) * SC)
                nc.vector.tensor_copy(a.q[:, :], a.qT[:, ds(b * P, P)]).then_inc(a.q_held, 1)

            def chunk(b, c, mark, weigh):
                here = k(b) & 1
                if mark:
                    if c == 0:
                        dve.wait_ge(a.count_back, k(b) * 16 + 16)
                    dve.wait_ge(a.scored, k(b) * SC + c + 1)
                    nc.vector.scalar_tensor_tensor(out=a.t[:, ds(here * NP + c * HALF, HALF)],
                                                   in0=a.cnt[:, ds(here, 1), c * HALF:(c + 1) * HALF].rearrange("p o n -> p (o n)"),
                                                   scalar=0.5, in1=s.ps[:, c % 4, 0:HALF], op0=ALU.is_lt, op1=ALU.subtract).then_inc(a.masked, 1)
                if weigh:
                    w = b - 1
                    there = k(w) & 1
                    if c == 0:
                        dve.wait_ge(a.turned, k(w) * GROUPS + 1)
                    if c % (SC // 2) == 0:
                        dve.wait_ge(a.exped, k(w) * 2 + c // (SC // 2) + 1)
                    ins = nc.vector.tensor_tensor(a.pm[:, c * HALF:(c + 1) * HALF], a.t[:, ds(there * NP + c * HALF, HALF)],
                                                  a.cnt[:, ds(there, 1), c * HALF:(c + 1) * HALF].rearrange("p o n -> p (o n)"), ALU.mult)
                    ins.then_inc(a.weighed, 1)
                    if c == SC - 1:
                        dve.wait_ge(a.weighed, k(w) * SC + SC)
                        dve.sem_inc(a.count_used, 1)

            def greatest(b):
                dve.wait_ge(a.masked, k(b) * SC + SC + 4)
                dve.sem_inc(a.passed, 1)
                nc.vector.tensor_reduce(out=a.least[:, 0:1], in_=a.t[:, ds((k(b) & 1) * NP, NP)], axis=AX.X, op=ALU.min).then_inc(a.least_ready, 1)
                dve.wait_ge(a.least_ready, k(b) + 1)
                dve.wait_ge(a.exped, k(b) * 2) if not (isinstance(b, int) and b == 0) else None
                nc.vector.tensor_scalar(a.bias[:, 0:1], a.least[:, 0:1], SCALE / SHRINK, None, ALU.mult).then_inc(a.biased, 1)

            def result(b):
                dve.wait_ge(a.summed, k(b) + 2)
                nc.vector.tensor_scalar(a.den[:, 0:1], s.ps[:, 6, P:P + 1], 1e-30, None, ALU.max).then_inc(a.den_ready, 1)
                dve.wait_ge(a.den_ready, k(b) + 1)
                nc.vector.reciprocal(a.den[:, 1:2], a.den[:, 0:1]).then_inc(a.inv_ready, 1)
                dve.wait_ge(a.inv_ready, k(b) + 1)
                dve.wait_ge(a.msg_turned, k(b)) if not (isinstance(b, int) and b == 0) else None
                nc.vector.tensor_scalar(a.msg[:, :], s.ps[:, 6, 0:P], a.den[:, 1:2], None, ALU.mult).then_inc(a.msg_read, 1)

            hold_q(0)
            for c in range(SC):
                chunk(0, c, True, False)
            hold_q(1)
            greatest(0)
            for c in range(SC):
                chunk(1, c, True, True)
            hold_q(2)
            greatest(1)
            with dve.Fori(2, NB - 1) as b:
                for c in range(SC):
                    chunk(b, c, True, True)
                hold_q(b + 1)
                result(b - 2)
                greatest(b)
            for c in range(SC):
                chunk(NB - 1, c, True, True)
            result(NB - 3)
            greatest(NB - 1)
            for c in range(SC):
                chunk(NB, c, False, True)
            result(NB - 2)
            result(NB - 1)


def attention_layers(nc, s, WQ, WK, WV, bV, WO):
    a = Shared()
    a.WQ, a.WK, a.WV, a.bV, a.WO = WQ, WK, WV, bV, WO
    a.weights_loaded, a.columns, a.lin, a.moved, a.held, a.made, a.read, a.count_used, a.count_back = (
        s.sem("att_" + n) for n in "weights_loaded columns lin moved held made read count_used count_back".split())
    a.q_held, a.scored, a.masked, a.least_ready, a.biased, a.exped, a.weighed, a.turned, a.pt_read = (
        s.sem("att_" + n) for n in "q_held scored masked least_ready biased exped weighed turned pt_read".split())
    a.summed, a.den_ready, a.inv_ready, a.msg_read, a.msg_turned, a.att_read, a.passed = (
        s.sem("att_" + n) for n in "summed den_ready inv_ready msg_read msg_turned att_read passed".split())
    with ExitStack() as ctx:
        def sb(name, shape):
            return ctx.enter_context(nc.sbuf_tensor("att_" + name, shape, F32))
        a.w, a.bv, a.col, a.hold, a.q = sb("w", [P, 4, P]), sb("bv", [1, P]), sb("col", [P, 5]), sb("hold", [P, P]), sb("q", [P, P])
        a.qT, a.kT, a.v = sb("qT", [P, NP]), sb("kT", [P, NP]), sb("v", [P, NB, P + 1])
        a.cnt, a.t, a.pm, a.pt = sb("cnt", [P, 2, NP]), sb("t", [P, 2 * NP]), sb("pm", [P, NP]), sb("pt", [P, NP])
        a.least, a.bias, a.den, a.msg = sb("least", [P, 1]), sb("bias", [P, 1]), sb("den", [P, 2]), sb("msg", [P, P])
        with nc.Block() as block:
            @block.gpsimd
            def _(pool):
                pool.memset(s.placing.record[:, :, :], 0.0).then_inc(s.placing.cleared, 1)

            @block.vector
            def _(dve):
                nc.vector.memset(a.v[:, :, P:P + 1], 1.0)
                for sem, credit in ((a.moved, 2), (a.read, 1), (a.made, 1), (a.count_used, 2), (a.masked, 4), (a.pt_read, 2),
                                    (a.summed, 1), (a.turned, 1), (a.msg_read, 1), (a.att_read, 1)):
                    dve.sem_inc(sem, credit)
        with nc.Fori(0, LAYERS2) as l:
            project(nc, s, a, l)
            attend(nc, s, a, l)
            node_phase(nc, s, "att", a.w[:, 3, :], s.aggT, ACT.Identity, a.col[:, 2:3], s.hT, gain=a.col[:, 3:4], shift=a.col[:, 4:5], layer=l)
    s.norm.turns += LAYERS2 * NCH
    s.norm.gained += LAYERS2 * NCH


class Residual:

    def __init__(self, s):
        self.given, self.lin, self.sig, self.gated, self.added = (s.sem("res_" + n) for n in ("given", "lin", "sig", "gated", "added"))

    def pe(self, nc, pe, s, r, w0, w1, source):
        pe.wait_ge(self.given, r + 1)
        for stage, (w, x) in enumerate(((w0, source), (w1, s.res_h))):
            if stage:
                pe.wait_ge(self.gated, r * 2 + 1)
            for h in range(2):
                last = nc.tensor.matmul(s.ps[:, 4 + h, 0:HALF], w, x[:, h, :], start=True, stop=True)
            last.then_inc(self.lin, 1)

    def act(self, nc, act, s, r, b0, b1):
        for stage, b in enumerate((b0, b1)):
            act.wait_ge(self.lin, r * 2 + stage + 1)
            nc.scalar.activation(s.res_g[:, :, :], s.ps[:, 4:6, 0:HALF], ACT.Sigmoid, bias=b).then_inc(self.sig, 1)

    def dve(self, nc, dve, s, r, b0, b1, source, out):
        for stage, b in enumerate((b0, b1)):
            dve.wait_ge(self.sig, r * 2 + stage + 1)
            nc.vector.scalar_tensor_tensor(out=s.res_h[:, :, :], in0=s.ps[:, 4:6, 0:HALF], scalar=b, in1=s.res_g[:, :, :],
                                           op0=ALU.add, op1=ALU.mult).then_inc(self.gated, 1)
        dve.wait_ge(self.gated, r * 2 + 2)
        nc.vector.tensor_tensor(out, s.res_h[:, :, :], source, ALU.add).then_inc(self.added, 1)


def embed(nc, s, f):
    with nc.Block() as block:

        @block.sync
        def _(sp):
            for dest, dram in f.loads:
                sp.dma_start(dest, dram).then_inc(f.loaded, 16)

        @block.gpsimd
        def _(pool):
            for turn in range(LAYERS2 * PLACE_TURNS, NT // RT):
                place_records(nc, pool, s, turn)

        @block.tensor
        def _(pe):
            pe.wait_ge(f.loaded, 16 * len(f.loads))
            with pe.Fori(0, NCH) as c:
                for e in range(2):
                    s.res.pe(nc, pe, s, c * 2 + e, f.W_emb[:, 2 * e, :], f.W_emb[:, 2 * e + 1, :], halves(s.xT[:, ds(c * CH, CH)]))

        @block.scalar
        def _(act):
            act.wait_ge(f.loaded, 16 * len(f.loads))
            with act.Fori(0, NCH) as c:
                for e in range(2):
                    s.res.act(nc, act, s, c * 2 + e, f.b_emb[:, 2 * e:2 * e + 1], f.b_emb[:, 2 * e + 1:2 * e + 2])

        @block.vector
        def _(dve):
            dve.wait_ge(f.loaded, 16 * len(f.loads))
            with dve.Fori(0, NCH) as c:
                for e, out in enumerate((f.srcT, s.hT)):
                    dve.sem_inc(s.res.given, 1)
                    s.res.dve(nc, dve, s, c * 2 + e, f.b_emb[:, 2 * e:2 * e + 1], f.b_emb[:, 2 * e + 1:2 * e + 2],
                              halves(s.xT[:, ds(c * CH, CH)]), halves(out[:, ds(c * CH, CH)]))
                    dve.wait_ge(s.res.added, c * 2 + e + 1)


def place_edges(nc, s):
    done, counted, based, chain = s.sem("place_done"), s.sem("place_counted"), s.sem("place_based"), s.sem("place_chain")
    BUCKETS = NB + 1
    with ExitStack() as ctx:
        def sb(name, shape, dt=F32):
            return ctx.enter_context(nc.sbuf_tensor("place_" + name, shape, dt))
        blk_i, blk, hit, run, slot = sb("blk_i", [P, NT], I32), sb("blk", [P, NT]), sb("hit", [P, NT]), sb("run", [P, NT]), sb("slot", [P, NT])
        count, total, upto, base = sb("count", [P, BUCKETS]), sb("total", [P, BUCKETS]), sb("upto", [P, BUCKETS]), sb("base", [P, BUCKETS])
        row_i, row = sb("row_i", [1, 3, NB], I32), sb("row", [1, NB])
        block = ctx.enter_context(nc.Block())

        @block.tensor
        def _(pe):
            pe.wait_ge(counted, 1)
            nc.tensor.matmul(s.ps[:, 0, 0:BUCKETS], s.ones[:, :], count[:, :], start=True, stop=True).then_inc(based, 1)
            nc.tensor.matmul(s.ps[:, 1, 0:BUCKETS], s.before[:, :], count[:, :], start=True, stop=True).then_inc(based, 1)

        @block.vector
        def _(dve):
            step = [0]

            def link(ins):
                step[0] += 1
                ins.then_inc(done, 1)
                dve.wait_ge(done, step[0])

            link(nc.vector.tensor_copy(blk_i[:, :], s.src[:, 0:NT]))
            link(nc.vector.tensor_scalar(blk_i[:, :], blk_i[:, :], P.bit_length() - 1, None, ALU.arith_shift_right))
            link(nc.vector.tensor_copy(blk[:, :], blk_i[:, :]))
            link(nc.vector.memset(slot[:, :], 0.0))
            with dve.Fori(0, BUCKETS) as b:
                nc.vector.tensor_scalar(hit[:, :], blk[:, :], s.ramp[:, ds(b, 1)], None, ALU.is_equal, ALU.add,
                                        accum_out=count[:, ds(b, 1)]).then_inc(chain, 1)
                dve.wait_ge(chain, b + 1)
            dve.sem_inc(counted, 1)
            dve.wait_ge(based, 2)
            link(nc.vector.tensor_copy(total[:, :], s.ps[:, 0, 0:BUCKETS]))
            link(nc.vector.tensor_tensor_scan(upto[:, :], total[:, :], total[:, :], 0.0, ALU.add, ALU.max))
            link(nc.vector.tensor_tensor(total[:, :], upto[:, :], total[:, :], ALU.subtract))
            link(nc.vector.tensor_tensor(base[:, :], total[:, :], s.ps[:, 1, 0:BUCKETS], ALU.add))
            link(nc.vector.tensor_scalar(base[:, :], base[:, :], -1.0, None, ALU.add))
            with dve.Fori(0, BUCKETS) as b:
                nc.vector.tensor_scalar(hit[:, :], blk[:, :], s.ramp[:, ds(b, 1)], None, ALU.is_equal).then_inc(chain, 1)
                dve.wait_ge(chain, b * 4 + BUCKETS + 1)
                nc.vector.tensor_tensor_scan(run[:, :], hit[:, :], hit[:, :], 0.0, ALU.add, ALU.max).then_inc(chain, 1)
                dve.wait_ge(chain, b * 4 + BUCKETS + 2)
                nc.vector.scalar_tensor_tensor(out=run[:, :], in0=run[:, :], scalar=base[:, ds(b, 1)], in1=hit[:, :],
                                               op0=ALU.add, op1=ALU.mult).then_inc(chain, 1)
                dve.wait_ge(chain, b * 4 + BUCKETS + 3)
                nc.vector.tensor_tensor(slot[:, :], slot[:, :], run[:, :], ALU.add).then_inc(chain, 1)
            dve.wait_ge(chain, BUCKETS * 5)
            link(nc.vector.tensor_copy(s.place[:, :], slot[:, :]))
            SHIFT = P.bit_length() - 1
            link(nc.vector.tensor_copy(row_i[0:1, 0, :], total[0:1, 0:NB]))
            link(nc.vector.tensor_scalar(row[0:1, :], upto[0:1, 0:NB], float(P - 1), None, ALU.add))
            link(nc.vector.tensor_copy(row_i[0:1, 1, :], row[0:1, :]))
            link(nc.vector.tensor_scalar(row_i[0:1, 0:2, :], row_i[0:1, 0:2, :], SHIFT, None, ALU.arith_shift_right))
            link(nc.vector.tensor_copy(s.src_range[0:1, 0, :], row_i[0:1, 0, :]))
            link(nc.vector.tensor_tensor(row_i[0:1, 1, :], row_i[0:1, 1, :], row_i[0:1, 0, :], ALU.subtract))
            link(nc.vector.tensor_scalar(row_i[0:1, 1, :], row_i[0:1, 1, :], float(TG - 1), float(TG), ALU.add, ALU.max))
            link(nc.vector.tensor_scalar(row_i[0:1, 2, :], row_i[0:1, 1, :], TG.bit_length() - 1, None, ALU.arith_shift_right))
            link(nc.vector.tensor_copy(s.src_range[0:1, 1, :], row_i[0:1, 2, :]))
            link(nc.vector.tensor_copy(row[0:1, :], row_i[0:1, 2, :]))
            link(nc.vector.tensor_tensor_scan(upto[0:1, 0:NB], row[0:1, :], row[0:1, :], 0.0, ALU.add, ALU.max))
            link(nc.vector.tensor_tensor(s.src_range[0:1, 2, :], upto[0:1, 0:NB], row[0:1, :], ALU.subtract))


def convolve(nc, s, f):
    scaled, mixed = s.sem("conv_scaled"), s.sem("conv_mixed")
    R0 = 2 * NCH
    weights = [(f.W_conv, f.b_conv, 0), (f.W_conv, f.b_conv, 1), (f.W_out, f.b_out, 0), (f.W_out, f.b_out, 1)]
    n = s.norm
    with nc.Block() as block:

        @block.tensor
        def _(pe):
            with pe.Fori(0, NCH) as c:
                for e, (w, _, r) in enumerate(weights):
                    s.res.pe(nc, pe, s, c * 4 + (R0 + e), w[:, 2 * r, :], w[:, 2 * r + 1, :], s.y)
                n.pe(nc, pe, s, n.turns + c)

        @block.scalar
        def _(act):
            with act.Fori(0, NCH) as c:
                for e, (_, b, r) in enumerate(weights):
                    s.res.act(nc, act, s, c * 4 + (R0 + e), b[:, 2 * r:2 * r + 1], b[:, 2 * r + 1:2 * r + 2])
                n.act(nc, act, s, n.turns + c)

        @block.vector
        def _(dve):
            with dve.Fori(0, NCH) as c:
                at = ds(c * CH, CH)
                dve.wait_ge(n.normed, n.turns + c + 1)
                nc.vector.tensor_scalar(s.y[:, :, :], halves(s.aggT[:, at]), f.C[:, 0:1], None, ALU.mult).then_inc(scaled, 1)
                dve.wait_ge(scaled, c + 1)
                dve.sem_inc(s.res.given, 1)
                for e, (_, b, r) in enumerate(weights):
                    s.res.dve(nc, dve, s, c * 4 + (R0 + e), b[:, 2 * r:2 * r + 1], b[:, 2 * r + 1:2 * r + 2], s.y[:, :, :], s.y[:, :, :])
                    dve.wait_ge(s.res.added, c * 4 + (R0 + e + 1))
                    if e == 1:
                        nc.vector.tensor_tensor(s.y[:, :, :], s.y[:, :, :], halves(f.srcT[:, at]), ALU.mult).then_inc(mixed, 1)
                        dve.wait_ge(mixed, c + 1)
                    if e < 3:
                        dve.sem_inc(s.res.given, 1)
                nc.vector.tensor_tensor(s.y[:, :, :], s.y[:, :, :], halves(s.xT[:, at]), ALU.add).then_inc(n.given, 1)
                n.dve(nc, dve, s, n.turns + c, halves(s.xT[:, at]))


def gnn_kernel(nc, d_x, d_src, d_dst, d_ef, d_type, d_weight, d_weight1, W0, b0, proj_w, proj_b, edge_W, edge_b,
               wih, whh, bih, bhh, out_w, out_b, Wn, bn, WQ, bQ, WK, bK, WV, bV, WO, bO, ln_g, ln_b, Wout, bout,
               C, W_emb, b_emb, We, W_conv, b_conv, W_out, b_out, out):
    with ExitStack() as ctx:
        def sb(name, shape, dt=F32):
            return ctx.enter_context(nc.sbuf_tensor(name, shape, dt))

        s = Shared()
        s.sem = lambda name: ctx.enter_context(nc.semaphore(name))

        def phase(step, *args, **kwargs):
            kept, own = s.sem, []

            def take(name):
                own.append(nc.alloc_semaphore(name))
                return own[-1]
            s.sem = take
            step(nc, s, *args, **kwargs)
            s.sem = kept
            nc.clear_and_free_semaphores(own)
            nc.all_engine_barrier()
        s.ps = ctx.enter_context(nc.psum_tensor("ps", [P, 8, 512], F32))
        s.groups_of = groups_of
        s.d_x, s.d_src, s.d_dst, s.d_type, s.d_weight = d_x, d_src, d_dst, d_type, d_weight
        s.d_weight1 = d_weight1.rearrange("e o -> (e o)")
        s.d_proj_w, s.d_out_w, s.d_edge_W, s.d_wih, s.d_whh = proj_w, out_w, edge_W, wih, whh
        s.d_W0, s.d_Wn, s.d_Wout = W0, Wn, Wout

        s.edge_rows = nc.dram_tensor("edge_rows", (NT * P, P), F32, kind="Internal").ap()
        s.counts = nc.dram_tensor("counts", (NB, P, NP), F32, kind="Internal").ap()
        s.typed = nc.dram_tensor("typed", (TYPES * NP, P), F32, kind="Internal").ap()
        s.plain = nc.dram_tensor("plain", (NP, P), F32, kind="Internal").ap()
        s.records = nc.dram_tensor("records", (NT * P, REC), F32, kind="Internal").ap()

        s.ident, s.before, s.mean_w, s.ones = (sb(n, [P, P]) for n in ("ident", "before", "mean_w", "ones"))
        s.zeros_bf = sb("zeros_bf", [P, 512], BF16)
        s.eps = sb("eps", [P, 1])
        s.ramp = sb("ramp", [P, NP])
        s.tile_i, s.tile_no = sb("tile_i", [P, TC], I32), sb("tile_no", [P, TC])
        s.start_i, s.start = sb("start_i", [P, NB + 1], I32), sb("start", [P, NB + 1])
        s.src, s.weight1, s.dst_row = sb("src", [P, TC * P]), sb("weight1", [P, TC * P]), sb("dst_row", [P, NT], I32)
        s.dst_range = sb("dst_range", [1, 3, NB], I32)
        s.src_range = sb("src_range", [1, 3, NB], I32)
        s.place = sb("place", [P, NT], I32)
        s.xT, s.hT, s.aggT = (sb(n, [P, NP]) for n in ("xT", "hT", "aggT"))
        s.W0, s.Wn, s.Wout = (sb(n, [P, P]) for n in ("W0", "Wn", "Wout"))
        s.y, s.yc, s.sq, s.std = (sb(n, [P, 2, HALF]) for n in ("norm_y", "norm_yc", "norm_sq", "norm_sd"))
        s.bih, s.bhh, s.b_rz = sb("bih", [P, LAYERS1, 3]), sb("bhh", [P, LAYERS1, 3]), sb("b_rz", [P, LAYERS1, 2])
        s.bias_loads = []

        def column(name, dram, cols):
            c = sb("col_" + name, [P, cols])
            s.bias_loads.append((c[:, :], dram))
            return c
        one = "(f o) -> f o"
        s.b0, s.b_proj, s.b_out1 = (column(n, a.rearrange(one, o=1), 1) for n, a in (("b0", b0), ("proj", proj_b), ("out1", out_b)))
        s.bn, s.b_out2 = (column(n, a.rearrange(one, o=1), 1) for n, a in (("bn", bn), ("out2", bout)))
        s.bQ, s.bK, s.bO, s.ln_g, s.ln_b = (column(n, a.rearrange("l f -> f l"), LAYERS2)
                                            for n, a in (("bQ", bQ), ("bK", bK), ("bO", bO), ("g", ln_g), ("b", ln_b)))
        for l in range(LAYERS1):
            s.bias_loads += [(s.bih[:, l, :], bih[l].rearrange("(g f) -> f g", f=P)), (s.bhh[:, l, :], bhh[l].rearrange("(g f) -> f g", f=P))]
        s.norm = Norm(s)

        early = ExitStack()

        def sb_early(name, shape, dt=F32):
            return early.enter_context(nc.sbuf_tensor(name, shape, dt))
        s.ramp16 = sb_early("ramp16", [P, NP], I16)
        s.dst, s.typ, s.weight = (sb_early(n, [P, TC * P]) for n in ("dst", "typ", "weight"))
        s.src_row, s.typed_row = (sb_early(n, [P, NT], I32) for n in ("src_row", "typed_row"))
        s.wT = sb_early("wT", [P, 2 + LAYERS1 * (TYPES + 6), P])

        with nc.allow_non_contiguous_dma(reason="bias columns"):
            phase(constants)
            phase(load_edges)
            phase(load_nodes)
        phase(place_edges)

        def write_table(table, types):
            view = table.rearrange("(t n) f -> n t f", t=types)

            def write(sp, b, row, stored):
                sp.dma_start(view[ds(b * P, P), :, :], row.rearrange("p (t f) -> p t f", t=types)).then_inc(stored, 16)
            return write

        def write_out(sp, b, row, stored):
            if isinstance(b, int):
                sp.dma_start(out[b * P:NODES, :], row[0:NODES - b * P, :]).then_inc(stored, 16)
            else:
                sp.dma_start(out[ds(b * P, P), :], row).then_inc(stored, 16)

        thirds = [(0, 1024), (1024, 2112), (2112, NP)]

        def run():
            phase(edge_pass, "sum0", s.d_x[:, :], s.src_row, s.dst_range, weighted=True, columns=thirds[0])
            node_phase(nc, s, "0", s.W0[:, :], s.aggT, ACT.Relu, s.b0[:, 0:1], s.xT,
                       second=(s.wT[:, 0, :], ACT.Relu, s.b_proj[:, 0:1], s.hT))
            s.norm.turns += NCH
            for l in range(LAYERS1):
                o = 2 + l * (TYPES + 6)
                phase(node_rows, f"typed{l}", s.hT, s.wT[:, o:o + TYPES, :].rearrange("p t f -> p (t f)"), TYPES * P, write_table(s.typed, TYPES))
                phase(edge_pass, f"sum1{l}", s.typed[:, :], s.typed_row, s.dst_range, columns=thirds[1 + l])
                phase(gru, l)
            node_phase(nc, s, "1", s.wT[:, 1, :], s.hT, ACT.Identity, s.b_out1[:, 0:1], s.xT,
                       second=(s.Wn[:, :], ACT.Identity, s.bn[:, 0:1], s.hT))
            s.norm.turns += NCH
            early.close()
            r = s.placing = Shared()
            r.ef_back, r.copied, r.passed, r.scattered, r.cleared = (
                s.sem("place_" + n) for n in "ef_back copied passed scattered cleared".split())
            r.record, r.place = sb("place_record", [P, RT, REC]), sb("place_index", [P, RT], I32)
            r.features = d_ef[0:FULL_TILES * P, :].rearrange("(t p) k -> p t k", p=P)
            r.last_features = d_ef[FULL_TILES * P:EDGES, :]
            r.loads, r.clears = LAYERS2 * PLACE_TURNS, 1
            attention_layers(nc, s, WQ, WK, WV, bV, WO)
            node_phase(nc, s, "2", s.Wout[:, :], s.hT, ACT.Identity, s.b_out2[:, 0:1], s.xT)
            s.norm.turns += NCH
            late = ExitStack()
            f = Shared()
            f.loaded, f.loads = s.sem("late_loaded"), []

            def sb_late(name, shape, dram=None, dt=F32):
                t = late.enter_context(nc.sbuf_tensor("late_" + name, shape, dt))
                if dram is not None:
                    f.loads.append((t[:], dram))
                return t
            two = "a b i o -> i (a b) o"
            f.W_emb, f.W_conv, f.W_out = (sb_late(n, [P, 4, P], a.rearrange(two)) for n, a in (("W_emb", W_emb), ("W_conv", W_conv), ("W_out", W_out)))
            f.b_emb, f.b_conv, f.b_out = (sb_late(n, [P, 4], a.rearrange("a b f -> f (a b)")) for n, a in (("b_emb", b_emb), ("b_conv", b_conv), ("b_out", b_out)))
            f.We = sb_late("We", [EF, P], We)
            f.C = sb_late("C", [P, 1], C.rearrange("(o c) -> o c", o=1).broadcast_to([P, 1]))
            f.srcT = sb_late("srcT", [P, NP])
            s.res_h, s.res_g = sb_late("res_h", [P, 2, HALF]), sb_late("res_g", [P, 2, HALF])
            s.res = Residual(s)
            with nc.allow_non_contiguous_dma(reason="bias columns"):
                embed(nc, s, f)
            phase(node_rows, "plain", s.hT, s.ident[:, :], P, write_table(s.plain, 1))
            phase(edge_pass, "sum3", s.plain[:, :], None, s.src_range, We=f.We[:, :])
            phase(convolve, f)
            late.close()
            return s.xT
        final = run()
        phase(node_rows, "out", final, s.ident[:, :], P, write_out)




_INS = ['x', 'src', 'dst', 'edge_attr_32', 'edge_type_8', 'edge_weight', 'edge_weight1', 'L0_gnn_W', 'L0_gnn_b',
        'L1_gnn_node_proj_w', 'L1_gnn_node_proj_b', 'L1_gnn_edge_W', 'L1_gnn_edge_b', 'L1_gnn_gru_wih',
        'L1_gnn_gru_whh', 'L1_gnn_gru_bih', 'L1_gnn_gru_bhh', 'L1_gnn_out_w', 'L1_gnn_out_b', 'L2_gnn_Wn',
        'L2_gnn_bn', 'L2_gnn_WQ', 'L2_gnn_bQ', 'L2_gnn_WK', 'L2_gnn_bK', 'L2_gnn_WV', 'L2_gnn_bV', 'L2_gnn_WO',
        'L2_gnn_bO', 'L2_gnn_ln_g', 'L2_gnn_ln_b', 'L2_gnn_Wout', 'L2_gnn_bout', 'L3_gnn_C', 'L3_gnn_W_emb',
        'L3_gnn_b_emb', 'L3_gnn_We', 'L3_gnn_W_conv', 'L3_gnn_b_conv', 'L3_gnn_W_out', 'L3_gnn_b_out']
_OUTS = [((3125, 128), 'float32')]


def kernel(**inputs):
    import numpy as _np
    import concourse.bacc as _bacc
    from concourse import mybir as _mybir
    from concourse.bass_utils import run_bass_kernel_spmd as _run

    nc = _bacc.Bacc("TRN2", target_bir_lowering=False, num_devices=1)
    arrays, args = {}, []
    for name in _INS:
        a = _np.ascontiguousarray(inputs[name])
        arrays[f"in_{name}_dram"] = a
        args.append(nc.dram_tensor(f"in_{name}_dram", a.shape, _mybir.dt.from_np(a.dtype), kind="ExternalInput").ap())
    for i, (shape, dtype) in enumerate(_OUTS):
        dt = _mybir.dt.from_np(_np.dtype(dtype))
        args.append(nc.dram_tensor(f"out_{i}_dram", shape, dt, kind="ExternalOutput").ap())
    gnn_kernel(nc, *args)
    r = _run(nc, [arrays], core_ids=[0])
    got = tuple(r.results[0][f"out_{i}_dram"] for i in range(len(_OUTS)))
    return got[0]
```

```python
import concourse.bass as bass
from concourse import mybir
from contextlib import ExitStack

F32 = mybir.dt.float32
BF16 = mybir.dt.bfloat16
I32 = mybir.dt.int32
I16 = mybir.dt.int16
ALU = mybir.AluOpType
ACT = mybir.ActivationFunctionType
AX = mybir.AxisListType
ds = bass.ds

P = 128
NODES = 3125
EDGES = 100000
NB = -(-NODES // P)
NP = NB * P
FULL_TILES = EDGES // P
LAST = EDGES - FULL_TILES * P
TILES = -(-EDGES // P)
TG = 8
PARTS = 4
PT = TG // PARTS
GT = 8
RT = 10
NT = -(-(TILES + 2 * TG) // (2 * TG)) * 2 * TG
TC = -(-NT // P)
PAD_NODE = NP + 5
TYPES = 8
LAYERS1 = 2
LAYERS2 = 4
EF = 32
HALF = 400
CH = 2 * HALF
NCH = NP // CH
EPS = 1e-5
BIG = 4096.0
SHRINK = 2.0 ** -64
SCALE = float(P) ** -0.5
REC = EF + 4
PLACE_TURNS = FULL_TILES // (LAYERS2 * RT)


class Shared:
    pass


def halves(ap):
    return ap.rearrange("p (h n) -> p h n", h=2)


def bounded(value, top):
    return value.with_bounds(min_val=0, max_val=top, guaranteed_mod_val=0, out_of_modulus=1)


def constants(nc, s):
    filled, made = s.sem("const_filled"), s.sem("const_made")
    with nc.sbuf_tensor("ramp_i", [P, NP], I32) as ramp_i, nc.Block() as block:

        @block.vector
        def _(dve):
            dve.sem_inc(s.norm.normed, 2)

        @block.gpsimd
        def _(pool):
            pool.memset(s.ident[:, :], 0.0).then_inc(filled, 1)
            pool.memset(s.before[:, :], 0.0).then_inc(filled, 1)
            pool.memset(s.mean_w[:, :], 1.0 / P).then_inc(filled, 1)
            pool.memset(s.ones[:, :], 1.0).then_inc(filled, 1)
            pool.memset(s.zeros_bf[:, :], 0.0).then_inc(filled, 1)
            pool.memset(s.eps[:, :], EPS).then_inc(filled, 1)
            pool.iota(ramp_i[:, :], pattern=[[1, NP]], base=0, channel_multiplier=0).then_inc(filled, 1)
            pool.iota(s.tile_i[:, :], pattern=[[P, TC]], base=0, channel_multiplier=1).then_inc(filled, 1)
            pool.iota(s.start_i[:, :], pattern=[[P, NB + 1]], base=0, channel_multiplier=0).then_inc(filled, 1)
            pool.wait_ge(filled, 9)
            pool.affine_select(out=s.ident[:, :], in_=s.ident[:, :], compare_op=ALU.not_equal, fill=1.0,
                               base=0, pattern=[[-1, P]], channel_multiplier=1).then_inc(made, 1)
            pool.affine_select(out=s.before[:, :], in_=s.before[:, :], compare_op=ALU.is_ge, fill=1.0,
                               base=0, pattern=[[-1, P]], channel_multiplier=1).then_inc(made, 1)
            pool.tensor_copy(s.ramp[:, :], ramp_i[:, :]).then_inc(made, 1)
            pool.tensor_copy(s.ramp16[:, :], ramp_i[:, :]).then_inc(made, 1)
            pool.tensor_copy(s.tile_no[:, :], s.tile_i[:, :]).then_inc(made, 1)
            pool.tensor_copy(s.start[:, :], s.start_i[:, :]).then_inc(made, 1)
            pool.wait_ge(made, 6)
            pool.tensor_tensor(out=s.centre[:, :], in0=s.ident[:, :], in1=s.mean_w[:, :], op=ALU.subtract).then_inc(made, 1)
            pool.wait_ge(made, 7)


def load_edges(nc, s):
    padded, loaded, cast = s.sem("edge_padded"), s.sem("edge_loaded"), s.sem("edge_cast")
    turned, copied, ranged = s.sem("edge_turned"), s.sem("edge_copied"), s.sem("edge_ranged")
    range_pe, indexed = s.sem("edge_range_pe"), s.sem("edge_indexed")
    with ExitStack() as ctx:
        nat_i = ctx.enter_context(nc.sbuf_tensor("nat_i", [P, 3, TC, P], I32))
        nat = ctx.enter_context(nc.sbuf_tensor("nat", [P, 5, TC, P], F32))
        span = ctx.enter_context(nc.sbuf_tensor("span", [P, 2, TC], F32))
        tile_m = ctx.enter_context(nc.sbuf_tensor("tile_m", [P, 2, TC], F32))
        hit = ctx.enter_context(nc.sbuf_tensor("hit", [P, 3, TC, NB], F32))
        edge_t = ctx.enter_context(nc.sbuf_tensor("edge_t", [NB, 8], F32))
        edge_i = ctx.enter_context(nc.sbuf_tensor("edge_i", [NB, 2], I32))
        tmp = ctx.enter_context(nc.sbuf_tensor("index_tmp", [P, NT], F32))
        block = ctx.enter_context(nc.Block())
        sources = [(nat_i[:, 0], s.d_src), (nat_i[:, 1], s.d_dst), (nat_i[:, 2], s.d_type),
                   (nat[:, 3], s.d_weight), (nat[:, 4], s.d_weight1)]
        whole = FULL_TILES // P
        rest = FULL_TILES - whole * P

        @block.gpsimd
        def _(pool):
            for (dest, _), pad in zip(sources, [PAD_NODE, PAD_NODE, 0, 0.0, 0.0]):
                pool.memset(dest[:, whole, :], pad).then_inc(padded, 1)

        @block.sync
        def _(sp):
            sp.wait_ge(padded, 5)
            for dest, dram in sources:
                sp.dma_start(dest[:, 0:whole, :],
                             dram[0:whole * P * P].rearrange("(c p j) -> p c j", c=whole, p=P)).then_inc(loaded, 16)
                sp.dma_start(dest[0:rest, whole, :],
                             dram[whole * P * P:FULL_TILES * P].rearrange("(p j) -> p j", j=P)).then_inc(loaded, 16)
                sp.dma_start(dest[rest:rest + 1, whole, 0:LAST],
                             dram[FULL_TILES * P:EDGES].rearrange("(p j) -> p j", p=1)).then_inc(loaded, 16)

        banks = [s.ps[:, n, :] for n in range(8)]

        @block.tensor
        def _(pe):
            pe.wait_ge(cast, 3)
            for n in range(5):
                if n >= 3:
                    pe.wait_ge(copied, 2 * (n - 2))
                for c in range(TC):
                    nc.tensor.transpose(banks[2 * (n % 3) + c // 4][:, (c % 4) * P:(c % 4 + 1) * P],
                                        nat[:, n, c, :], s.ident[:, :]).then_inc(turned, 1)
            pe.wait_ge(ranged, 2 + 4 * TC + 2)
            pe.wait_ge(copied, 10)
            for v in range(2):
                for c in range(TC):
                    nc.tensor.transpose(banks[2 * v + c // 4][0:NB, (c % 4) * P:(c % 4 + 1) * P],
                                        hit[:, 1 + v, c, :], s.ident[:, :]).then_inc(range_pe, 1)
            pe.wait_ge(indexed, 7)
            nc.tensor.matmul(banks[4][0:1, 0:NB], edge_t[:, 4:5], s.ident[0:NB, 0:NB], start=True, stop=True).then_inc(range_pe, 1)
            nc.tensor.matmul(banks[5][0:1, 0:NB], edge_t[:, 5:6], s.ident[0:NB, 0:NB], start=True, stop=True).then_inc(range_pe, 1)
            nc.tensor.matmul(banks[6][0:1, 0:NB], edge_t[:, 5:6], s.before[0:NB, 0:NB], start=True, stop=True).then_inc(range_pe, 1)

        @block.vector
        def _(dve):
            dve.wait_ge(loaded, 16 * 15)
            for n in range(3):
                nc.vector.tensor_copy(nat[:, n], nat_i[:, n]).then_inc(cast, 1)
            dve.wait_ge(cast, 3)
            nc.vector.tensor_reduce(out=span[:, 0, :], in_=nat[:, 1], axis=AX.X, op=ALU.min).then_inc(ranged, 1)
            nc.vector.tensor_reduce(out=span[:, 1, :], in_=nat[:, 1], axis=AX.X, op=ALU.max).then_inc(ranged, 1)
            nc.vector.tensor_scalar(tile_m[:, 0, :], s.tile_no[:, :], -BIG, None, ALU.add).then_inc(ranged, 1)
            nc.vector.tensor_scalar(tile_m[:, 1, :], s.tile_no[:, :], 1.0, None, ALU.add).then_inc(ranged, 1)
            dve.wait_ge(ranged, 4)
            for c in range(TC):
                nc.vector.tensor_scalar(hit[:, 0, c, :], s.start[:, 0:NB], span[:, 1, c:c + 1], None, ALU.is_le).then_inc(ranged, 1)
                dve.wait_ge(ranged, 4 + 4 * c + 1)
                nc.vector.scalar_tensor_tensor(out=hit[:, 0, c, :], in0=s.start[:, 1:NB + 1], scalar=span[:, 0, c:c + 1],
                                               in1=hit[:, 0, c, :], op0=ALU.is_gt, op1=ALU.mult).then_inc(ranged, 1)
                dve.wait_ge(ranged, 4 + 4 * c + 2)
                nc.vector.tensor_scalar(hit[:, 1, c, :], hit[:, 0, c, :], tile_m[:, 0, c:c + 1], BIG, ALU.mult, ALU.add).then_inc(ranged, 1)
                nc.vector.tensor_scalar(hit[:, 2, c, :], hit[:, 0, c, :], tile_m[:, 1, c:c + 1], None, ALU.mult).then_inc(ranged, 1)
            for n, column in enumerate([s.src, s.dst, s.typ, s.weight, s.weight1]):
                for h, (lo, hi) in enumerate([(0, 4), (4, TC)]):
                    dve.wait_ge(turned, TC * n + hi)
                    nc.vector.tensor_copy(column[:, lo * P:hi * P], banks[2 * (n % 3) + h][:, 0:(hi - lo) * P]).then_inc(copied, 1)
            dve.wait_ge(range_pe, 2 * TC)
            for v, op in enumerate([ALU.min, ALU.max]):
                nc.vector.tensor_reduce(out=edge_t[:, 2 * v:2 * v + 1], in_=banks[2 * v][0:NB, 0:4 * P], axis=AX.X, op=op).then_inc(indexed, 1)
                nc.vector.tensor_reduce(out=edge_t[:, 2 * v + 1:2 * v + 2], in_=banks[2 * v + 1][0:NB, 0:(TC - 4) * P], axis=AX.X, op=op).then_inc(indexed, 1)
            dve.wait_ge(indexed, 4)
            nc.vector.tensor_tensor(edge_t[:, 4:5], edge_t[:, 0:1], edge_t[:, 1:2], ALU.min).then_inc(indexed, 1)
            nc.vector.tensor_tensor(edge_t[:, 6:7], edge_t[:, 2:3], edge_t[:, 3:4], ALU.max).then_inc(indexed, 1)
            dve.wait_ge(indexed, 6)
            s.groups_of(nc, dve, edge_t, edge_i, 4, 6, 5, s.sem("edge_groups"), indexed)
            dve.wait_ge(range_pe, 2 * TC + 3)
            for r in range(3):
                nc.vector.tensor_copy(s.dst_range[0:1, r, :], banks[4 + r][0:1, 0:NB]).then_inc(ranged, 1)
            dve.wait_ge(copied, 10)
            nc.vector.tensor_scalar(s.src_row[:, :], s.src[:, 0:NT], float(NODES - 1), None, ALU.min).then_inc(ranged, 1)
            nc.vector.tensor_scalar(s.dst_row[:, :], s.dst[:, 0:NT], float(NODES - 1), None, ALU.min).then_inc(ranged, 1)
            nc.vector.tensor_scalar(tmp[:, :], s.src[:, 0:NT], float(NODES - 1), None, ALU.min).then_inc(indexed, 1)
            dve.wait_ge(indexed, 8)
            nc.vector.scalar_tensor_tensor(out=s.typed_row[:, :], in0=s.typ[:, 0:NT], scalar=float(NP), in1=tmp[:, :],
                                           op0=ALU.mult, op1=ALU.add).then_inc(ranged, 1)


def groups_of(nc, dve, t, ti, lo, hi, out, chain, done):
    nc.vector.tensor_scalar(t[:, lo:lo + 1], t[:, lo:lo + 1], float(NT - 2 * TG), None, ALU.min).then_inc(chain, 1)
    dve.wait_ge(chain, 1)
    nc.vector.tensor_tensor(t[:, hi:hi + 1], t[:, hi:hi + 1], t[:, lo:lo + 1], ALU.subtract).then_inc(chain, 1)
    dve.wait_ge(chain, 2)
    nc.vector.tensor_scalar(ti[:, 0:1], t[:, hi:hi + 1], float(TG - 1), float(2 * TG), ALU.add, ALU.max).then_inc(chain, 1)
    dve.wait_ge(chain, 3)
    nc.vector.tensor_scalar(ti[:, 1:2], ti[:, 0:1], TG.bit_length() - 1, None, ALU.arith_shift_right).then_inc(chain, 1)
    dve.wait_ge(chain, 4)
    nc.vector.tensor_copy(t[:, out:out + 1], ti[:, 1:2]).then_inc(done, 1)


def load_nodes(nc, s):
    loaded, turned, copied, padded = s.sem("node_loaded"), s.sem("node_turned"), s.sem("node_copied"), s.sem("node_padded")
    with ExitStack() as ctx:
        xn = ctx.enter_context(nc.sbuf_tensor("x_nodes", [P, NB, P], F32))
        zeroed, zero_rows = s.sem("node_zeroed"), s.sem("node_zero_rows")
        zeros = ctx.enter_context(nc.sbuf_tensor("zero_rows", [P, NT - -(-TILES // (2 * GT)) * 2 * GT, P], F32))
        nw = 2 + LAYERS1 * (TYPES + 6)
        wn = ctx.enter_context(nc.sbuf_tensor("w_rows", [P, nw, P], F32))
        block = ctx.enter_context(nc.Block())

        @block.gpsimd
        def _(pool):
            pool.memset(xn[:, NB - 1, :], 0.0).then_inc(padded, 1)
            pool.memset(zeros[:, :, :], 0.0).then_inc(zeroed, 1)

        @block.scalar
        def _(act):
            act.dma_start(wn[:, 0, :], s.d_proj_w).then_inc(loaded, 16)
            act.dma_start(wn[:, 1, :], s.d_out_w).then_inc(loaded, 16)
            for l in range(LAYERS1):
                o = 2 + l * (TYPES + 6)
                act.dma_start(wn[:, o:o + TYPES, :], s.d_edge_W[l].rearrange("t d h -> d t h")).then_inc(loaded, 16)
                act.dma_start(wn[:, o + TYPES:o + TYPES + 3, :], s.d_wih[l].rearrange("(g d) h -> d g h", d=P)).then_inc(loaded, 16)
                act.dma_start(wn[:, o + TYPES + 3:o + TYPES + 6, :], s.d_whh[l].rearrange("(g d) h -> d g h", d=P)).then_inc(loaded, 16)
            for column, dram in s.bias_loads:
                act.dma_start(column, dram).then_inc(loaded, 16)
            act.dma_start(s.W0[:, :], s.d_W0).then_inc(loaded, 16)
            act.dma_start(s.Wn[:, :], s.d_Wn).then_inc(loaded, 16)
            act.dma_start(s.Wout[:, :], s.d_Wout).then_inc(loaded, 16)

        @block.sync
        def _(sp):
            sp.wait_ge(padded, 1)
            sp.dma_start(xn[:, 0:NB - 1, :], s.d_x[0:(NB - 1) * P, :].rearrange("(b p) f -> p b f", p=P)).then_inc(loaded, 16)
            sp.dma_start(xn[0:NODES - (NB - 1) * P, NB - 1, :], s.d_x[(NB - 1) * P:NODES, :]).then_inc(loaded, 16)
            sp.wait_ge(zeroed, 1)
            gathered = -(-TILES // (2 * GT)) * 2 * GT
            sp.dma_start(s.edge_rows[gathered * P:NT * P, :].rearrange("(t p) f -> p t f", p=P), zeros[:, :, :]).then_inc(zero_rows, 16)
            sp.wait_ge(zero_rows, 16)

        count = 16 * (2 + 2 + 3 * LAYERS1 + len(s.bias_loads) + 3)
        todo = [(xn[:, b, :], s.xT[:, b * P:(b + 1) * P]) for b in range(NB)]
        todo += [(wn[:, n, :], s.wT[:, n, :]) for n in range(nw)]

        @block.tensor
        def _(pe):
            pe.wait_ge(loaded, count)
            for k, (source, _) in enumerate(todo):
                if k >= 8:
                    pe.wait_ge(copied, k - 7)
                nc.tensor.transpose(s.ps[:, k % 8, 0:P], source, s.ident[:, :]).then_inc(turned, 1)

        @block.vector
        def _(dve):
            for k, (_, dest) in enumerate(todo):
                dve.wait_ge(turned, k + 1)
                nc.vector.tensor_copy(dest, s.ps[:, k % 8, 0:P]).then_inc(copied, 1)
            dve.wait_ge(loaded, count)
            nc.vector.tensor_tensor(s.b_rz[:, :, :], s.bih[:, :, 0:2], s.bhh[:, :, 0:2], ALU.add).then_inc(padded, 1)


def edge_pass(nc, s, name, table, rows, ranges, weighted=False, columns=None, We=None, beside=None):
    records = We is not None
    copied, granted = s.sem(name + "_index_copied"), s.sem(name + "_granted")
    gathered = [s.sem(f"{name}_gathered{h}") for h in range(2)]
    row_free = [s.sem(f"{name}_row_free{h}") for h in range(2)]
    stored = [s.sem(f"{name}_stored{h}") for h in range(2)]
    copies = columns is not None and not weighted
    narrowed = [s.sem(f"{name}_narrowed{h}") for h in range(PARTS)]
    rec_back = [s.sem(f"{name}_rec_back{h}") for h in range(PARTS)]
    record_back = [s.sem(f"{name}_record_back{h}") for h in range(2)]
    back = [s.sem(f"{name}_back{h}") for h in range(PARTS)]
    picked = [s.sem(f"{name}_picked{h}") for h in range(PARTS)]
    used = [s.sem(f"{name}_used{h}") for h in range(PARTS)]
    turned = [s.sem(f"{name}_turned{h}") for h in range(PARTS)]
    turned_read = [s.sem(f"{name}_turned_read{h}") for h in range(PARTS)]
    filtered = [s.sem(f"{name}_filtered{h}") for h in range(PARTS)]
    summed, sum_read, cleared = s.sem(name + "_summed"), s.sem(name + "_sum_read"), s.sem(name + "_cleared")
    count_read, count_stored = s.sem(name + "_count_read"), s.sem(name + "_count_stored")
    turns = -(-TILES // (2 * GT))
    with ExitStack() as ctx:
        def sb(key, count, shape, dt=F32):
            return [ctx.enter_context(nc.sbuf_tensor(f"{name}_{key}{h}", shape, dt)) for h in range(count)]
        index, fetched = sb("index", 2, [P, GT], I32), sb("fetched", 2, [P, GT, P])
        feat, pick = sb("feat", PARTS, [P, PT, P]), sb("pick", PARTS, [P, PT, P])
        edge_rows = s.edge_rows[:, :].rearrange("(t p) f -> p t f", p=P)
        record_rows = s.records[:, :].rearrange("(t p) f -> p t f", p=P)
        if records:
            msg, side = sb("msg", PARTS, [P, PT, P]), sb("side", PARTS, [P, PT, 2])
            index_rec, rec, efT = sb("index_rec", 2, [P, GT, REC]), sb("rec", PARTS, [P, PT, P // PT]), sb("efT", PARTS, [P, P])
        if columns:
            lo, hi = columns
            width = hi - lo
            cuts = [(c, min(-(-width // 3), width - c)) for c in range(0, width, -(-width // 3))]
            pick_d, pick_s = sb("pick_d", PARTS, [P, PT, P], BF16), sb("pick_s", PARTS, [P, PT, width], BF16)
            count_row = sb("count_row", 1, [P, width])[0]
        if beside:
            beside.open(nc, s, ctx)
        block = ctx.enter_context(nc.Block())
        ps = s.ps[:, :, :].rearrange("p b n -> p (b n)")

        def agg(b):
            return ps[:, ds((b & 1) * 512 + 6 * 512, P)]

        def pairs(b, bank, n):
            return ps[:, ds((b & 1) * (3 * 512) + bank * 512, n)]

        @block.gpsimd
        def _(pool):
            with pool.Fori(0, turns) as i:
                for h in range(2):
                    pool.wait_ge(row_free[h], i + 1)
                    if records:
                        pool.wait_ge(record_back[h], i * 16 + 16)
                        pool.sem_inc(granted, 1)
                        source = index_rec[h][:, :, EF + 2:EF + 3].rearrange("p t o -> p (t o)")
                    else:
                        source = rows[:, ds(i * (2 * GT) + GT * h, GT)]
                    nc.gpsimd.tensor_copy(index[h][:, :], source).then_inc(copied, 1)
                    pool.wait_ge(copied, i * 2 + h + 1)
                    pool.sem_inc(granted, 1)
                    for j in range(GT):
                        nc.gpsimd.indirect_dma_start(out=fetched[h][:, j, :], out_offset=None, in_=table,
                                                     in_offset=bass.IndirectOffsetOnAxis(ap=index[h][:, j:j + 1], axis=0)
                                                     ).then_inc(gathered[h], 16)

        @block.sync
        def _(sp):
            def load_index(i, h):
                sp.dma_start(index_rec[h][:, :, :], record_rows[:, ds(i * (2 * GT) + GT * h, GT), :]).then_inc(record_back[h], 16)

            def turn(i, last):
                for h in range(2):
                    sp.wait_ge(gathered[h], i * (16 * GT) + 16 * GT)
                    sp.dma_start(edge_rows[:, ds(i * (2 * GT) + GT * h, GT), :], fetched[h][:, :, :]).then_inc(stored[h], 16)
                    if records and not last:
                        load_index(i + 1, h)
                    sp.wait_ge(stored[h], i * 16 + 16)
                    sp.sem_inc(row_free[h], 1)

            for h in range(2):
                sp.sem_inc(row_free[h], 1)
                if records:
                    load_index(0, h)
            with sp.Fori(0, turns - 1) as i:
                turn(i, False)
            turn(turns - 1, True)
            for h in range(2):
                sp.sem_inc(stored[h], 16 * (NT // (2 * GT) - turns))

        @block.scalar
        def _(act):
            def load_block(b):
                first = act.value_load(ranges[0:1, 0, ds(b, 1)], min_val=0, max_val=NT - 2 * TG)
                groups = act.value_load(ranges[0:1, 1, ds(b, 1)], min_val=2, max_val=NT // TG)
                before = act.value_load(ranges[0:1, 2, ds(b, 1)], min_val=0, max_val=NB * NT // TG)
                with act.Fori(0, groups) as i:
                    for h in range(PARTS):
                        tile = bounded(first + i * TG + PT * h, NT - PT)
                        turn = ((tile + (PT - 1)) >> (2 * GT).bit_length() - 1) + 1
                        if records:
                            act.wait_ge(turned_read[h], before + i + 1)
                            act.sem_inc(granted, 1)
                            act.dma_start(rec[h][:, :, 0:REC], record_rows[:, ds(tile, PT), :]).then_inc(rec_back[h], 16)
                        act.wait_ge((picked if records else used)[h], before + i + 1)
                        act.wait_ge(stored[0], turn * 16)
                        act.wait_ge(stored[1], turn * 16)
                        act.dma_start(feat[h][:, :, :], edge_rows[:, ds(tile, PT), :]).then_inc(back[h], 16)
                        if copies:
                            act.wait_ge(picked[h], before + i + 1)
                            nc.scalar.activation(pick_d[h][:, :, :], pick[h][:, :, :], ACT.Copy).then_inc(narrowed[h], 1)

            def store_counts(b):
                act.wait_ge(count_read, b + 3)
                act.sem_inc(granted, 1)
                act.dma_start(s.counts[ds(b, 1), :, lo:hi].rearrange("o p n -> (o p) n"), count_row[:, :]).then_inc(count_stored, 16)

            if records:
                act.wait_ge(cleared, PARTS)
            load_block(0)
            with act.Fori(1, NB) as b:
                load_block(b)
                if columns:
                    store_counts(b - 1)
            if columns:
                store_counts(NB - 1)
                act.wait_ge(count_stored, 16 * NB + 16)

        @block.vector
        def _(dve):
            def picks(h, tile, n, here):
                for j in range(PT):
                    if records:
                        last = nc.vector.tensor_scalar(pick[h][:, j, :], here, side[h][:, j, 1:2], None, ALU.is_equal)
                        continue
                    at = ds(bounded(tile + j, NT - 1), 1)
                    if columns:
                        nc.vector.tensor_scalar(pick_s[h][:, j, :], s.ramp16[:, lo:hi], s.src[:, at], None, ALU.is_equal)
                    if columns and not copies:
                        nc.vector.tensor_scalar(pick_d[h][:, j, :], here, s.dst[:, at], None, ALU.is_equal)
                    if weighted:
                        last = nc.vector.tensor_scalar(pick[h][:, j, :], here, s.dst[:, at], s.weight[:, at], ALU.is_equal, ALU.mult)
                    else:
                        last = nc.vector.tensor_scalar(pick[h][:, j, :], here, s.dst[:, at], None, ALU.is_equal)
                return last

            def group(b, n, first):
                here = s.ramp[:, ds(b * P, P)]
                for h in range(PARTS):
                    if records and h < 2:
                        for k in (2 * h, 2 * h + 1):
                            dve.wait_ge(turned[k], n + 1)
                            dve.wait_ge(filtered[k], n + 1)
                            nc.vector.tensor_copy(side[k][:, :, :], rec[k][:, :, EF:EF + 2])
                            nc.vector.tensor_copy(efT[k][:, :], s.ps[:, k % 2, 0:P]).then_inc(turned_read[k], 1)
                    dve.wait_ge(used[h], n + 1)
                    if records:
                        dve.wait_ge(filtered[h], n + 2)
                        dve.wait_ge(turned_read[h], n + 2)
                        dve.wait_ge(back[h], n * 16 + 16)
                        for j in range(PT):
                            nc.vector.scalar_tensor_tensor(out=msg[h][:, j, :], in0=s.ps[:, 2 + h, j * P:(j + 1) * P],
                                                           scalar=side[h][:, j, 0:1], in1=feat[h][:, j, :], op0=ALU.mult, op1=ALU.mult)
                    picks(h, first + PT * h, n, here).then_inc(picked[h], 1)

            def read_sums(b):
                dve.wait_ge(summed, b + 1)
                nc.vector.tensor_copy(s.aggT[:, ds(b * P, P)], agg(b)).then_inc(sum_read, 1)
                if columns:
                    dve.wait_ge(count_stored, b * 16 + 16)
                    for k, (c, n) in enumerate(cuts):
                        last = nc.vector.tensor_copy(count_row[:, c:c + n], pairs(b, k, n))
                    last.then_inc(count_read, 1)

            def node_block(b, sums=True):
                first = dve.value_load(ranges[0:1, 0, ds(b, 1)], min_val=0, max_val=NT - 2 * TG)
                groups = dve.value_load(ranges[0:1, 1, ds(b, 1)], min_val=2, max_val=NT // TG)
                before = dve.value_load(ranges[0:1, 2, ds(b, 1)], min_val=0, max_val=NB * NT // TG)
                group(b, before, first)
                if sums:
                    read_sums(b - 1)
                with dve.Fori(1, groups) as i:
                    group(b, before + i, first + i * TG)

            if records:
                for h in range(PARTS):
                    nc.vector.memset(rec[h][:, :, :], 0.0).then_inc(cleared, 1)
            if beside:
                beside.dve(nc, dve, s)
            node_block(0, False)
            with dve.Fori(1, NB) as b:
                node_block(b)
            read_sums(NB - 1)

        @block.tensor
        def _(pe):
            if beside:
                beside.pe(nc, pe, s)
            for h in range(PARTS):
                pe.sem_inc(used[h], 1)
                if records:
                    for sem in (turned_read[h], filtered[h], picked[h]):
                        pe.sem_inc(sem, 1)
            pe.sem_inc(sum_read, 2)
            pe.sem_inc(count_read, 2)
            pe.sem_inc(count_stored, 16)

            def turn_features(b, n, h):
                pe.wait_ge(rec_back[h], n * 16 + 16)
                pe.wait_ge(turned_read[(h + 2) % PARTS], n + 1 + h // 2)
                nc.tensor.transpose(s.ps[:, h % 2, 0:P], rec[h][:, :, :].rearrange("p t k -> p (t k)"), s.ident[:, :]).then_inc(turned[h], 1)

            def filter_part(b, n, h):
                pe.wait_ge(turned_read[h], n + 2)
                pe.wait_ge(picked[h], n + 1)
                nc.tensor.matmul(s.ps[:, 2 + h, 0:PT * P], efT[h][:, :], We, start=True, stop=True).then_inc(filtered[h], 1)

            def collect_part(b, n, h):
                pe.wait_ge(picked[h], n + (2 if records else 1))
                if copies:
                    pe.wait_ge(narrowed[h], n + 1)
                if columns:
                    for j in range(PT):
                        for k, (c, m) in enumerate(cuts):
                            nc.tensor.matmul(pairs(b, k, m), pick_d[h][:, j, :], pick_s[h][:, j, c:c + m], start=False, stop=False)
                if not records:
                    pe.wait_ge(back[h], n * 16 + 16)
                for j in range(PT):
                    last = nc.tensor.matmul(agg(b), (msg if records else feat)[h][:, j, :], pick[h][:, j, :], start=False, stop=False)
                last.then_inc(used[h], 1)

            with pe.Fori(0, NB) as b:
                groups = pe.value_load(ranges[0:1, 1, ds(b, 1)], min_val=2, max_val=NT // TG)
                before = pe.value_load(ranges[0:1, 2, ds(b, 1)], min_val=0, max_val=NB * NT // TG)
                pe.wait_ge(sum_read, b + 1)
                nc.tensor.matmul(agg(b), s.zeros_bf[:, 0:P], s.zeros_bf[:, 0:P], start=True, stop=False)
                if columns:
                    pe.wait_ge(count_read, b + 1)
                    for k, (c, m) in enumerate(cuts):
                        nc.tensor.matmul(pairs(b, k, m), s.zeros_bf[:, 0:P], s.zeros_bf[:, 0:m], start=True, stop=False)
                with pe.Fori(0, groups) as i:
                    n = before + i
                    if records:
                        for step, parts in ((turn_features, (0, 1)), (filter_part, (0, 1)), (turn_features, (2, 3)), (collect_part, (0,)),
                                            (filter_part, (2, 3)), (collect_part, (1, 2, 3))):
                            for h in parts:
                                step(b, n, h)
                    else:
                        for h in range(PARTS):
                            collect_part(b, n, h)
                if columns:
                    for k, (c, m) in enumerate(cuts):
                        nc.tensor.matmul(pairs(b, k, m), s.zeros_bf[:, 0:P], s.zeros_bf[:, 0:m], start=False, stop=True)
                nc.tensor.matmul(agg(b), s.zeros_bf[:, 0:P], s.zeros_bf[:, 0:P], start=False, stop=True).then_inc(summed, 1)


class Norm:

    def __init__(self, s):
        self.given, self.centred, self.squared = s.sem("norm_given"), s.sem("norm_centred"), s.sem("norm_squared")
        self.var_ready, self.log_ready, self.rstd_ready = s.sem("norm_var"), s.sem("norm_log"), s.sem("norm_rstd")
        self.scaled, self.normed = s.sem("norm_scaled"), s.sem("norm_done")
        self.turns = 0
        self.gained = 0

    def pe(self, nc, pe, s, t):
        for h in range(2):
            pe.wait_ge(self.given, 2 * t + (h + 1))
            nc.tensor.matmul(s.ps[:, h, 0:HALF], s.centre[:, :], s.y[:, h, :], start=True, stop=True).then_inc(self.centred, 1)
        for h in range(2):
            pe.wait_ge(self.squared, 2 * t + (h + 1))
            nc.tensor.matmul(s.ps[:, 2 + h, 0:HALF], s.mean_w[:, :], s.sq[:, h, :], start=True, stop=True).then_inc(self.var_ready, 1)

    def act(self, nc, act, s, t):
        for h in range(2):
            act.wait_ge(self.centred, 2 * t + (h + 1))
            nc.scalar.activation(s.sq[:, h, :], s.ps[:, h, 0:HALF], ACT.Square).then_inc(self.squared, 1)
        for h in range(2):
            act.wait_ge(self.var_ready, 2 * t + (h + 1))
            nc.scalar.activation(s.rstd[:, h, :], s.ps[:, 2 + h, 0:HALF], ACT.Ln, bias=s.eps[:, 0:1]).then_inc(self.log_ready, 1)
        for h in range(2):
            act.wait_ge(self.log_ready, 2 * t + (h + 1))
            nc.scalar.activation(s.rstd[:, h, :], s.rstd[:, h, :], ACT.Exp, scale=-0.5).then_inc(self.rstd_ready, 1)

    def dve(self, nc, dve, s, t, out, gain=None, shift=None, gained=0):
        for h in range(2):
            dve.wait_ge(self.rstd_ready, 2 * t + (h + 1))
            if gain is None:
                nc.vector.tensor_tensor(out[:, h, :], s.ps[:, h, 0:HALF], s.rstd[:, h, :], ALU.mult).then_inc(self.normed, 1)
            else:
                nc.vector.scalar_tensor_tensor(out=s.yc[:, h, :], in0=s.ps[:, h, 0:HALF], scalar=gain, in1=s.rstd[:, h, :],
                                               op0=ALU.mult, op1=ALU.mult).then_inc(self.scaled, 1)
        for h in range(2):
            if gain is not None:
                dve.wait_ge(self.scaled, 2 * gained + (h + 1))
                nc.vector.tensor_scalar(out[:, h, :], s.yc[:, h, :], shift, None, ALU.add).then_inc(self.normed, 1)


def node_phase(nc, s, name, weight, source, func, bias, base, gain=None, shift=None, second=None, layer=0):
    key = "node_" + name
    lin, applied, lin2, applied2 = s.sem(key + "_lin"), s.sem(key + "_applied"), s.sem(key + "_lin2"), s.sem(key + "_applied2")
    n = s.norm
    start = n.turns + layer * NCH
    with nc.Block() as block:

        @block.tensor
        def _(pe):
            with pe.Fori(0, NCH) as c:
                for h in range(2):
                    pe.wait_ge(n.normed, 2 * (start + c) + (h + 1))
                    nc.tensor.matmul(s.ps[:, 4 + h, 0:HALF], weight, source[:, ds(c * CH + h * HALF, HALF)], start=True, stop=True).then_inc(lin, 1)
                n.pe(nc, pe, s, start + c)
                if second:
                    for h in range(2):
                        pe.wait_ge(n.normed, 2 * (start + c) + (h + 3))
                        pe.wait_ge(applied2, 2 * c + (h + 1))
                        nc.tensor.matmul(s.ps[:, 6 + h, 0:HALF], second[0], base[:, ds(c * CH + h * HALF, HALF)], start=True, stop=True).then_inc(lin2, 1)

        @block.scalar
        def _(act):
            if second:
                act.sem_inc(applied2, 2)
            with act.Fori(0, NCH) as c:
                if func != ACT.Identity:
                    for h in range(2):
                        act.wait_ge(lin, 2 * (layer * NCH + c) + (h + 1))
                        nc.scalar.activation(s.y[:, h, :], s.ps[:, 4 + h, 0:HALF], func, bias=bias).then_inc(applied, 1)
                n.act(nc, act, s, start + c)
                if second:
                    for h in range(2):
                        act.wait_ge(lin2, 2 * c + (h + 1))
                        nc.scalar.activation(second[3][:, ds(c * CH + h * HALF, HALF)], s.ps[:, 6 + h, 0:HALF], second[1], bias=second[2]).then_inc(applied2, 1)

        @block.vector
        def _(dve):
            with dve.Fori(0, NCH) as c:
                for h in range(2):
                    here = base[:, ds(c * CH + h * HALF, HALF)]
                    if func != ACT.Identity:
                        dve.wait_ge(applied, 2 * (layer * NCH + c) + (h + 1))
                        nc.vector.tensor_tensor(s.y[:, h, :], s.y[:, h, :], here, ALU.add).then_inc(n.given, 1)
                    else:
                        dve.wait_ge(lin, 2 * (layer * NCH + c) + (h + 1))
                        nc.vector.scalar_tensor_tensor(out=s.y[:, h, :], in0=s.ps[:, 4 + h, 0:HALF], scalar=bias, in1=here,
                                                       op0=ALU.add, op1=ALU.add).then_inc(n.given, 1)
                n.dve(nc, dve, s, start + c, halves(base[:, ds(c * CH, CH)]), gain, shift, n.gained + layer * NCH + c)


def node_rows(nc, s, name, source, right, width, write):
    key = "rows_" + name
    held, made, read, row_free = (s.sem(f"{key}_{x}") for x in ("held", "made", "read", "free"))
    stored = [s.sem(f"{key}_stored{h}") for h in range(2)]
    ROWS = 4
    with ExitStack() as ctx:
        hold = [ctx.enter_context(nc.sbuf_tensor(f"{key}_hold{h}", [P, P], F32)) for h in range(2)]
        row = ctx.enter_context(nc.sbuf_tensor(key + "_row", [P, ROWS, width], F32))
        block = ctx.enter_context(nc.Block())
        banks = -(-width // 512)
        ps = s.ps[:, :, :].rearrange("p b n -> p (b n)")

        @block.vector
        def _(dve):
            def step(b, h, first=False):
                if not first:
                    dve.wait_ge(made, b - 1)
                nc.vector.tensor_copy(hold[h][:, :], source[:, ds(b * P, P)]).then_inc(held, 1)
            step(0, 0, True)
            step(1, 1, True)
            with dve.Fori(1, NB // 2) as p:
                for h in range(2):
                    step(p * 2 + h, h)
            step(NB - 1, 0)

        @block.tensor
        def _(pe):
            def step(b, h):
                pe.wait_ge(held, b + 1)
                pe.wait_ge(read, b + 1)
                for c in range(0, width, 512):
                    n = min(512, width - c)
                    last = nc.tensor.matmul(ps[:, h * 512 * banks + c:h * 512 * banks + c + n], hold[h][:, :],
                                            right[:, c:c + n], start=True, stop=True)
                last.then_inc(made, 1)
            with pe.Fori(0, NB // 2) as p:
                for h in range(2):
                    step(p * 2 + h, h)
            step(NB - 1, 0)

        @block.scalar
        def _(act):
            act.sem_inc(read, 2)
            with act.Fori(0, NB) as b:
                act.wait_ge(made, b + 1)
                act.wait_ge(row_free, b + 1)
                nc.scalar.activation(row[:, ds(b & (ROWS - 1), 1), :].rearrange("p o n -> p (o n)"), ps[:, ds((b & 1) * (512 * banks), width)], ACT.Copy).then_inc(read, 1)

        @block.sync
        def _(sp):
            sp.sem_inc(row_free, ROWS)

            def step(b, p, h, first=False):
                if not first:
                    sp.wait_ge(stored[h], p * 16)
                    sp.sem_inc(row_free, 1)
                sp.wait_ge(read, b + 3)
                write(sp, b, row[:, ds(b & (ROWS - 1), 1), :].rearrange("p o n -> p (o n)"), stored[h])
            step(0, 0, 0, True)
            step(1, 0, 1, True)
            with sp.Fori(1, NB // 2) as p:
                for h in range(2):
                    step(p * 2 + h, p, h)
            step(NB - 1, NB // 2, 0)
            for h in range(2):
                sp.wait_ge(stored[h], 16 * (NB - NB // 2 - h * (NB % 2)))


def gru(nc, s, l):
    key = f"gru{l}"
    gates, rz, hn, pre, tanh = (s.sem(f"{key}_{x}") for x in ("gates", "rz", "hn", "pre", "tanh"))
    diff, mixed, summed, done = (s.sem(f"{key}_{x}") for x in ("diff", "mixed", "summed", "done"))
    with ExitStack() as ctx:
        r, z, n, d = (ctx.enter_context(nc.sbuf_tensor(f"{key}_t{x}", [P, 2, HALF], F32)) for x in "rznd")
        block = ctx.enter_context(nc.Block())
        o = 2 + l * (TYPES + 6) + TYPES

        @block.tensor
        def _(pe):
            pe.sem_inc(pre, 2)
            with pe.Fori(0, NCH) as c:
                for h in range(2):
                    pe.wait_ge(pre, 2 * c + (h + 1))
                    at = ds(c * CH + h * HALF, HALF)
                    for g in range(2):
                        nc.tensor.matmul(s.ps[:, 2 * g + h, 0:HALF], s.wT[:, o + g, :], s.aggT[:, at], start=True, stop=False)
                        nc.tensor.matmul(s.ps[:, 2 * g + h, 0:HALF], s.wT[:, o + 3 + g, :], s.hT[:, at], start=False, stop=True)
                    nc.tensor.matmul(s.ps[:, 4 + h, 0:HALF], s.wT[:, o + 2, :], s.aggT[:, at], start=True, stop=True)
                    nc.tensor.matmul(s.ps[:, 6 + h, 0:HALF], s.wT[:, o + 5, :], s.hT[:, at], start=True, stop=True).then_inc(gates, 1)

        @block.scalar
        def _(act):
            act.sem_inc(mixed, 2)
            with act.Fori(0, NCH) as c:
                for h in range(2):
                    act.wait_ge(gates, 2 * c + (h + 1))
                    nc.scalar.activation(r[:, h, :], s.ps[:, h, 0:HALF], ACT.Sigmoid, bias=s.b_rz[:, l, 0:1]).then_inc(rz, 1)
                    act.wait_ge(mixed, 2 * c + (h + 1))
                    nc.scalar.activation(z[:, h, :], s.ps[:, 2 + h, 0:HALF], ACT.Sigmoid, bias=s.b_rz[:, l, 1:2]).then_inc(rz, 1)
                for h in range(2):
                    act.wait_ge(pre, 2 * c + (h + 3))
                    nc.scalar.activation(n[:, h, :], d[:, h, :], ACT.Tanh, bias=s.bih[:, l, 2:3]).then_inc(tanh, 1)

        @block.vector
        def _(dve):
            with dve.Fori(0, NCH) as c:
                old = halves(s.hT[:, ds(c * CH, CH)])
                for h in range(2):
                    dve.wait_ge(rz, 4 * c + (2 * h + 2))
                    nc.vector.scalar_tensor_tensor(out=r[:, h, :], in0=s.ps[:, 6 + h, 0:HALF], scalar=s.bhh[:, l, 2:3], in1=r[:, h, :],
                                                   op0=ALU.add, op1=ALU.mult).then_inc(hn, 1)
                    dve.wait_ge(hn, 2 * c + (h + 1))
                    nc.vector.tensor_tensor(d[:, h, :], r[:, h, :], s.ps[:, 4 + h, 0:HALF], ALU.add).then_inc(pre, 1)
                for h in range(2):
                    dve.wait_ge(tanh, 2 * c + (h + 1))
                    nc.vector.tensor_tensor(d[:, h, :], old[:, h, :], n[:, h, :], ALU.subtract).then_inc(diff, 1)
                for h in range(2):
                    dve.wait_ge(diff, 2 * c + (h + 1))
                    nc.vector.tensor_tensor(d[:, h, :], d[:, h, :], z[:, h, :], ALU.mult).then_inc(mixed, 1)
                for h in range(2):
                    dve.wait_ge(mixed, 2 * c + (h + 3))
                    nc.vector.tensor_tensor(d[:, h, :], d[:, h, :], n[:, h, :], ALU.add).then_inc(summed, 1)
                for h in range(2):
                    dve.wait_ge(summed, 2 * c + (h + 1))
                    nc.vector.tensor_scalar(old[:, h, :], d[:, h, :], 0.0, None, ALU.max).then_inc(done, 1)


def place_records(nc, pool, s, turn):
    r = s.placing
    if isinstance(turn, int):
        first = turn * RT
        whole = min(max(FULL_TILES - first, 0), RT)
        if whole < RT:
            pool.memset(r.record[:, :, :], 0.0).then_inc(r.cleared, 1)
            r.clears += 1
            pool.wait_ge(r.cleared, r.clears)
        if whole:
            pool.dma_start(r.record[:, 0:whole, 0:EF], r.features[:, first:first + whole, :]).then_inc(r.ef_back, 16)
            r.loads += 1
        if whole < RT and first + whole == FULL_TILES:
            pool.dma_start(r.record[0:LAST, whole, 0:EF], r.last_features).then_inc(r.ef_back, 16)
            r.loads += 1
        loads = r.loads * 16
    else:
        first = bounded(turn * RT, (LAYERS2 * PLACE_TURNS - 1) * RT)
        pool.dma_start(r.record[:, :, 0:EF], r.features[:, ds(first, RT), :]).then_inc(r.ef_back, 16)
        loads = turn * 16 + 16
    for n, column in enumerate((s.weight1, s.src, s.dst_row)):
        nc.gpsimd.tensor_copy(r.record[:, :, EF + n:EF + n + 1].rearrange("p t o -> p (t o)"), column[:, ds(first, RT)]).then_inc(r.copied, 1)
    nc.gpsimd.tensor_copy(r.place[:, :], s.place[:, ds(first, RT)]).then_inc(r.copied, 1)
    pool.wait_ge(r.copied, turn * 4 + 4)
    pool.sem_inc(r.passed, 1)
    pool.wait_ge(r.ef_back, loads)
    pool.sem_inc(r.passed, 1)
    for j in range(RT):
        nc.gpsimd.indirect_dma_start(out=s.records[:, :], out_offset=bass.IndirectOffsetOnAxis(ap=r.place[:, j:j + 1], axis=0),
                                     in_=r.record[:, j, :], in_offset=None).then_inc(r.scattered, 16)
    pool.wait_ge(r.scattered, turn * (16 * RT) + 16 * RT)
    pool.sem_inc(r.passed, 1)


def project(nc, s, a, l):
    loaded, cols, lin, moved = a.weights_loaded, a.columns, a.lin, a.moved
    held, made, read = a.held, a.made, a.read
    with nc.Block() as block:

        @block.sync
        def _(sp):
            for n, w in enumerate((a.WQ, a.WK, a.WV, a.WO)):
                sp.dma_start(a.w[:, n, :], w[ds(l, 1), :, :].rearrange("l i o -> (l i) o")).then_inc(loaded, 16)
            sp.dma_start(a.bv[:, :], a.bV[ds(l, 1), :]).then_inc(loaded, 16)

        @block.tensor
        def _(pe):
            pe.wait_ge(loaded, l * 80 + 80)
            pe.sem_inc(a.passed, 1)
            with pe.Fori(0, NCH) as c:
                for n in range(2):
                    pe.wait_ge(moved, (l * NCH + c) * 2 + (n + 1))
                    for h in range(2):
                        last = nc.tensor.matmul(s.ps[:, 2 * n + h, 0:HALF], a.w[:, n, :], s.hT[:, ds(c * CH + h * HALF, HALF)], start=True, stop=True)
                    last.then_inc(lin, 1)

            def value_rows(b, h):
                pe.wait_ge(held, l * NB + b + 1)
                pe.wait_ge(read, l * NB + b + 1)
                nc.tensor.matmul(s.ps[:, 4 + h, 0:P], a.hold[h][:, :], a.w[:, 2, :], start=True, stop=False)
                nc.tensor.matmul(s.ps[:, 4 + h, 0:P], s.ones[0:1, :], a.bv[0:1, :], start=False, stop=True).then_inc(made, 1)
            with pe.Fori(0, NB // 2) as p:
                for h in range(2):
                    value_rows(p * 2 + h, h)
            value_rows(NB - 1, 0)

        @block.scalar
        def _(act):
            act.wait_ge(cols, (l + 1) * 5)
            with act.Fori(0, NCH) as c:
                act.wait_ge(lin, (l * NCH + c) * 2 + 1)
                nc.scalar.activation(halves(a.qT[:, ds(c * CH, CH)]), s.ps[:, 0:2, 0:HALF], ACT.Identity, bias=a.col[:, 0:1]).then_inc(moved, 1)
                act.wait_ge(lin, (l * NCH + c) * 2 + 2)
                nc.scalar.activation(halves(a.kT[:, ds(c * CH, CH)]), s.ps[:, 2:4, 0:HALF], ACT.Identity, bias=a.col[:, 1:2], scale=SHRINK).then_inc(moved, 1)

            def value_rows(b, h):
                act.wait_ge(made, l * NB + b + 1)
                nc.scalar.activation(a.v[:, ds(b, 1), 0:P].rearrange("p o f -> p (o f)"), s.ps[:, 4 + h, 0:P], ACT.Copy).then_inc(read, 1)
            with act.Fori(0, NB // 2) as p:
                for h in range(2):
                    value_rows(p * 2 + h, h)
            value_rows(NB - 1, 0)

        @block.vector
        def _(dve):
            for n, (column, factor) in enumerate(((s.bQ, 1.0), (s.bK, SHRINK), (s.bO, 1.0), (s.ln_g, 1.0), (s.ln_b, 1.0))):
                nc.vector.tensor_scalar(a.col[:, n:n + 1], column[:, ds(l, 1)], factor, None, ALU.mult).then_inc(cols, 1)

            def hold(b, h, first=False):
                if not first:
                    dve.wait_ge(made, l * NB + b - 1)
                nc.vector.tensor_copy(a.hold[h][:, :], s.hT[:, ds(b * P, P)]).then_inc(held, 1)
            hold(0, 0, True)
            hold(1, 1, True)
            with dve.Fori(1, NB // 2) as p:
                for h in range(2):
                    hold(p * 2 + h, h)
            hold(NB - 1, 0)


def attend(nc, s, a, l):
    SC = NP // HALF
    GROUPS = -(-NB // 4)
    with nc.Block() as block:
        def k(b):
            return l * NB + b

        @block.sync
        def _(sp):
            with sp.Fori(0, NB) as b:
                sp.wait_ge(a.count_used, k(b) + 1)
                sp.sem_inc(a.passed, 1)
                sp.dma_start(a.cnt[:, ds(k(b) & 1, 1), :].rearrange("p o n -> p (o n)"),
                             s.counts[ds(b, 1), :, :].rearrange("o p n -> (o p) n")).then_inc(a.count_back, 16)
                sp.wait_ge(a.count_back, k(b) * 16 + 16)
                sp.sem_inc(a.passed, 1)

        @block.gpsimd
        def _(pool):
            with pool.Fori(0, PLACE_TURNS) as i:
                place_records(nc, pool, s, l * PLACE_TURNS + i)

        @block.tensor
        def _(pe):
            def scores(b):
                pe.wait_ge(a.q_held, k(b) + 1)
                for c in range(SC):
                    pe.wait_ge(a.masked, k(b) * SC + c + 1)
                    nc.tensor.matmul(s.ps[:, c % 4, 0:HALF], a.q[:, :], a.kT[:, c * HALF:(c + 1) * HALF], start=True, stop=True).then_inc(a.scored, 1)

            def turn_result(b):
                pe.wait_ge(a.msg_read, k(b) + 2)
                pe.wait_ge(a.att_read, k(b) + 1)
                nc.tensor.transpose(s.ps[:, 7, 0:P], a.msg[:, :], s.ident[:, :]).then_inc(a.msg_turned, 1)

            def values(b):
                def turn_group(g):
                    pe.wait_ge(a.weighed, k(b) * SC + min(-(-4 * P * (g + 1) // HALF), SC))
                    pe.wait_ge(a.pt_read, k(b) * GROUPS + g + 1)
                    for n in range(4 * g, min(4 * g + 4, NB)):
                        last = nc.tensor.transpose(s.ps[:, 4 + g % 2, (n % 4) * P:(n % 4 + 1) * P], a.pm[:, n * P:(n + 1) * P], s.ident[:, :])
                    last.then_inc(a.turned, 1)

                def add_group(g):
                    pe.wait_ge(a.pt_read, k(b) * GROUPS + g + 3)
                    for n in range(4 * g, min(4 * g + 4, NB)):
                        last = nc.tensor.matmul(s.ps[:, 6, 0:P + 1], a.pt[:, n * P:(n + 1) * P], a.v[:, n, 0:P + 1], start=n == 0, stop=n == NB - 1)
                    return last

                turn_group(0)
                turn_group(1)
                pe.wait_ge(a.msg_read, k(b) + 1)
                for g in range(GROUPS):
                    last = add_group(g)
                    if g + 2 < GROUPS:
                        turn_group(g + 2)
                last.then_inc(a.summed, 1)

            scores(0)
            scores(1)
            values(0)
            with pe.Fori(2, NB) as b:
                scores(b)
                turn_result(b - 2)
                values(b - 1)
            turn_result(NB - 2)
            values(NB - 1)
            turn_result(NB - 1)

        @block.scalar
        def _(act):
            def exps(b):
                act.wait_ge(a.biased, k(b) + 1)
                for h in range(2):
                    at = ds((k(b) & 1) * NP + h * (NP // 2), NP // 2)
                    nc.scalar.activation(a.t[:, at], a.t[:, at], ACT.Exp, bias=a.bias[:, 0:1], scale=-SCALE / SHRINK).then_inc(a.exped, 1)

            def copy_result(b):
                act.wait_ge(a.msg_turned, k(b) + 1)
                nc.scalar.activation(s.aggT[:, ds(b * P, P)], s.ps[:, 7, 0:P], ACT.Copy).then_inc(a.att_read, 1)

            def copy_groups(b):
                act.wait_ge(a.summed, k(b) + 1)
                for g in range(GROUPS):
                    n = min(4 * g + 4, NB) - 4 * g
                    act.wait_ge(a.turned, k(b) * GROUPS + g + 2)
                    nc.scalar.activation(a.pt[:, 4 * g * P:(4 * g + n) * P], s.ps[:, 4 + g % 2, 0:n * P], ACT.Copy).then_inc(a.pt_read, 1)

            exps(0)
            copy_groups(0)
            exps(1)
            with act.Fori(2, NB) as b:
                copy_result(b - 2)
                copy_groups(b - 1)
                exps(b)
            copy_result(NB - 2)
            copy_groups(NB - 1)
            copy_result(NB - 1)

        @block.vector
        def _(dve):
            def hold_q(b):
                if isinstance(b, int) and b == 0:
                    pass
                else:
                    dve.wait_ge(a.scored, k(b) * SC)
                nc.vector.tensor_copy(a.q[:, :], a.qT[:, ds(b * P, P)]).then_inc(a.q_held, 1)

            def chunk(b, c, mark, weigh):
                here = k(b) & 1
                if mark:
                    if c == 0:
                        dve.wait_ge(a.count_back, k(b) * 16 + 16)
                    dve.wait_ge(a.scored, k(b) * SC + c + 1)
                    nc.vector.scalar_tensor_tensor(out=a.t[:, ds(here * NP + c * HALF, HALF)],
                                                   in0=a.cnt[:, ds(here, 1), c * HALF:(c + 1) * HALF].rearrange("p o n -> p (o n)"),
                                                   scalar=0.5, in1=s.ps[:, c % 4, 0:HALF], op0=ALU.is_lt, op1=ALU.subtract).then_inc(a.masked, 1)
                if weigh:
                    w = b - 1
                    there = k(w) & 1
                    if c == 0:
                        dve.wait_ge(a.turned, k(w) * GROUPS + 1)
                    if c % (SC // 2) == 0:
                        dve.wait_ge(a.exped, k(w) * 2 + c // (SC // 2) + 1)
                    ins = nc.vector.tensor_tensor(a.pm[:, c * HALF:(c + 1) * HALF], a.t[:, ds(there * NP + c * HALF, HALF)],
                                                  a.cnt[:, ds(there, 1), c * HALF:(c + 1) * HALF].rearrange("p o n -> p (o n)"), ALU.mult)
                    ins.then_inc(a.weighed, 1)
                    if c == SC - 1:
                        dve.wait_ge(a.weighed, k(w) * SC + SC)
                        dve.sem_inc(a.count_used, 1)

            def greatest(b):
                dve.wait_ge(a.masked, k(b) * SC + SC + 4)
                dve.sem_inc(a.passed, 1)
                nc.vector.tensor_reduce(out=a.least[:, 0:1], in_=a.t[:, ds((k(b) & 1) * NP, NP)], axis=AX.X, op=ALU.min).then_inc(a.least_ready, 1)
                dve.wait_ge(a.least_ready, k(b) + 1)
                dve.wait_ge(a.exped, k(b) * 2) if not (isinstance(b, int) and b == 0) else None
                nc.vector.tensor_scalar(a.bias[:, 0:1], a.least[:, 0:1], SCALE / SHRINK, None, ALU.mult).then_inc(a.biased, 1)

            def result(b):
                dve.wait_ge(a.summed, k(b) + 2)
                nc.vector.tensor_scalar(a.den[:, 0:1], s.ps[:, 6, P:P + 1], 1e-30, None, ALU.max).then_inc(a.den_ready, 1)
                dve.wait_ge(a.den_ready, k(b) + 1)
                nc.vector.reciprocal(a.den[:, 1:2], a.den[:, 0:1]).then_inc(a.inv_ready, 1)
                dve.wait_ge(a.inv_ready, k(b) + 1)
                dve.wait_ge(a.msg_turned, k(b)) if not (isinstance(b, int) and b == 0) else None
                nc.vector.tensor_scalar(a.msg[:, :], s.ps[:, 6, 0:P], a.den[:, 1:2], None, ALU.mult).then_inc(a.msg_read, 1)

            hold_q(0)
            for c in range(SC):
                chunk(0, c, True, False)
            hold_q(1)
            greatest(0)
            for c in range(SC):
                chunk(1, c, True, True)
            hold_q(2)
            greatest(1)
            with dve.Fori(2, NB - 1) as b:
                result(b - 2)
                for c in range(SC):
                    chunk(b, c, True, True)
                hold_q(b + 1)
                greatest(b)
            result(NB - 3)
            for c in range(SC):
                chunk(NB - 1, c, True, True)
            greatest(NB - 1)
            result(NB - 2)
            for c in range(SC):
                chunk(NB, c, False, True)
            result(NB - 1)


def attention_layers(nc, s, WQ, WK, WV, bV, WO):
    a = Shared()
    a.WQ, a.WK, a.WV, a.bV, a.WO = WQ, WK, WV, bV, WO
    a.weights_loaded, a.columns, a.lin, a.moved, a.held, a.made, a.read, a.count_used, a.count_back = (
        s.sem("att_" + n) for n in "weights_loaded columns lin moved held made read count_used count_back".split())
    a.q_held, a.scored, a.masked, a.least_ready, a.biased, a.exped, a.weighed, a.turned, a.pt_read = (
        s.sem("att_" + n) for n in "q_held scored masked least_ready biased exped weighed turned pt_read".split())
    a.summed, a.den_ready, a.inv_ready, a.msg_read, a.msg_turned, a.att_read, a.passed = (
        s.sem("att_" + n) for n in "summed den_ready inv_ready msg_read msg_turned att_read passed".split())
    with ExitStack() as ctx:
        def sb(name, shape):
            return ctx.enter_context(nc.sbuf_tensor("att_" + name, shape, F32))
        a.w, a.bv, a.col, a.q = sb("w", [P, 4, P]), sb("bv", [1, P]), sb("col", [P, 5]), sb("q", [P, P])
        a.hold = [sb(f"hold{h}", [P, P]) for h in range(2)]
        a.qT, a.kT, a.v = sb("qT", [P, NP]), sb("kT", [P, NP]), sb("v", [P, NB, P + 1])
        a.cnt, a.t, a.pm, a.pt = sb("cnt", [P, 2, NP]), sb("t", [P, 2 * NP]), sb("pm", [P, NP]), sb("pt", [P, NP])
        a.least, a.bias, a.den, a.msg = sb("least", [P, 1]), sb("bias", [P, 1]), sb("den", [P, 2]), sb("msg", [P, P])
        with nc.Block() as block:
            @block.gpsimd
            def _(pool):
                pool.memset(s.placing.record[:, :, :], 0.0).then_inc(s.placing.cleared, 1)

            @block.vector
            def _(dve):
                nc.vector.memset(a.v[:, :, P:P + 1], 1.0)
                for sem, credit in ((a.moved, 2), (a.read, 2), (a.count_used, 2), (a.masked, 4), (a.pt_read, 2),
                                    (a.summed, 1), (a.turned, 1), (a.msg_read, 1), (a.att_read, 1)):
                    dve.sem_inc(sem, credit)
        with nc.Fori(0, LAYERS2) as l:
            project(nc, s, a, l)
            attend(nc, s, a, l)
            node_phase(nc, s, "att", a.w[:, 3, :], s.aggT, ACT.Identity, a.col[:, 2:3], s.hT, gain=a.col[:, 3:4], shift=a.col[:, 4:5], layer=l)
    s.norm.turns += LAYERS2 * NCH
    s.norm.gained += LAYERS2 * NCH


class Residual:

    def __init__(self, s):
        self.given, self.lin, self.sig, self.gated, self.added = (s.sem("res_" + n) for n in ("given", "lin", "sig", "gated", "added"))

    def pe(self, nc, pe, s, r, w0, w1, source):
        for stage, (w, x) in enumerate(((w0, source), (w1, s.res_h))):
            for h in range(2):
                if stage == 0:
                    pe.wait_ge(self.given, 2 * r + (h + 1))
                else:
                    pe.wait_ge(self.gated, 4 * r + (h + 1))
                nc.tensor.matmul(s.ps[:, 4 + h, 0:HALF], w, x[:, h, :], start=True, stop=True).then_inc(self.lin, 1)

    def act(self, nc, act, s, r, b0, b1):
        for stage, b in enumerate((b0, b1)):
            for h in range(2):
                act.wait_ge(self.lin, 4 * r + (2 * stage + h + 1))
                nc.scalar.activation(s.res_g[:, h, :], s.ps[:, 4 + h, 0:HALF], ACT.Sigmoid, bias=b).then_inc(self.sig, 1)

    def dve(self, nc, dve, s, r, b0, b1, source, out):
        for stage, b in enumerate((b0, b1)):
            for h in range(2):
                dve.wait_ge(self.sig, 4 * r + (2 * stage + h + 1))
                nc.vector.scalar_tensor_tensor(out=s.res_h[:, h, :], in0=s.ps[:, 4 + h, 0:HALF], scalar=b, in1=s.res_g[:, h, :],
                                               op0=ALU.add, op1=ALU.mult).then_inc(self.gated, 1)
        for h in range(2):
            dve.wait_ge(self.gated, 4 * r + (h + 3))
            nc.vector.tensor_tensor(out[:, h, :], s.res_h[:, h, :], source[:, h, :], ALU.add).then_inc(self.added, 1)


def embed(nc, s, f):
    with nc.Block() as block:

        @block.sync
        def _(sp):
            sp.wait_ge(f.cleared, 1)
            for dest, dram in f.loads:
                sp.dma_start(dest, dram).then_inc(f.loaded, 16)

        @block.gpsimd
        def _(pool):
            pool.memset(f.We[:, :, :], 0.0).then_inc(f.cleared, 1)
            for turn in range(LAYERS2 * PLACE_TURNS, NT // RT):
                place_records(nc, pool, s, turn)

        @block.tensor
        def _(pe):
            pe.wait_ge(f.loaded, 16 * len(f.loads))
            with pe.Fori(0, NCH) as c:
                for e in range(2):
                    s.res.pe(nc, pe, s, c * 2 + e, f.W_emb[:, 2 * e, :], f.W_emb[:, 2 * e + 1, :], halves(s.xT[:, ds(c * CH, CH)]))

        @block.scalar
        def _(act):
            act.wait_ge(f.loaded, 16 * len(f.loads))
            with act.Fori(0, NCH) as c:
                for e in range(2):
                    s.res.act(nc, act, s, c * 2 + e, f.b_emb[:, 2 * e:2 * e + 1], f.b_emb[:, 2 * e + 1:2 * e + 2])

        @block.vector
        def _(dve):
            dve.wait_ge(f.loaded, 16 * len(f.loads))
            with dve.Fori(0, NCH) as c:
                for e, out in enumerate((f.srcT, s.hT)):
                    dve.sem_inc(s.res.given, 2)
                    s.res.dve(nc, dve, s, c * 2 + e, f.b_emb[:, 2 * e:2 * e + 1], f.b_emb[:, 2 * e + 1:2 * e + 2],
                              halves(s.xT[:, ds(c * CH, CH)]), halves(out[:, ds(c * CH, CH)]))
                    dve.wait_ge(s.res.added, 2 * (c * 2 + e) + 2)


class Placing:

    def open(self, nc, s, ctx):
        self.done, self.counted, self.based, self.chain, self.read = (
            s.sem("place_" + n) for n in ("done", "counted", "based", "chain", "read"))

        def sb(name, shape, dt=F32):
            return ctx.enter_context(nc.sbuf_tensor("place_" + name, shape, dt))
        self.blk_i, self.blk, self.hit, self.run, self.slot = sb("blk_i", [P, NT], I32), sb("blk", [P, NT]), sb("hit", [P, NT]), sb("run", [P, NT]), sb("slot", [P, NT])
        self.count, self.total, self.upto, self.base = (sb(n, [P, NB + 1]) for n in ("count", "total", "upto", "base"))
        self.row_i, self.row = sb("row_i", [1, 3, NB], I32), sb("row", [1, NB])

    def pe(self, nc, pe, s):
        pe.wait_ge(self.counted, 1)
        nc.tensor.matmul(s.ps[:, 0, 0:NB + 1], s.ones[:, :], self.count[:, :], start=True, stop=True).then_inc(self.based, 1)
        nc.tensor.matmul(s.ps[:, 1, 0:NB + 1], s.before[:, :], self.count[:, :], start=True, stop=True).then_inc(self.based, 1)
        pe.wait_ge(self.read, 2)

    def dve(self, nc, dve, s):
        BUCKETS = NB + 1
        done, chain = self.done, self.chain
        blk_i, blk, hit, run, slot, count, total, upto, base, row_i, row = (
            self.blk_i, self.blk, self.hit, self.run, self.slot, self.count, self.total, self.upto, self.base, self.row_i, self.row)
        step = [0]

        def link(ins):
            step[0] += 1
            ins.then_inc(done, 1)
            dve.wait_ge(done, step[0])

        link(nc.vector.tensor_copy(blk_i[:, :], s.src[:, 0:NT]))
        link(nc.vector.tensor_scalar(blk_i[:, :], blk_i[:, :], P.bit_length() - 1, None, ALU.arith_shift_right))
        link(nc.vector.tensor_copy(blk[:, :], blk_i[:, :]))
        link(nc.vector.memset(slot[:, :], 0.0))
        with dve.Fori(0, BUCKETS) as b:
            nc.vector.tensor_scalar(hit[:, :], blk[:, :], s.ramp[:, ds(b, 1)], None, ALU.is_equal, ALU.add,
                                    accum_out=count[:, ds(b, 1)]).then_inc(chain, 1)
            dve.wait_ge(chain, b + 1)
        dve.sem_inc(self.counted, 1)
        dve.wait_ge(self.based, 2)
        link(nc.vector.tensor_copy(total[:, :], s.ps[:, 0, 0:BUCKETS]))
        dve.sem_inc(self.read, 1)
        link(nc.vector.tensor_tensor_scan(upto[:, :], total[:, :], total[:, :], 0.0, ALU.add, ALU.max))
        link(nc.vector.tensor_tensor(total[:, :], upto[:, :], total[:, :], ALU.subtract))
        link(nc.vector.tensor_tensor(base[:, :], total[:, :], s.ps[:, 1, 0:BUCKETS], ALU.add))
        dve.sem_inc(self.read, 1)
        link(nc.vector.tensor_scalar(base[:, :], base[:, :], -1.0, None, ALU.add))
        with dve.Fori(0, BUCKETS) as b:
            nc.vector.tensor_scalar(hit[:, :], blk[:, :], s.ramp[:, ds(b, 1)], None, ALU.is_equal).then_inc(chain, 1)
            dve.wait_ge(chain, b * 4 + BUCKETS + 1)
            nc.vector.tensor_tensor_scan(run[:, :], hit[:, :], hit[:, :], 0.0, ALU.add, ALU.max).then_inc(chain, 1)
            dve.wait_ge(chain, b * 4 + BUCKETS + 2)
            nc.vector.scalar_tensor_tensor(out=run[:, :], in0=run[:, :], scalar=base[:, ds(b, 1)], in1=hit[:, :],
                                           op0=ALU.add, op1=ALU.mult).then_inc(chain, 1)
            dve.wait_ge(chain, b * 4 + BUCKETS + 3)
            nc.vector.tensor_tensor(slot[:, :], slot[:, :], run[:, :], ALU.add).then_inc(chain, 1)
        dve.wait_ge(chain, BUCKETS * 5)
        link(nc.vector.tensor_copy(s.place[:, :], slot[:, :]))
        SHIFT = P.bit_length() - 1
        link(nc.vector.tensor_copy(row_i[0:1, 0, :], total[0:1, 0:NB]))
        link(nc.vector.tensor_scalar(row[0:1, :], upto[0:1, 0:NB], float(P - 1), None, ALU.add))
        link(nc.vector.tensor_copy(row_i[0:1, 1, :], row[0:1, :]))
        link(nc.vector.tensor_scalar(row_i[0:1, 0:2, :], row_i[0:1, 0:2, :], SHIFT, None, ALU.arith_shift_right))
        link(nc.vector.tensor_copy(s.src_range[0:1, 0, :], row_i[0:1, 0, :]))
        link(nc.vector.tensor_tensor(row_i[0:1, 1, :], row_i[0:1, 1, :], row_i[0:1, 0, :], ALU.subtract))
        link(nc.vector.tensor_scalar(row_i[0:1, 1, :], row_i[0:1, 1, :], float(TG - 1), float(2 * TG), ALU.add, ALU.max))
        link(nc.vector.tensor_scalar(row_i[0:1, 2, :], row_i[0:1, 1, :], TG.bit_length() - 1, None, ALU.arith_shift_right))
        link(nc.vector.tensor_copy(s.src_range[0:1, 1, :], row_i[0:1, 2, :]))
        link(nc.vector.tensor_copy(row[0:1, :], row_i[0:1, 2, :]))
        link(nc.vector.tensor_tensor_scan(upto[0:1, 0:NB], row[0:1, :], row[0:1, :], 0.0, ALU.add, ALU.max))
        link(nc.vector.tensor_tensor(s.src_range[0:1, 2, :], upto[0:1, 0:NB], row[0:1, :], ALU.subtract))


def convolve(nc, s, f):
    R0 = 2 * NCH
    weights = [(f.W_conv, f.b_conv, 0), (f.W_conv, f.b_conv, 1), (f.W_out, f.b_out, 0), (f.W_out, f.b_out, 1)]
    n = s.norm
    with nc.Block() as block:

        @block.tensor
        def _(pe):
            with pe.Fori(0, NCH) as c:
                for e, (w, _, r) in enumerate(weights):
                    s.res.pe(nc, pe, s, c * 4 + (R0 + e), w[:, 2 * r, :], w[:, 2 * r + 1, :], s.y)
                n.pe(nc, pe, s, n.turns + c)

        @block.scalar
        def _(act):
            with act.Fori(0, NCH) as c:
                for e, (_, b, r) in enumerate(weights):
                    s.res.act(nc, act, s, c * 4 + (R0 + e), b[:, 2 * r:2 * r + 1], b[:, 2 * r + 1:2 * r + 2])
                n.act(nc, act, s, n.turns + c)

        @block.vector
        def _(dve):
            with dve.Fori(0, NCH) as c:
                at = ds(c * CH, CH)
                for h in range(2):
                    dve.wait_ge(n.normed, 2 * (n.turns + c) + (h + 1))
                    nc.vector.tensor_scalar(s.y[:, h, :], halves(s.aggT[:, at])[:, h, :], f.C[:, 0:1], None, ALU.mult).then_inc(s.res.given, 1)
                dve.wait_ge(s.res.given, 2 * (c * 4 + R0) + 2)
                for e, (_, b, r) in enumerate(weights):
                    s.res.dve(nc, dve, s, c * 4 + (R0 + e), b[:, 2 * r:2 * r + 1], b[:, 2 * r + 1:2 * r + 2], s.y, s.y)
                    for h in range(2):
                        dve.wait_ge(s.res.added, 2 * (c * 4 + (R0 + e)) + (h + 1))
                        if e == 1:
                            nc.vector.tensor_tensor(s.y[:, h, :], s.y[:, h, :], halves(f.srcT[:, at])[:, h, :], ALU.mult).then_inc(s.res.given, 1)
                        elif e < 3:
                            dve.sem_inc(s.res.given, 1)
                        else:
                            nc.vector.tensor_tensor(s.y[:, h, :], s.y[:, h, :], halves(s.xT[:, at])[:, h, :], ALU.add).then_inc(n.given, 1)
                    if e == 1:
                        dve.wait_ge(s.res.given, 2 * (c * 4 + R0 + 2) + 2)
                n.dve(nc, dve, s, n.turns + c, halves(s.xT[:, at]))




def gnn_kernel(nc, d_x, d_src, d_dst, d_ef, d_type, d_weight, d_weight1, W0, b0, proj_w, proj_b, edge_W, edge_b,
               wih, whh, bih, bhh, out_w, out_b, Wn, bn, WQ, bQ, WK, bK, WV, bV, WO, bO, ln_g, ln_b, Wout, bout,
               C, W_emb, b_emb, We, W_conv, b_conv, W_out, b_out, out):
    with ExitStack() as ctx:
        def sb(name, shape, dt=F32):
            return ctx.enter_context(nc.sbuf_tensor(name, shape, dt))

        s = Shared()
        s.sem = lambda name: ctx.enter_context(nc.semaphore(name))

        def phase(step, *args, **kwargs):
            kept, own = s.sem, []

            def take(name):
                own.append(nc.alloc_semaphore(name))
                return own[-1]
            s.sem = take
            step(nc, s, *args, **kwargs)
            s.sem = kept
            nc.clear_and_free_semaphores(own)
            nc.all_engine_barrier()
        s.ps = ctx.enter_context(nc.psum_tensor("ps", [P, 8, 512], F32))
        s.groups_of = groups_of
        s.d_x, s.d_src, s.d_dst, s.d_type, s.d_weight = d_x, d_src, d_dst, d_type, d_weight
        s.d_weight1 = d_weight1.rearrange("e o -> (e o)")
        s.d_proj_w, s.d_out_w, s.d_edge_W, s.d_wih, s.d_whh = proj_w, out_w, edge_W, wih, whh
        s.d_W0, s.d_Wn, s.d_Wout = W0, Wn, Wout

        s.edge_rows = nc.dram_tensor("edge_rows", (NT * P, P), F32, kind="Internal").ap()
        s.counts = nc.dram_tensor("counts", (NB, P, NP), F32, kind="Internal").ap()
        s.typed = nc.dram_tensor("typed", (TYPES * NP, P), F32, kind="Internal").ap()
        s.plain = nc.dram_tensor("plain", (NP, P), F32, kind="Internal").ap()
        s.records = nc.dram_tensor("records", (NT * P, REC), F32, kind="Internal").ap()

        s.ident, s.before, s.mean_w, s.ones, s.centre = (sb(n, [P, P]) for n in ("ident", "before", "mean_w", "ones", "centre"))
        s.eps = sb("eps", [P, 1])
        s.zeros_bf = sb("zeros_bf", [P, 512], BF16)
        s.ramp = sb("ramp", [P, NP])
        s.tile_i, s.tile_no = sb("tile_i", [P, TC], I32), sb("tile_no", [P, TC])
        s.start_i, s.start = sb("start_i", [P, NB + 1], I32), sb("start", [P, NB + 1])
        s.src, s.weight1, s.dst_row = sb("src", [P, TC * P]), sb("weight1", [P, TC * P]), sb("dst_row", [P, NT], I32)
        s.dst_range = sb("dst_range", [1, 3, NB], I32)
        s.src_range = sb("src_range", [1, 3, NB], I32)
        s.place = sb("place", [P, NT], I32)
        s.xT, s.hT, s.aggT = (sb(n, [P, NP]) for n in ("xT", "hT", "aggT"))
        s.W0, s.Wn, s.Wout = (sb(n, [P, P]) for n in ("W0", "Wn", "Wout"))
        s.y, s.yc, s.sq, s.rstd = (sb(n, [P, 2, HALF]) for n in ("norm_y", "norm_yc", "norm_sq", "norm_rs"))
        s.bih, s.bhh, s.b_rz = sb("bih", [P, LAYERS1, 3]), sb("bhh", [P, LAYERS1, 3]), sb("b_rz", [P, LAYERS1, 2])
        s.bias_loads = []

        def column(name, dram, cols):
            c = sb("col_" + name, [P, cols])
            s.bias_loads.append((c[:, :], dram))
            return c
        one = "(f o) -> f o"
        s.b0, s.b_proj, s.b_out1 = (column(n, a.rearrange(one, o=1), 1) for n, a in (("b0", b0), ("proj", proj_b), ("out1", out_b)))
        s.bn, s.b_out2 = (column(n, a.rearrange(one, o=1), 1) for n, a in (("bn", bn), ("out2", bout)))
        s.bQ, s.bK, s.bO, s.ln_g, s.ln_b = (column(n, a.rearrange("l f -> f l"), LAYERS2)
                                            for n, a in (("bQ", bQ), ("bK", bK), ("bO", bO), ("g", ln_g), ("b", ln_b)))
        for l in range(LAYERS1):
            s.bias_loads += [(s.bih[:, l, :], bih[l].rearrange("(g f) -> f g", f=P)), (s.bhh[:, l, :], bhh[l].rearrange("(g f) -> f g", f=P))]
        s.norm = Norm(s)

        early = ExitStack()

        def sb_early(name, shape, dt=F32):
            return early.enter_context(nc.sbuf_tensor(name, shape, dt))
        s.ramp16 = sb_early("ramp16", [P, NP], I16)
        s.dst, s.typ, s.weight = (sb_early(n, [P, TC * P]) for n in ("dst", "typ", "weight"))
        s.src_row, s.typed_row = (sb_early(n, [P, NT], I32) for n in ("src_row", "typed_row"))
        s.wT = sb_early("wT", [P, 2 + LAYERS1 * (TYPES + 6), P])

        with nc.allow_non_contiguous_dma(reason="bias columns"):
            phase(constants)
            phase(load_edges)
            phase(load_nodes)

        def write_table(table, types):
            view = table.rearrange("(t n) f -> n t f", t=types)

            def write(sp, b, row, stored):
                sp.dma_start(view[ds(b * P, P), :, :], row.rearrange("p (t f) -> p t f", t=types)).then_inc(stored, 16)
            return write

        def write_out(sp, b, row, stored):
            if isinstance(b, int):
                rows = min(P, NODES - b * P)
                sp.dma_start(out[b * P:b * P + rows, :], row[0:rows, :]).then_inc(stored, 16)
            else:
                sp.dma_start(out[ds(b * P, P), :], row).then_inc(stored, 16)

        shares = [(0, 768), (768, 1984), (1984, NP)]

        def run():
            phase(edge_pass, "sum0", s.d_x[:, :], s.src_row, s.dst_range, weighted=True, columns=shares[0], beside=Placing())
            node_phase(nc, s, "0", s.W0[:, :], s.aggT, ACT.Relu, s.b0[:, 0:1], s.xT,
                       second=(s.wT[:, 0, :], ACT.Relu, s.b_proj[:, 0:1], s.hT))
            s.norm.turns += NCH
            for l in range(LAYERS1):
                o = 2 + l * (TYPES + 6)
                phase(node_rows, f"typed{l}", s.hT, s.wT[:, o:o + TYPES, :].rearrange("p t f -> p (t f)"), TYPES * P, write_table(s.typed, TYPES))
                phase(edge_pass, f"sum1{l}", s.typed[:, :], s.typed_row, s.dst_range, columns=shares[1 + l])
                phase(gru, l)
            node_phase(nc, s, "1", s.wT[:, 1, :], s.hT, ACT.Identity, s.b_out1[:, 0:1], s.xT,
                       second=(s.Wn[:, :], ACT.Identity, s.bn[:, 0:1], s.hT))
            s.norm.turns += NCH
            early.close()
            r = s.placing = Shared()
            r.ef_back, r.copied, r.passed, r.scattered, r.cleared = (
                s.sem("place_" + n) for n in "ef_back copied passed scattered cleared".split())
            r.record, r.place = sb("place_record", [P, RT, REC]), sb("place_index", [P, RT], I32)
            r.features = d_ef[0:FULL_TILES * P, :].rearrange("(t p) k -> p t k", p=P)
            r.last_features = d_ef[FULL_TILES * P:EDGES, :]
            r.loads, r.clears = LAYERS2 * PLACE_TURNS, 1
            attention_layers(nc, s, WQ, WK, WV, bV, WO)
            node_phase(nc, s, "2", s.Wout[:, :], s.hT, ACT.Identity, s.b_out2[:, 0:1], s.xT)
            s.norm.turns += NCH
            late = ExitStack()
            f = Shared()
            f.loaded, f.cleared, f.loads = s.sem("late_loaded"), s.sem("late_cleared"), []

            def sb_late(name, shape, dram=None, dt=F32):
                t = late.enter_context(nc.sbuf_tensor("late_" + name, shape, dt))
                if dram is not None:
                    f.loads.append((t[:], dram))
                return t
            two = "a b i o -> i (a b) o"
            f.W_emb, f.W_conv, f.W_out = (sb_late(n, [P, 4, P], a.rearrange(two)) for n, a in (("W_emb", W_emb), ("W_conv", W_conv), ("W_out", W_out)))
            f.b_emb, f.b_conv, f.b_out = (sb_late(n, [P, 4], a.rearrange("a b f -> f (a b)")) for n, a in (("b_emb", b_emb), ("b_conv", b_conv), ("b_out", b_out)))
            f.We = sb_late("We", [P, PT, P])
            f.loads += [(f.We[j * (P // PT):j * (P // PT) + EF, j, :], We) for j in range(PT)]
            f.C = sb_late("C", [P, 1], C.rearrange("(o c) -> o c", o=1).broadcast_to([P, 1]))
            f.srcT = sb_late("srcT", [P, NP])
            s.res_h, s.res_g = sb_late("res_h", [P, 2, HALF]), sb_late("res_g", [P, 2, HALF])
            s.res = Residual(s)
            with nc.allow_non_contiguous_dma(reason="bias columns"):
                embed(nc, s, f)
            phase(node_rows, "plain", s.hT, s.ident[:, :], P, write_table(s.plain, 1))
            phase(edge_pass, "sum3", s.plain[:, :], None, s.src_range, We=f.We[:, :, :].rearrange("p t f -> p (t f)"))
            phase(convolve, f)
            late.close()
            return s.xT
        final = run()
        phase(node_rows, "out", final, s.ident[:, :], P, write_out)




_INS = ['x', 'src', 'dst', 'edge_attr_32', 'edge_type_8', 'edge_weight', 'edge_weight1', 'L0_gnn_W', 'L0_gnn_b',
        'L1_gnn_node_proj_w', 'L1_gnn_node_proj_b', 'L1_gnn_edge_W', 'L1_gnn_edge_b', 'L1_gnn_gru_wih',
        'L1_gnn_gru_whh', 'L1_gnn_gru_bih', 'L1_gnn_gru_bhh', 'L1_gnn_out_w', 'L1_gnn_out_b', 'L2_gnn_Wn',
        'L2_gnn_bn', 'L2_gnn_WQ', 'L2_gnn_bQ', 'L2_gnn_WK', 'L2_gnn_bK', 'L2_gnn_WV', 'L2_gnn_bV', 'L2_gnn_WO',
        'L2_gnn_bO', 'L2_gnn_ln_g', 'L2_gnn_ln_b', 'L2_gnn_Wout', 'L2_gnn_bout', 'L3_gnn_C', 'L3_gnn_W_emb',
        'L3_gnn_b_emb', 'L3_gnn_We', 'L3_gnn_W_conv', 'L3_gnn_b_conv', 'L3_gnn_W_out', 'L3_gnn_b_out']
_OUTS = [((3125, 128), 'float32')]


def kernel(**inputs):
    import numpy as _np
    import concourse.bacc as _bacc
    from concourse import mybir as _mybir
    from concourse.bass_utils import run_bass_kernel_spmd as _run

    nc = _bacc.Bacc("TRN2", target_bir_lowering=False, num_devices=1)
    arrays, args = {}, []
    for name in _INS:
        a = _np.ascontiguousarray(inputs[name])
        arrays[f"in_{name}_dram"] = a
        args.append(nc.dram_tensor(f"in_{name}_dram", a.shape, _mybir.dt.from_np(a.dtype), kind="ExternalInput").ap())
    for i, (shape, dtype) in enumerate(_OUTS):
        dt = _mybir.dt.from_np(_np.dtype(dtype))
        args.append(nc.dram_tensor(f"out_{i}_dram", shape, dt, kind="ExternalOutput").ap())
    gnn_kernel(nc, *args)
    r = _run(nc, [arrays], core_ids=[0])
    got = tuple(r.results[0][f"out_{i}_dram"] for i in range(len(_OUTS)))
    return got[0]
```
